# Optimizing a Trainium2 kernel written in Bass

```python
import numpy as np
import jax
import jax.numpy as jnp

def _softmax(x, axis=-1):
    return jax.nn.softmax(x, axis=axis)

def _gelu(x):
    return jax.nn.gelu(x, approximate=True)

def _silu(x):
    return jax.nn.silu(x)

def _sigmoid(x):
    return jax.nn.sigmoid(x)

def _layernorm(x, axis=-1, eps=1e-05):
    m = jnp.mean(x, axis=axis, keepdims=True)
    v = jnp.var(x, axis=axis, keepdims=True)
    return (x - m) / jnp.sqrt(v + eps)

def _scatter_add(tgt, idx, src, axis=0):
    return tgt.at[idx].add(src)

def _segment_sum(src, seg, n):
    return jax.ops.segment_sum(src, seg, n)
kernel_name = 'mk_gnn_preln_d4_gnn_r16_82a6d6'

def setup_inputs(seed: int=0):
    np.random.seed(seed)
    _w = jnp.asarray

    def _rec_inputs():
        import jax
        import jax.numpy as jnp
        _gk = jax.random.key(seed)
        x = -8.776e-05 + 1 * jax.random.normal(jax.random.fold_in(_gk, 1), (6250, 256), jnp.float32)
        _s = jax.random.randint(jax.random.fold_in(_gk, 2), (50000,), 0, 6250, jnp.int32)
        _d = jax.random.randint(jax.random.fold_in(_gk, 3), (50000,), 0, 6250, jnp.int32)
        _loop = jnp.arange(6250, dtype=jnp.int32)
        src = jnp.concatenate([_s, _d, _loop])
        dst = jnp.concatenate([_d, _s, _loop])
        _o = jnp.argsort(dst, stable=True)
        src = src[_o]
        dst = dst[_o]
        edge_attr_10 = jax.random.uniform(jax.random.fold_in(_gk, 13), (106250, 10), jnp.float32, 0.0, 1)
        edge_attr_4 = 0.000924777 + 0.999162 * jax.random.normal(jax.random.fold_in(_gk, 14), (106250, 4), jnp.float32)
        edge_weight = jax.random.uniform(jax.random.fold_in(_gk, 16), (106250,), jnp.float32, 0.0, 1)
        node_vec1 = jax.random.uniform(jax.random.fold_in(_gk, 17), (6250, 1), jnp.float32, 0.0, 1)
        return (x, src, dst, edge_attr_10, edge_attr_4, edge_weight, node_vec1)
    x, src, dst, edge_attr_10, edge_attr_4, edge_weight, node_vec1 = _rec_inputs()

    def _L0_gnn_setup():
        import jax, jax.numpy as jnp
        import numpy as np
        import math
        N_NODES = 1250
        N_EDGES = 20000
        MUL = 64
        N_BASIS = 10
        N_HID = 100
        W_NUMEL = 4 * MUL

        def _split(x):
            s = x[..., :MUL]
            v = x[..., MUL:].reshape(x.shape[:-1] + (MUL, 3))
            return (s, v)

        def _fctp(s, v, W0, W1, attr, fan_in):
            inv = 1.0 / math.sqrt(fan_in)
            o0 = jnp.einsum('nu,uk->nk', s, W0) * attr * inv
            o1 = jnp.einsum('num,uk->nkm', v, W1) * attr[..., None] * inv
            return (o0, o1)
        key = jax.random.key(seed)
        ks = jax.random.split(key, 16)
        node_input = jax.random.normal(ks[0], (N_NODES, 4 * MUL), dtype=jnp.float32)
        node_attr = jnp.ones((N_NODES, 1), dtype=jnp.float32)
        node_deg = jax.random.randint(ks[1], (N_NODES, 1), 1, 33).astype(jnp.float32)
        edge_src = jax.random.randint(ks[2], (N_EDGES,), 0, N_NODES)
        edge_dst = jax.random.randint(ks[3], (N_EDGES,), 0, N_NODES)
        edge_attr = jax.random.normal(ks[4], (N_EDGES, 4), dtype=jnp.float32)
        edge_length_embedded = jax.random.uniform(ks[5], (N_EDGES, N_BASIS), dtype=jnp.float32)
        W_li0 = jax.random.normal(ks[6], (MUL, MUL), dtype=jnp.float32)
        W_li1 = jax.random.normal(ks[7], (MUL, MUL), dtype=jnp.float32)
        W_lm0 = jax.random.normal(ks[8], (MUL, MUL), dtype=jnp.float32)
        W_lm1 = jax.random.normal(ks[9], (MUL, MUL), dtype=jnp.float32)
        W_mlp1 = jax.random.normal(ks[10], (N_BASIS, N_HID), dtype=jnp.float32)
        W_mlp2 = jax.random.normal(ks[11], (N_HID, W_NUMEL), dtype=jnp.float32)
        W_lo0 = jax.random.normal(ks[12], (2 * MUL, MUL), dtype=jnp.float32)
        W_lo1 = jax.random.normal(ks[13], (2 * MUL, MUL), dtype=jnp.float32)
        return dict(node_input=node_input, node_attr=node_attr, node_deg=node_deg, edge_attr=edge_attr, edge_length_embedded=edge_length_embedded, W_li0=W_li0, W_li1=W_li1, W_lm0=W_lm0, W_lm1=W_lm1, W_mlp1=W_mlp1, W_mlp2=W_mlp2, W_lo0=W_lo0, W_lo1=W_lo1, edge_src=edge_src, edge_dst=edge_dst)
    _L0_gnn_all = _L0_gnn_setup()
    _L0_gnn_in = {k: v for k, v in _L0_gnn_all.items() if k in ('W_li0', 'W_li1', 'W_lm0', 'W_lm1', 'W_mlp1', 'W_mlp2', 'W_lo0', 'W_lo1')}
    del _L0_gnn_all

    def _L1_gnn_setup():
        import jax, jax.numpy as jnp
        import numpy as np
        NEG = -1000.0
        SLOPE = 0.01
        N_NODES, N_EDGES, D_IN, D_OUT, N_HEADS = (6250, 100000, 256, 64, 4)
        key = jax.random.key(seed)
        k0, k1, k2, k3, k4 = jax.random.split(key, 5)
        h = jax.random.normal(k0, (N_NODES, D_IN), jnp.float32)
        src = jax.random.randint(k1, (N_EDGES,), 0, N_NODES)
        dst = jax.random.randint(k2, (N_EDGES,), 0, N_NODES)
        W = jax.random.normal(k3, (N_HEADS, D_IN, D_OUT), jnp.float32) / np.sqrt(D_IN)
        att = jax.random.normal(k4, (N_HEADS, 2 * D_OUT), jnp.float32) / np.sqrt(2.0 * D_OUT)
        return {'h': h, 'W': W, 'att': att, 'src': src, 'dst': dst}
    _L1_gnn_all = _L1_gnn_setup()
    _L1_gnn_in = {k: v for k, v in _L1_gnn_all.items() if k in ('W', 'att')}
    del _L1_gnn_all

    def _L2_gnn_setup():
        import jax, jax.numpy as jnp
        import numpy as np
        N_NODES = 6250
        N_EDGES = 200000
        D_IN = 256
        D_OUT = 256
        key = jax.random.key(seed)
        k1, k2, k3, k4, k5, k6 = jax.random.split(key, 6)
        x = jax.random.normal(k1, (N_NODES, D_IN), dtype=jnp.float32)
        edge_src = jax.random.randint(k2, (N_EDGES,), 0, N_NODES, dtype=jnp.int64)
        edge_dst = jax.random.randint(k3, (N_EDGES,), 0, N_NODES, dtype=jnp.int64)
        adj_vals = jax.random.uniform(k4, (N_EDGES,), dtype=jnp.float32)
        bound = 2.0 * np.sqrt(6.0 / (D_IN + D_OUT))
        w_nbr = jax.random.uniform(k5, (D_IN, D_OUT), dtype=jnp.float32, minval=-bound, maxval=bound)
        w_own = jax.random.uniform(k6, (D_IN, D_OUT), dtype=jnp.float32, minval=-bound, maxval=bound)
        bias = jnp.zeros((D_OUT,), dtype=jnp.float32)
        return {'x': x, 'edge_src': edge_src, 'edge_dst': edge_dst, 'adj_vals': adj_vals, 'w_nbr': w_nbr, 'w_own': w_own, 'bias': bias}
    _L2_gnn_all = _L2_gnn_setup()
    _L2_gnn_in = {k: v for k, v in _L2_gnn_all.items() if k in ('w_nbr', 'w_own', 'bias')}
    del _L2_gnn_all

    def _L3_gnn_setup():
        import jax, jax.numpy as jnp
        import numpy as np
        N_NODES = 3125
        N_EDGES = 50000
        D_MODEL = 256
        NUM_HEADS = 8
        HEAD_DIM = D_MODEL // NUM_HEADS
        D_FF = 2 * D_MODEL
        NEG_SLOPE = 0.2
        BN_EPS = 1e-05

        def _batch_norm(h, g, b):
            mean = jnp.mean(h, axis=0)
            var = jnp.mean((h - mean) ** 2, axis=0)
            return (h - mean) * jax.lax.rsqrt(var + BN_EPS) * g + b
        key = jax.random.key(seed)
        ks = jax.random.split(key, 16)
        x = jax.random.normal(ks[0], (N_NODES, D_MODEL), dtype=jnp.float32)
        src = jax.random.randint(ks[1], (N_EDGES,), 0, N_NODES)
        off = jax.random.randint(ks[2], (N_EDGES,), 1, N_NODES)
        dst = (src + off) % N_NODES
        edge_index = jnp.stack([src, dst]).astype(jnp.int64)

        def lin(k, fi, fo):
            s = 1.0 / np.sqrt(fi)
            return jax.random.uniform(k, (fi, fo), jnp.float32, -s, s)
        inp = {'x': x, 'edge_index': edge_index, 'Wq': lin(ks[3], D_MODEL, D_MODEL), 'bq': jnp.zeros((D_MODEL,), jnp.float32), 'Wk': lin(ks[4], D_MODEL, D_MODEL), 'bk': jnp.zeros((D_MODEL,), jnp.float32), 'Wv': lin(ks[5], D_MODEL, D_MODEL), 'bv': jnp.zeros((D_MODEL,), jnp.float32), 'Wo': lin(ks[6], D_MODEL, D_MODEL), 'bo': jnp.zeros((D_MODEL,), jnp.float32), 'W1': lin(ks[7], D_MODEL, D_FF), 'b1': jnp.zeros((D_FF,), jnp.float32), 'W2': lin(ks[8], D_FF, D_MODEL), 'b2': jnp.zeros((D_MODEL,), jnp.float32), 'bn1_g': jnp.ones((D_MODEL,), jnp.float32), 'bn1_b': jnp.zeros((D_MODEL,), jnp.float32), 'bn2_g': jnp.ones((D_MODEL,), jnp.float32), 'bn2_b': jnp.zeros((D_MODEL,), jnp.float32)}
        return inp
    _L3_gnn_all = _L3_gnn_setup()
    _L3_gnn_in = {k: v for k, v in _L3_gnn_all.items() if k in ('Wq', 'bq', 'Wk', 'bk', 'Wv', 'bv', 'Wo', 'bo', 'W1', 'b1', 'W2', 'b2', 'bn1_g', 'bn1_b', 'bn2_g', 'bn2_b')}
    del _L3_gnn_all
    return {'x': x, 'src': src, 'dst': dst, 'edge_attr_10': edge_attr_10, 'edge_attr_4': edge_attr_4, 'edge_weight': edge_weight, 'node_vec1': node_vec1, 'L0_gnn_W_li0': _L0_gnn_in['W_li0'], 'L0_gnn_W_li1': _L0_gnn_in['W_li1'], 'L0_gnn_W_lm0': _L0_gnn_in['W_lm0'], 'L0_gnn_W_lm1': _L0_gnn_in['W_lm1'], 'L0_gnn_W_mlp1': _L0_gnn_in['W_mlp1'], 'L0_gnn_W_mlp2': _L0_gnn_in['W_mlp2'], 'L0_gnn_W_lo0': _L0_gnn_in['W_lo0'], 'L0_gnn_W_lo1': _L0_gnn_in['W_lo1'], 'L1_gnn_W': _L1_gnn_in['W'], 'L1_gnn_att': _L1_gnn_in['att'], 'L2_gnn_w_nbr': _L2_gnn_in['w_nbr'], 'L2_gnn_w_own': _L2_gnn_in['w_own'], 'L2_gnn_bias': _L2_gnn_in['bias'], 'L3_gnn_Wq': _L3_gnn_in['Wq'], 'L3_gnn_bq': _L3_gnn_in['bq'], 'L3_gnn_Wk': _L3_gnn_in['Wk'], 'L3_gnn_bk': _L3_gnn_in['bk'], 'L3_gnn_Wv': _L3_gnn_in['Wv'], 'L3_gnn_bv': _L3_gnn_in['bv'], 'L3_gnn_Wo': _L3_gnn_in['Wo'], 'L3_gnn_bo': _L3_gnn_in['bo'], 'L3_gnn_W1': _L3_gnn_in['W1'], 'L3_gnn_b1': _L3_gnn_in['b1'], 'L3_gnn_W2': _L3_gnn_in['W2'], 'L3_gnn_b2': _L3_gnn_in['b2'], 'L3_gnn_bn1_g': _L3_gnn_in['bn1_g'], 'L3_gnn_bn1_b': _L3_gnn_in['bn1_b'], 'L3_gnn_bn2_g': _L3_gnn_in['bn2_g'], 'L3_gnn_bn2_b': _L3_gnn_in['bn2_b']}

def reference(x, src, dst, edge_attr_10, edge_attr_4, edge_weight, node_vec1, L0_gnn_W_li0, L0_gnn_W_li1, L0_gnn_W_lm0, L0_gnn_W_lm1, L0_gnn_W_mlp1, L0_gnn_W_mlp2, L0_gnn_W_lo0, L0_gnn_W_lo1, L1_gnn_W, L1_gnn_att, L2_gnn_w_nbr, L2_gnn_w_own, L2_gnn_bias, L3_gnn_Wq, L3_gnn_bq, L3_gnn_Wk, L3_gnn_bk, L3_gnn_Wv, L3_gnn_bv, L3_gnn_Wo, L3_gnn_bo, L3_gnn_W1, L3_gnn_b1, L3_gnn_W2, L3_gnn_b2, L3_gnn_bn1_g, L3_gnn_bn1_b, L3_gnn_bn2_g, L3_gnn_bn2_b):
    import jax
    import jax.numpy as jnp

    def _L0_gnn_ref(node_input, node_attr, node_deg, edge_attr, edge_length_embedded, W_li0, W_li1, W_lm0, W_lm1, W_mlp1, W_mlp2, W_lo0, W_lo1, edge_src, edge_dst):
        import jax, jax.numpy as jnp
        import numpy as np
        import math
        N_NODES = 1250
        N_EDGES = 20000
        MUL = 64
        N_BASIS = 10
        N_HID = 100
        W_NUMEL = 4 * MUL

        def _split(x):
            s = x[..., :MUL]
            v = x[..., MUL:].reshape(x.shape[:-1] + (MUL, 3))
            return (s, v)

        def _fctp(s, v, W0, W1, attr, fan_in):
            inv = 1.0 / math.sqrt(fan_in)
            o0 = jnp.einsum('nu,uk->nk', s, W0) * attr * inv
            o1 = jnp.einsum('num,uk->nkm', v, W1) * attr[..., None] * inv
            return (o0, o1)
        N = node_input.shape[0]
        x0, x1 = _split(node_input)
        f0, f1 = _fctp(x0, x1, W_li0, W_li1, node_attr, MUL)
        deg_isqrt = 1.0 / jnp.sqrt(node_deg)
        f0 = f0 * deg_isqrt
        f1 = f1 * deg_isqrt[..., None]
        m0, m1 = _fctp(x0, x1, W_lm0, W_lm1, node_attr, MUL)
        h = jax.nn.silu(edge_length_embedded @ W_mlp1 / math.sqrt(N_BASIS))
        ew = h @ W_mlp2 / math.sqrt(N_HID)
        wa, wb, wc, wd = (ew[:, :MUL], ew[:, MUL:2 * MUL], ew[:, 2 * MUL:3 * MUL], ew[:, 3 * MUL:])
        g0 = f0[edge_src]
        g1 = f1[edge_src]
        y0 = edge_attr[:, 0]
        y1 = edge_attr[:, 1:4]
        m0a = wa * g0 * y0[:, None]
        m0b = wb * jnp.einsum('eum,em->eu', g1, y1) / math.sqrt(3.0)
        m1a = wc[:, :, None] * g0[:, :, None] * y1[:, None, :]
        m1b = wd[:, :, None] * g1 * y0[:, None, None]
        s_mid = jax.ops.segment_sum(jnp.concatenate([m0a, m0b], axis=1), edge_dst, num_segments=N)
        v_mid = jax.ops.segment_sum(jnp.concatenate([m1a, m1b], axis=1), edge_dst, num_segments=N)
        s_mid = s_mid * deg_isqrt
        v_mid = v_mid * deg_isqrt[..., None]
        o0, o1 = _fctp(s_mid, v_mid, W_lo0, W_lo1, node_attr, 2 * MUL)
        c_s, c_x = (math.sin(math.pi / 8), math.cos(math.pi / 8))
        out0 = c_s * m0 + c_x * o0
        out1 = c_s * m1 + c_x * o1
        return jnp.concatenate([out0, out1.reshape(N, 3 * MUL)], axis=1)

    def _L1_gnn_ref(h, W, att, src, dst):
        import jax, jax.numpy as jnp
        import numpy as np
        NEG = -1000.0
        SLOPE = 0.01
        N_NODES, N_EDGES, D_IN, D_OUT, N_HEADS = (6250, 100000, 256, 64, 4)
        N = h.shape[0]
        H, _, F = W.shape
        z = jnp.einsum('nd,hdf->nhf', h, W)
        a_src, a_dst = (att[:, :F], att[:, F:])
        es = jnp.einsum('nhf,hf->nh', z, a_src)
        ed = jnp.einsum('nhf,hf->nh', z, a_dst)
        e = jax.nn.leaky_relu(es[src] + ed[dst], SLOPE)
        e = jnp.where(e == 0.0, NEG, e)
        m = jax.ops.segment_max(e, dst, num_segments=N)
        m = jnp.where(jnp.isfinite(m), m, 0.0)
        ex = jnp.exp(e - m[dst])
        denom = jax.ops.segment_sum(ex, dst, num_segments=N)
        safe = jnp.where(denom[dst] > 0.0, denom[dst], 1.0)
        alpha = ex / safe
        out = jax.ops.segment_sum(alpha[:, :, None] * z[src], dst, num_segments=N)
        return out.reshape(N, H * F)

    def _L2_gnn_ref(x, edge_src, edge_dst, adj_vals, w_nbr, w_own, bias):
        import jax, jax.numpy as jnp
        import numpy as np
        N_NODES = 6250
        N_EDGES = 200000
        D_IN = 256
        D_OUT = 256
        h = x @ w_nbr
        msgs = adj_vals[:, None] * h[edge_src]
        agg = jax.ops.segment_sum(msgs, edge_dst, num_segments=x.shape[0])
        return agg + x @ w_own + bias

    def _L3_gnn_ref(x, edge_index, Wq, bq, Wk, bk, Wv, bv, Wo, bo, W1, b1, W2, b2, bn1_g, bn1_b, bn2_g, bn2_b):
        import jax, jax.numpy as jnp
        import numpy as np
        N_NODES = 3125
        N_EDGES = 50000
        D_MODEL = 256
        NUM_HEADS = 8
        HEAD_DIM = D_MODEL // NUM_HEADS
        D_FF = 2 * D_MODEL
        NEG_SLOPE = 0.2
        BN_EPS = 1e-05

        def _batch_norm(h, g, b):
            mean = jnp.mean(h, axis=0)
            var = jnp.mean((h - mean) ** 2, axis=0)
            return (h - mean) * jax.lax.rsqrt(var + BN_EPS) * g + b
        N = x.shape[0]
        Qh = (x @ Wq + bq).reshape(N, NUM_HEADS, HEAD_DIM)
        Kh = (x @ Wk + bk).reshape(N, NUM_HEADS, HEAD_DIM)
        Vh = (x @ Wv + bv).reshape(N, NUM_HEADS, HEAD_DIM)
        s = jnp.einsum('nhc,nhc->nh', Qh, Kh) / jnp.sqrt(jnp.float32(HEAD_DIM))
        loops = jnp.arange(N, dtype=edge_index.dtype)
        src = jnp.concatenate([edge_index[0], loops])
        dst = jnp.concatenate([edge_index[1], loops])
        alpha = jax.nn.leaky_relu(s[src] + s[dst], NEG_SLOPE)
        m = jax.ops.segment_max(alpha, dst, num_segments=N)
        e = jnp.exp(alpha - m[dst])
        denom = jax.ops.segment_sum(e, dst, num_segments=N)
        a = e / denom[dst]
        msg = Vh[src] * a[:, :, None]
        attn = jax.ops.segment_sum(msg, dst, num_segments=N).reshape(N, D_MODEL)
        h = attn @ Wo + bo
        h = x + h
        h = _batch_norm(h, bn1_g, bn1_b)
        h2 = jax.nn.relu(h @ W1 + b1) @ W2 + b2
        h = _batch_norm(h + h2, bn2_g, bn2_b)
        return h
    edge_index = jnp.stack([src, dst])
    deg = jnp.maximum(jax.ops.segment_sum(jnp.ones(dst.shape, jnp.float32), dst, num_segments=6250), 1.0)
    h = jnp.maximum(_layernorm(x, axis=-1), 0.0)
    x = x + _L0_gnn_ref(h, node_vec1, deg[:, None], edge_attr_4, edge_attr_10, L0_gnn_W_li0, L0_gnn_W_li1, L0_gnn_W_lm0, L0_gnn_W_lm1, L0_gnn_W_mlp1, L0_gnn_W_mlp2, L0_gnn_W_lo0, L0_gnn_W_lo1, src, dst)
    h = jnp.maximum(_layernorm(x, axis=-1), 0.0)
    x = x + _L1_gnn_ref(h, L1_gnn_W, L1_gnn_att, src, dst)
    h = jnp.maximum(_layernorm(x, axis=-1), 0.0)
    x = x + _L2_gnn_ref(h, src, dst, edge_weight, L2_gnn_w_nbr, L2_gnn_w_own, L2_gnn_bias)
    h = jnp.maximum(_layernorm(x, axis=-1), 0.0)
    x = x + _L3_gnn_ref(h, edge_index, L3_gnn_Wq, L3_gnn_bq, L3_gnn_Wk, L3_gnn_bk, L3_gnn_Wv, L3_gnn_bv, L3_gnn_Wo, L3_gnn_bo, L3_gnn_W1, L3_gnn_b1, L3_gnn_W2, L3_gnn_b2, L3_gnn_bn1_g, L3_gnn_bn1_b, L3_gnn_bn2_g, L3_gnn_bn2_b)
    return x

_drawn_inputs = setup_inputs


def setup_inputs(seed=0):
    import zlib

    import numpy as np

    out = dict(_drawn_inputs(seed))
    spreads = {'L2_gnn_bias': (0.0, 2.0),
     'L3_gnn_bq': (0.0, 2.0),
     'L3_gnn_bk': (0.0, 2.0),
     'L3_gnn_bv': (0.0, 2.0),
     'L3_gnn_bo': (0.0, 2.0),
     'L3_gnn_b1': (0.0, 2.0),
     'L3_gnn_b2': (0.0, 2.0),
     'L3_gnn_bn1_g': (1.0, 0.6),
     'L3_gnn_bn1_b': (0.0, 2.0),
     'L3_gnn_bn2_g': (1.0, 0.6),
     'L3_gnn_bn2_b': (0.0, 2.0)}
    factors = {'edge_attr_10': 8.0,
     'edge_attr_4': 5.568,
     'L0_gnn_W_li0': 7.486,
     'L0_gnn_W_li1': 8.0,
     'L0_gnn_W_mlp1': 5.407,
     'L0_gnn_W_mlp2': 5.723,
     'L0_gnn_W_lo0': 8.0,
     'L0_gnn_W_lo1': 6.502,
     'L3_gnn_Wq': 200.0,
     'L3_gnn_Wk': 200.0,
     'edge_weight': 8.0,
     'L0_gnn_W_lm0': 64.0,
     'L0_gnn_W_lm1': 64.0,
     'L1_gnn_W': 64.0,
     'L1_gnn_att': 64.0,
     'L2_gnn_w_nbr': 8.0,
     'L2_gnn_w_own': 64.0,
     'L3_gnn_Wv': 64.0,
     'L3_gnn_Wo': 64.0,
     'L3_gnn_W1': 64.0,
     'L3_gnn_W2': 64.0}
    for name, (base, spread) in spreads.items():
        noise = np.random.default_rng([zlib.crc32(name.encode()), seed]).standard_normal(out[name].shape)
        drawn = base * np.exp(spread * noise) if base else spread * noise
        out[name] = jnp.asarray(drawn.astype(out[name].dtype))
    for name, factor in factors.items():
        out[name] = (out[name] * factor).astype(out[name].dtype)
    return out
```

```python
import math

import numpy as np

N = 6250
D = 256
E = 106250
P = 128
NT = 2 * math.ceil(N / P / 2)
NP = NT * P
FULL, REST = N // P, N % P
ET = math.ceil(E / P)
EPAD = ET * P
U = 8
K = U * math.ceil((ET + math.ceil(N / P) - 1) / U)
KB = math.ceil(K / P)
KP = KB * P
NOWHERE = 16383
BIG = 1.0e38
EPS = 1e-5
MUL = 64
NBAS, NHID = 10, 100
H1, H3 = 4, 8


def build(nc, a, out):
    import concourse.bass as bass
    from concourse import mybir
    from contextlib import ExitStack

    F32, I32, BF16 = mybir.dt.float32, mybir.dt.int32, mybir.dt.bfloat16
    ALU = mybir.AluOpType
    ACT = mybir.ActivationFunctionType
    AX = mybir.AxisListType
    ds = bass.ds

    def dram(name, shape, dt=F32):
        return nc.dram_tensor(name, shape, dt).ap()

    stages = []

    class Stage(ExitStack):

        def __init__(self):
            super().__init__()
            stages.append(self)
            self.tag = f"_{len(stages)}"
            self.sems = []

        def sb(self, name, shape, dt=F32):
            return self.enter_context(nc.sbuf_tensor(name + self.tag, list(shape), dt))

        def ps(self, name, shape):
            bank = self.enter_context(nc.psum_tensor(name + self.tag, [P, 512], F32))
            view = bank[0:shape[0], 0:math.prod(shape[1:])]
            return view if len(shape) == 2 else view.rearrange("p (b c) -> p b c", b=shape[1])

        def sem(self, name):
            handle = nc.alloc_semaphore(name + self.tag)
            self.sems.append(handle)
            return handle

        def __exit__(self, *exc):
            if self.sems and exc[0] is None:
                nc.clear_and_free_semaphores(self.sems)
                nc.all_engine_barrier(sem_only=True)
            return super().__exit__(*exc)

    def chain(eng, sem, base=0):
        count = [0]

        def link(ins):
            count[0] += 1
            ins.then_inc(sem, 1)
            eng.wait_ge(sem, base + count[0])
        return link

    dst_pad, src_pad, w_pad = dram("dst_pad", [EPAD], I32), dram("src_pad", [EPAD], I32), dram("w_pad", [EPAD])
    a4_pad, a10_pad = dram("a4_pad", [EPAD * 4]), dram("a10_pad", [EPAD * NBAS])
    node_i, node_f = dram("step_node_i", [KP], I32), dram("step_node_f", [KP])
    wbig = dram("wbig", [D, 2 * D])
    table = [dram(f"table{n}", [NP, D]) for n in range(4)]
    small1, small3 = dram("small1", [NP, H1]), dram("small3", [NP, H3])
    base0, x1 = dram("base0", [NP, D]), dram("x1", [NP, D])

    top = Stage()
    with top:
        ident = top.sb("ident", [P, P])
        iota = top.sb("iota", [P, P])
        ones = top.sb("ones", [P, P])
        relS = top.sb("relS", [P, KP])
        wS = top.sb("wS", [P, KP])
        srcI = top.sb("srcI", [P, KP], I32)
        dstK = top.sb("dstK", [P, KB, P])
        outK = top.sb("outK", [P, KB, P])
        nodeR = top.sb("nodeR", [1, KP], I32)
        cnt = top.sb("cnt", [P, NT])
        dis = top.sb("dis", [P, NT])

        def gather_indices(act, ib, s_ib, s_cons, s_gt, i, first):
            for h in range(2):
                if not first:
                    act.wait_ge(s_cons, i * U - 4 + 4 * h)
                    act.wait_ge(s_gt, 2 * i + h)
                nc.scalar.activation(ib[:, 4 * h:4 * h + 4], srcI[:, ds(i * U + 4 * h, 4)], ACT.Copy).then_inc(s_ib, 1)

        def gather_rows(pool, G, ib, gate, rows, s_ib, s_g, s_gt, i):
            for h in range(2):
                pool.wait_ge(s_ib, 2 * i + h + 1)
                pool.tensor_tensor(gate[0:1, h:h + 1], gate[0:1, 2:3], gate[0:1, 2:3], ALU.mult).then_inc(s_gt, 1)
                for j in range(4 * h, 4 * h + 4):
                    pool.indirect_dma_start(G[j][:, :], None, rows,
                                            bass.IndirectOffsetOnAxis(ap=ib[:, j:j + 1], axis=0)).then_inc(s_g[j], 16)

        def edge_scores(small, node_sc, H, gS, dS):
            with Stage() as se:
                G = [se.sb(f"G{j}", [P, H]) for j in range(U)]
                ib, gate = se.sb("ib", [P, U], I32), se.sb("gate", [1, 3])
                one = [se.sb(f"one{j}", [P, P]) for j in range(2)]
                oneT = [se.sb(f"oneT{j}", [P, P]) for j in range(2)]
                pT = [se.ps(f"pT{j}", [P, P]) for j in range(2)]
                pD = [se.ps(f"pD{j}", [P, H]) for j in range(2)]
                s_ib, s_gt, s_cons, s_one, s_t, s_tc, s_d, s_dc, s_z = (
                    se.sem(n) for n in ("s_ib", "s_gt", "s_cons", "s_one", "s_t", "s_tc", "s_d", "s_dc", "s_z"))
                s_g = [se.sem(f"s_g{j}") for j in range(U)]
                with nc.Block() as block:
                    @block.gpsimd
                    def _(pool):
                        pool.memset(gate[:, :], 1.0).then_inc(s_gt, 1)
                        pool.wait_ge(s_gt, 1)
                        rolled(pool, lambda i, first: gather_rows(pool, G, ib, gate, small, s_ib, s_g, s_gt, i))

                    @block.vector
                    def _(dve):
                        nc.vector.memset(gS[:, K:KP, :], 0.0).then_inc(s_z, 1)
                        nc.vector.memset(dS[:, K:KP, :], 0.0).then_inc(s_z, 1)

                        def body(i, first):
                            for j in range(U):
                                k = U * i + j
                                if not first or j >= 2:
                                    dve.wait_ge(s_t, k - 1)
                                nc.vector.tensor_scalar(one[j % 2][:, :], iota[:, :], relS[:, ds(k, 1)], None, ALU.is_equal).then_inc(s_one, 1)
                                dve.wait_ge(s_g[j], 16 * i + 16)
                                nc.vector.tensor_copy(tile(gS, k), G[j][:, :]).then_inc(s_cons, 1)
                        rolled(dve, body)

                    @block.tensor
                    def _(pe):
                        def pick(k, j, early):
                            node = pe.value_load(nodeR[0:1, ds(k, 1)], min_val=0, max_val=NT - 1)
                            pe.wait_ge(s_tc, k + 1)
                            if not early:
                                pe.wait_ge(s_dc, k - 1)
                            nc.tensor.matmul(pD[j % 2][:, :], oneT[j % 2][:, :], tile(node_sc, node), start=True, stop=True).then_inc(s_d, 1)

                        def body(i, first):
                            for j in range(U):
                                k = U * i + j
                                pe.wait_ge(s_one, k + 1)
                                if not first or j >= 2:
                                    pe.wait_ge(s_tc, k - 1)
                                nc.tensor.transpose(pT[j % 2][:, :], one[j % 2][:, :], ident[:, :]).then_inc(s_t, 1)
                                if not first or j:
                                    pick(k - 1, (j - 1) % 2, first and j < 3)
                        rolled(pe, body)
                        pick(K - 1, (K - 1) % 2, False)

                    @block.scalar
                    def _(act):
                        def body(i, first):
                            gather_indices(act, ib, s_ib, s_cons, s_gt, i, first)
                            for j in range(U):
                                k = U * i + j
                                act.wait_ge(s_t, k + 1)
                                if not first or j >= 2:
                                    act.wait_ge(s_d, k - 1)
                                nc.scalar.activation(oneT[j % 2][:, :], pT[j % 2][:, :], ACT.Copy).then_inc(s_tc, 1)
                                if not first or j:
                                    act.wait_ge(s_d, k)
                                    nc.scalar.activation(tile(dS, k - 1), pD[(j - 1) % 2][:, :], ACT.Copy).then_inc(s_dc, 1)
                        rolled(act, body)
                        act.wait_ge(s_d, K)
                        nc.scalar.activation(dS[:, K - 1, :], pD[(K - 1) % 2][:, :], ACT.Copy).then_inc(s_dc, 1)

        def edge_softmax(H, gS, dS, slope, zero_to, loops):
            with Stage() as st:
                W = KB * P
                brk = st.sb("brk", [P, W + 1])
                notfirst, notlast = st.sb("notfirst", [P, KB, P]), st.sb("notlast", [P, KB, P])
                starts = st.sb("starts", [P, KB, P]) if loops else None
                bk = st.sb("bk", [P, KB])
                rF, rL = st.sb("rF", [1, KP]), st.sb("rL", [1, KP])
                join = st.sb("join", [1, KP + 1])
                many, thrF, thrB = st.sb("many", [1, KP]), st.sb("thrF", [1, KP]), st.sb("thrB", [1, KP])
                g_h, d_h = st.sb("g_h", [P, KP]), st.sb("d_h", [P, KP])
                gK, dK = st.sb("gK", [P, W]), st.sb("dK", [P, W])
                e, f, m = st.sb("e", [P, W]), st.sb("f", [P, W]), st.sb("m", [P, W])
                u = st.sb("u", [P, W]) if loops else e
                rowA, rowB = st.sb("rowA", [1, KP]), st.sb("rowB", [1, KP])
                cin = st.sb("cin", [P, 2 * KB])
                col = st.sb("col", [P, 2, KB])
                pX = [st.ps(f"pX{q}", [P, 512]) for q in range(4)]
                pR = st.ps("pR", [P, P])
                pC = st.ps("pC", [P, 2 * KB])
                s_v, s_row, s_rc, s_col, s_f, s_hc, s_tr, s_kc = (st.sem(n) for n in ("s_v", "s_row", "s_rc", "s_col", "s_f", "s_hc", "s_tr", "s_kc"))
                s_th, s_rr, s_ci, s_cc, s_df, s_ex, s_bt, s_bc = (st.sem(n) for n in ("s_th", "s_rr", "s_ci", "s_cc", "s_df", "s_ex", "s_bt", "s_bc"))
                R1 = (KB - 4) * P
                dst2 = dstK[:, :, :].rearrange("k b i -> k (b i)")
                out2 = outK[:, :, :].rearrange("k b i -> k (b i)")

                def to_rows(src, sem):
                    for q in range(2):
                        for b in range(KB):
                            ins = nc.tensor.transpose(pX[2 * q + b // 4][0:1, (b % 4) * P:(b % 4 + 1) * P], src[:, q, b:b + 1], ident[:, :])
                    ins.then_inc(sem, 1)

                def from_row(row, at):
                    for b in range(KB):
                        ins = nc.tensor.transpose(pC[:, at + b:at + b + 1], row[0:1, b * P:(b + 1) * P], ident[0:1, 0:1])
                    return ins

                def row_out(q, row):
                    nc.vector.tensor_copy(row[0:1, 0:512], pX[2 * q][0:1, :])
                    return nc.vector.tensor_copy(row[0:1, 512:KP], pX[2 * q + 1][0:1, 0:R1])

                VN = 10 + (2 if zero_to is not None else 0) + (4 if loops else 0)
                with nc.Block() as block:
                    @block.vector
                    def _(dve):
                        flat = lambda t: t[:, :, :].rearrange("k b i -> k (b i)")
                        link = chain(dve, s_f)
                        link(nc.vector.tensor_tensor(brk[:, 1:W], dst2[:, 1:W], dst2[:, 0:W - 1], ALU.not_equal))
                        link(nc.vector.tensor_scalar(brk[:, 1:W], brk[:, 1:W], -BIG, None, ALU.mult))
                        link(nc.vector.memset(brk[:, 0:W + 1:P], -BIG))
                        for out_, at in ((notfirst, 0), (notlast, P - 1)):
                            link(nc.vector.tensor_tensor(out_[:, :, :], dstK[:, :, :], dstK[:, :, at:at + 1].broadcast_to([P, KB, P]), ALU.not_equal))
                            link(nc.vector.tensor_scalar(out_[:, :, :], out_[:, :, :], -BIG, None, ALU.mult))
                            nc.vector.tensor_copy(col[:, at // (P - 1), :], dstK[:, :, at]).then_inc(s_col, 1)
                        dve.wait_ge(s_row, 1)
                        row_out(0, rF)
                        link(row_out(1, rL))
                        link(nc.vector.tensor_tensor(join[0:1, 1:KP], rF[0:1, 1:KP], rL[0:1, 0:KP - 1], ALU.not_equal))
                        link(nc.vector.tensor_scalar(join[0:1, 1:KP], join[0:1, 1:KP], -BIG, None, ALU.mult))
                        link(nc.vector.memset(join[0:1, 0:KP + 1:KP], -BIG))
                        link(nc.vector.tensor_tensor(many[:, :], rF[:, :], rL[:, :], ALU.not_equal))
                        link(nc.vector.tensor_scalar(many[:, :], many[:, :], -BIG, None, ALU.mult))
                        link(nc.vector.tensor_tensor(thrF[:, :], many[:, :], join[:, 0:KP], ALU.add))
                        nc.vector.tensor_tensor(thrB[:, :], many[:, :], join[:, 1:KP + 1], ALU.add).then_inc(s_rc, 1)
                        dve.wait_ge(s_rc, 1)
                        if loops:
                            dve.wait_ge(s_col, 3)
                            link(nc.vector.tensor_scalar(flat(starts), brk[:, 0:W], 0.0, None, ALU.is_lt))
                            link(nc.vector.tensor_scalar(starts[:, :, 0], pC[:, 0:KB], 0.0, None, ALU.is_lt))

                        with dve.Fori(0, H) as h:
                            link = chain(dve, s_v, VN * h)
                            dve.wait_ge(s_kc, h + 1)
                            link(nc.vector.tensor_tensor(gK[:, :], gK[:, :], dK[:, :], ALU.add))
                            link(nc.vector.scalar_tensor_tensor(e[:, :], gK[:, :], slope, gK[:, :], ALU.mult, ALU.max))
                            if zero_to is not None:
                                link(nc.vector.tensor_scalar(gK[:, :], gK[:, :], 0.0, zero_to, ALU.is_equal, ALU.mult))
                                link(nc.vector.tensor_tensor(e[:, :], e[:, :], gK[:, :], ALU.add))
                            link(nc.vector.tensor_tensor(e[:, :], e[:, :], out2, ALU.add))
                            if loops:
                                link(nc.vector.tensor_scalar(dK[:, :], dK[:, :], 2.0, None, ALU.mult))
                                link(nc.vector.scalar_tensor_tensor(dK[:, :], dK[:, :], slope, dK[:, :], ALU.mult, ALU.max))
                                link(nc.vector.tensor_tensor(dK[:, :], dK[:, :], out2, ALU.add))
                                link(nc.vector.tensor_tensor(u[:, :], e[:, :], dK[:, :], ALU.max))
                            link(nc.vector.tensor_tensor_scan(f[:, :], brk[:, 0:W], u[:, :], -BIG, ALU.add, ALU.max))
                            link(nc.vector.tensor_tensor_scan(m[:, ::-1], brk[:, 1:W + 1][:, ::-1], f[:, ::-1], -BIG, ALU.add, ALU.max))
                            m3 = m[:, :].rearrange("k (b i) -> k b i", b=KB)
                            nc.vector.tensor_copy(col[:, 0, :], m3[:, :, P - 1])
                            nc.vector.tensor_copy(col[:, 1, :], m3[:, :, 0]).then_inc(s_th, 1)
                            dve.wait_ge(s_rr, h + 1)
                            row_out(0, rowA)
                            link(row_out(1, rowB))
                            nc.vector.tensor_tensor_scan(rF[:, :], thrF[:, :], rowA[:, :], -BIG, ALU.add, ALU.max)
                            link(nc.vector.tensor_tensor_scan(rL[:, ::-1], thrB[:, ::-1], rowB[:, ::-1], -BIG, ALU.add, ALU.max))
                            nc.vector.memset(rowA[0:1, 0:1], -BIG)
                            nc.vector.tensor_tensor(rowA[0:1, 1:KP], rF[0:1, 0:KP - 1], join[0:1, 1:KP], ALU.add)
                            nc.vector.memset(rowB[0:1, KP - 1:KP], -BIG)
                            nc.vector.tensor_tensor(rowB[0:1, 0:KP - 1], rL[0:1, 1:KP], join[0:1, 1:KP], ALU.add).then_inc(s_ci, 1)
                            dve.wait_ge(s_cc, h + 1)
                            link(nc.vector.tensor_copy(cin[:, :], pC[:, :]))
                            for q, away in enumerate((notfirst, notlast)):
                                for b in range(KB):
                                    ins = nc.vector.scalar_tensor_tensor(m3[:, b, :], away[:, b, :], cin[:, q * KB + b:q * KB + b + 1],
                                                                         m3[:, b, :], ALU.add, ALU.max)
                                link(ins)
                            ins = nc.vector.tensor_tensor(e[:, :], e[:, :], m[:, :], ALU.subtract)
                            if loops:
                                ins = nc.vector.tensor_tensor(dK[:, :], dK[:, :], m[:, :], ALU.subtract)
                            ins.then_inc(s_df, 1)
                            if loops:
                                dve.wait_ge(s_ex, h + 1)
                                nc.vector.tensor_tensor(dK[:, :], dK[:, :], flat(starts), ALU.mult).then_inc(s_df, 1)

                            dve.wait_ge(s_bt, h + 1)
                            for q, t in enumerate((gS, dS) if loops else (gS,)):
                                nc.vector.tensor_scalar(t[:, 0:512, ds(h, 1)].rearrange("p k a -> p (k a)"), pX[2 * q][:, :], 1.0, None, ALU.mult)
                                ins = nc.vector.tensor_scalar(t[:, 512:KP, ds(h, 1)].rearrange("p k a -> p (k a)"), pX[2 * q + 1][:, 0:R1], 1.0, None, ALU.mult)
                            ins.then_inc(s_bc, 1)

                    DF = 2 if loops else 1

                    @block.scalar
                    def _(act):
                        with act.Fori(0, H) as h:
                            nc.scalar.activation(g_h[:, :], gS[:, :, ds(h, 1)].rearrange("p k a -> p (k a)"), ACT.Copy)
                            nc.scalar.activation(d_h[:, :], dS[:, :, ds(h, 1)].rearrange("p k a -> p (k a)"), ACT.Copy).then_inc(s_hc, 1)
                            act.wait_ge(s_tr, h + 1)
                            nc.scalar.activation(gK[:, 0:512], pX[0][:, :], ACT.Copy)
                            nc.scalar.activation(gK[:, 512:W], pX[1][:, 0:R1], ACT.Copy)
                            nc.scalar.activation(dK[:, 0:512], pX[2][:, :], ACT.Copy)
                            nc.scalar.activation(dK[:, 512:W], pX[3][:, 0:R1], ACT.Copy).then_inc(s_kc, 1)
                            act.wait_ge(s_df, DF * h + 1)
                            ins = nc.scalar.activation(e[:, :], e[:, :], ACT.Exp)
                            if loops:
                                ins = nc.scalar.activation(dK[:, :], dK[:, :], ACT.Exp)
                            ins.then_inc(s_ex, 1)
                            act.wait_ge(s_bc, h + 1)

                    @block.tensor
                    def _(pe):
                        pe.wait_ge(s_col, 2)
                        to_rows(col, s_row)
                        pe.wait_ge(s_rc, 1)
                        if loops:
                            from_row(join, 0).then_inc(s_col, 1)

                        def turn(src, q):
                            for b in range(KB):
                                ins = nc.tensor.transpose(pX[2 * q + b // 4][:, (b % 4) * P:(b % 4 + 1) * P], src[:, b * P:(b + 1) * P], ident[:, :])
                            return ins

                        with pe.Fori(0, H) as h:
                            pe.wait_ge(s_hc, h + 1)
                            turn(g_h, 0)
                            turn(d_h, 1).then_inc(s_tr, 1)
                            pe.wait_ge(s_th, h + 1)
                            to_rows(col, s_rr)
                            pe.wait_ge(s_ci, h + 1)
                            nc.tensor.transpose(pR[:, 0:P], ident[:, :], ident[:, :])
                            from_row(rowA, 0)
                            from_row(rowB, KB).then_inc(s_cc, 1)
                            if loops:
                                pe.wait_ge(s_df, DF * h + 2)
                                turn(e, 0)
                                turn(dK, 1).then_inc(s_bt, 1)
                            else:
                                pe.wait_ge(s_ex, h + 1)
                                turn(e, 0).then_inc(s_bt, 1)

        def edge_sum(rows, acc, W, heads, gS, dS):
            with Stage() as se:
                G = [se.sb(f"G{j}", [P, D]) for j in range(U)]
                ib, gate = se.sb("ib", [P, U], I32), se.sb("gate", [1, 3])
                R = 2
                one = [se.sb(f"one{j}", [P, P]) for j in range(R)]
                msg = [se.sb(f"msg{j}", [P, W]) for j in range(R)] if heads else None
                pM = [se.ps(f"pM{j}", [P, W]) for j in range(2)]
                s_ib, s_gt, s_one, s_ex, s_m, s_acc = (se.sem(n) for n in ("s_ib", "s_gt", "s_one", "s_ex", "s_m", "s_acc"))
                s_g = [se.sem(f"s_g{j}") for j in range(U)]
                s_cons = s_one if heads else s_m
                with nc.Block() as block:
                    @block.gpsimd
                    def _(pool):
                        pool.memset(gate[:, :], 1.0).then_inc(s_gt, 1)
                        pool.wait_ge(s_gt, 1)
                        rolled(pool, lambda i, first: gather_rows(pool, G, ib, gate, rows, s_ib, s_g, s_gt, i))

                    @block.scalar
                    def _(act):
                        def body(i, first):
                            gather_indices(act, ib, s_ib, s_cons, s_gt, i, first)
                            if heads:
                                for j in range(U):
                                    k = U * i + j
                                    if not first or j >= R:
                                        act.wait_ge(s_m, k - R + 1)
                                    ins = nc.scalar.activation(msg[j % R][:, D:D + heads], tile(gS, k), ACT.Copy)
                                    if dS is not None:
                                        ins = nc.scalar.activation(msg[j % R][:, D + heads:W], tile(dS, k), ACT.Copy)
                                    ins.then_inc(s_ex, 1)
                        rolled(act, body)

                    @block.vector
                    def _(dve):
                        def add(k, j):
                            node = dve.value_load(nodeR[0:1, ds(k, 1)], min_val=0, max_val=NT - 1)
                            dve.wait_ge(s_m, k + 1)
                            if type(k) is not int or k:
                                dve.wait_ge(s_acc, k)
                            nc.vector.tensor_tensor(tile(acc, node), tile(acc, node), pM[j % 2][:, :], ALU.add).then_inc(s_acc, 1)

                        def body(i, first):
                            for j in range(U):
                                k = U * i + j
                                if not first or j >= R:
                                    dve.wait_ge(s_m, k - R + 1)
                                if heads:
                                    nc.vector.tensor_scalar(one[j % R][:, :], iota[:, :], relS[:, ds(k, 1)], None, ALU.is_equal)
                                    dve.wait_ge(s_g[j], 16 * i + 16)
                                    nc.vector.tensor_tensor(msg[j % R][:, 0:D].rearrange("p (h c) -> p h c", h=heads),
                                                            G[j][:, :].rearrange("p (h c) -> p h c", h=heads),
                                                            gS[:, ds(k, 1), :].rearrange("p a h -> p h a").broadcast_to([P, heads, D // heads]),
                                                            ALU.mult).then_inc(s_one, 1)
                                else:
                                    nc.vector.tensor_scalar(one[j % R][:, :], iota[:, :], relS[:, ds(k, 1)], wS[:, ds(k, 1)],
                                                            ALU.is_equal, ALU.mult).then_inc(s_one, 1)
                                if not first or j:
                                    add(k - 1, (j - 1) % 2)
                        rolled(dve, body)
                        add(K - 1, (K - 1) % 2)

                    @block.tensor
                    def _(pe):
                        def body(i, first):
                            for j in range(U):
                                k = U * i + j
                                pe.wait_ge(s_one, k + 1)
                                if heads:
                                    pe.wait_ge(s_ex, k + 1)
                                else:
                                    pe.wait_ge(s_g[j], 16 * i + 16)
                                if not first or j >= 2:
                                    pe.wait_ge(s_acc, k - 1)
                                nc.tensor.matmul(pM[j % 2][:, :], one[j % R][:, :], (msg[j % R] if heads else G[j])[:, :],
                                                 start=True, stop=True).then_inc(s_m, 1)
                        rolled(pe, body)

        def batch_norm(acc, gain, bias, rsg, brow):
            with Stage() as st:
                lane = st.sb("lane", [P, 1])
                live = st.sb("live", [P, 1])
                part = st.sb("part", [P, D])
                mean, var, vt = st.sb("mean", [P, D]), st.sb("var", [P, D]), st.sb("vt", [P, D])
                sq = [st.sb(f"sq{j}", [P, D]) for j in range(2)]
                grow = st.sb("grow", [P, D])
                pS = st.ps("pS", [P, D])
                s_l, s_b, s_c, s_p, s_s, s_rt, s_q, s_a = (st.sem(n) for n in ("s_l", "s_b", "s_c", "s_p", "s_s", "s_rt", "s_q", "s_a"))
                nodes = lambda t: t[:, 0:FULL + 1, 0:D]
                with nc.Block() as block:
                    @block.gpsimd
                    def _(pool):
                        pool.iota(lane[:, :], [[0, 1]], base=0, channel_multiplier=1, allow_small_or_imprecise_dtypes=True).then_inc(s_l, 1)

                    @block.sync
                    def _(sp):
                        sp.dma_start(grow[:, :], gain.rearrange("(a n) -> a n", a=1).broadcast_to([P, D])).then_inc(s_b, 16)
                        sp.dma_start(brow[:, :], bias.rearrange("(a n) -> a n", a=1).broadcast_to([P, D])).then_inc(s_b, 16)

                    @block.vector
                    def _(dve):
                        link = chain(dve, s_c)
                        dve.wait_ge(s_l, 1)
                        link(nc.vector.tensor_scalar(live[:, :], lane[:, :], float(REST), None, ALU.is_lt))
                        link(nc.vector.tensor_scalar(acc[:, FULL, 0:D], acc[:, FULL, 0:D], live[:, :], None, ALU.mult))
                        nc.vector.tensor_reduce(part[:, :], nodes(acc).rearrange("p t c -> p c t"), AX.X, ALU.add).then_inc(s_p, 1)
                        dve.wait_ge(s_s, 1)
                        link(nc.vector.tensor_scalar(mean[:, :], pS[:, :], 1 / N, None, ALU.mult))
                        link(nc.vector.tensor_tensor(nodes(acc), nodes(acc), mean[:, :].unsqueeze(1).broadcast_to([P, FULL + 1, D]), ALU.subtract))
                        link(nc.vector.tensor_scalar(acc[:, FULL, 0:D], acc[:, FULL, 0:D], live[:, :], None, ALU.mult))
                        nc.vector.memset(part[:, :], 0.0).then_inc(s_q, 1)

                        def add_square(n, j):
                            dve.wait_ge(s_a, n + 1)
                            dve.wait_ge(s_q, n + 1)
                            nc.vector.tensor_tensor(part[:, :], part[:, :], sq[j][:, :], ALU.add).then_inc(s_q, 1)
                        with dve.Fori(0, FULL // 2) as i:
                            add_square(2 * i, 0)
                            add_square(2 * i + 1, 1)
                        add_square(FULL, 0)
                        dve.wait_ge(s_s, 2)
                        nc.vector.tensor_scalar(var[:, :], pS[:, :], 1 / N, EPS, ALU.mult, ALU.add).then_inc(s_rt, 1)
                        dve.wait_ge(s_rt, 2)
                        link(nc.vector.reciprocal(rsg[:, :], rsg[:, :]))
                        newton_rsqrt(link, rsg[:, :], var[:, :], vt[:, :])
                        dve.wait_ge(s_b, 32)
                        link(nc.vector.tensor_tensor(rsg[:, :], rsg[:, :], grow[:, :], ALU.mult))

                    @block.scalar
                    def _(act):
                        act.wait_ge(s_q, 1)

                        def square(n, j, early=False):
                            if not early:
                                act.wait_ge(s_q, n)
                            nc.scalar.activation(sq[j][:, :], tile(acc[:, :, 0:D], n), ACT.Square).then_inc(s_a, 1)
                        square(0, 0, True)
                        square(1, 1, True)
                        with act.Fori(1, FULL // 2) as i:
                            square(2 * i, 0)
                            square(2 * i + 1, 1)
                        square(FULL, 0)
                        act.wait_ge(s_rt, 1)
                        nc.scalar.activation(rsg[:, :], var[:, :], ACT.Sqrt).then_inc(s_rt, 1)

                    @block.tensor
                    def _(pe):
                        for sem, value in ((s_p, 1), (s_q, FULL + 2)):
                            pe.wait_ge(sem, value)
                            nc.tensor.matmul(pS[:, :], ones[:, :], part[:, :], start=True, stop=True).then_inc(s_s, 1)

        def tile_pairs(eng, body):
            body(0, True)
            with eng.Fori(1, NT // 2) as i:
                body(i, False)

        def newton_rsqrt(link, r, v, t):
            link(nc.vector.tensor_tensor(t, r, r, ALU.mult))
            link(nc.vector.tensor_tensor(t, t, v, ALU.mult))
            link(nc.vector.tensor_scalar(t, t, -0.5, 1.5, ALU.mult, ALU.add))
            link(nc.vector.tensor_tensor(r, r, t, ALU.mult))

        def tile(t, n):
            return t[:, ds(n, 1), :].rearrange("p a c -> p (a c)")

        def layernorm_stats(x_sb, rstd, shift):
            with Stage() as st:
                bn = st.sb("bn", [P, NT, 6])
                mean, dif, ve = st.sb("mean", [P, NT]), st.sb("dif", [P, NT]), st.sb("ve", [P, NT])
                s_bn, s_ve, s_rt, s_ch = (st.sem(n) for n in ("s_bn", "s_ve", "s_rt", "s_ch"))
                with nc.Block() as block:
                    @block.vector
                    def _(dve):
                        with dve.Fori(0, NT // 2) as i:
                            for j in range(2):
                                ins = nc.vector.bn_stats(tile(bn, 2 * i + j), tile(x_sb, 2 * i + j))
                            ins.then_inc(s_bn, 1)
                        dve.wait_ge(s_bn, NT // 2)
                        link = chain(dve, s_ch)
                        link(nc.vector.tensor_tensor(mean[:, :], bn[:, :, 1], bn[:, :, 4], ALU.add))
                        link(nc.vector.tensor_tensor(dif[:, :], bn[:, :, 1], bn[:, :, 4], ALU.subtract))
                        link(nc.vector.tensor_tensor(ve[:, :], bn[:, :, 2], bn[:, :, 5], ALU.add))
                        link(nc.vector.tensor_tensor(dif[:, :], dif[:, :], dif[:, :], ALU.mult))
                        link(nc.vector.tensor_scalar(ve[:, :], ve[:, :], 1 / D, EPS, ALU.mult, ALU.add))
                        nc.vector.scalar_tensor_tensor(ve[:, :], dif[:, :], 0.25, ve[:, :], ALU.mult, ALU.add).then_inc(s_ve, 1)
                        dve.wait_ge(s_rt, 1)
                        link(nc.vector.reciprocal(rstd[:, :], rstd[:, :]))
                        newton_rsqrt(link, rstd[:, :], ve[:, :], dif[:, :])
                        link(nc.vector.scalar_tensor_tensor(shift[:, :], mean[:, :], -0.5, rstd[:, :], ALU.mult, ALU.mult))

                    @block.scalar
                    def _(act):
                        act.wait_ge(s_ve, 1)
                        nc.scalar.activation(rstd[:, :], ve[:, :], ACT.Sqrt).then_inc(s_rt, 1)

        def node_stage(layer, x_sb, rstd, shift, wide, load, biases, act_end, dve_end, store, ready=None):
            with Stage() as st:
                y = [st.sb(f"y{j}", [P, D]) for j in range(2)]
                yT = [st.sb(f"yT{j}", [P, D]) for j in range(2)]
                ready = ready or {}
                w_sb = [ready[q] if q in ready else st.sb(f"w_sb{q}", [P, 2, w]) for q, w in enumerate(wide)]
                b_sb = [st.sb(f"b_sb{q}", [1, w]) if biases[q] else None for q, w in enumerate(wide)]
                pT = [st.ps(f"pT{j}", [P, D]) for j in range(2)]
                pO = [[st.ps(f"pO{j}_{q}", [P, w]) for q, w in enumerate(wide)] for j in range(2)]
                row = [st.sb(f"row{j}", [P, D]) for j in range(2)]
                aux = [st.sb(f"aux{j}", [P, D]) for j in range(2)]
                s_w, s_y, s_t, s_yt, s_o, s_ae, s_de = (st.sem(n) for n in ("s_w", "s_y", "s_t", "s_yt", "s_o", "s_ae", "s_de"))
                s_st = [st.sem(f"s_st{j}") for j in range(2)]
                loads = []
                n_st = len(store)

                with nc.Block() as block:
                    @block.sync
                    def _(sp):
                        for dst, src in load(w_sb, b_sb):
                            loads.append(sp.dma_start(dst, src).then_inc(s_w, 16))

                        def body(i, first):
                            for j in range(2):
                                sp.wait_ge(s_ae, 2 * i + j + 1)
                                sp.wait_ge(s_de, 2 * i + j + 1)
                                for dst, src in store:
                                    sp.dma_start(dst(2 * i + j), src(row[j], aux[j])).then_inc(s_st[j], 16)
                        tile_pairs(sp, body)
                        for j in range(2):
                            sp.wait_ge(s_st[j], 16 * n_st * (NT // 2))

                    @block.scalar
                    def _(act):
                        def body(i, first):
                            for j in range(2):
                                n = 2 * i + j
                                if not first:
                                    act.wait_ge(s_t, n - 1)
                                nc.scalar.activation(y[j][:, :], tile(x_sb, n), ACT.Relu, bias=shift[:, ds(n, 1)],
                                                     scale=rstd[:, ds(n, 1)]).then_inc(s_y, 1)
                            for j in range(2):
                                n = 2 * i + j
                                act.wait_ge(s_o, n + 1)
                                if not first:
                                    act.wait_ge(s_st[j], 16 * n_st * i)
                                act_end(act, n, j, pO[j], row[j], aux[j]).then_inc(s_ae, 1)
                        tile_pairs(act, body)

                    @block.vector
                    def _(dve):
                        def body(i, first):
                            for j in range(2):
                                n = 2 * i + j
                                dve.wait_ge(s_t, n + 1)
                                if not first:
                                    dve.wait_ge(s_o, n - 1)
                                nc.vector.tensor_copy(yT[j][:, :], pT[j][:, :]).then_inc(s_yt, 1)
                            for j in range(2):
                                n = 2 * i + j
                                dve.wait_ge(s_o, n + 1)
                                if not first:
                                    dve.wait_ge(s_st[j], 16 * n_st * i)
                                dve_end(dve, n, j, pO[j], row[j], aux[j], s_ae).then_inc(s_de, 1)
                        tile_pairs(dve, body)

                    @block.tensor
                    def _(pe):
                        pe.wait_ge(s_w, 16 * len(loads))

                        def body(i, first):
                            for j in range(2):
                                n = 2 * i + j
                                pe.wait_ge(s_y, n + 1)
                                if not first:
                                    pe.wait_ge(s_yt, n - 1)
                                for c in range(2):
                                    ins = nc.tensor.transpose(pT[j][:, c * P:(c + 1) * P], y[j][:, c * P:(c + 1) * P], ident[:, :])
                                ins.then_inc(s_t, 1)
                            for j in range(2):
                                n = 2 * i + j
                                pe.wait_ge(s_yt, n + 1)
                                if not first:
                                    pe.wait_ge(s_ae, n - 1)
                                    pe.wait_ge(s_de, n - 1)
                                for q, w in enumerate(wide):
                                    if biases[q]:
                                        nc.tensor.matmul(pO[j][q][:, :], ones[0:1, :], b_sb[q][0:1, :], start=True, stop=False)
                                    for c in range(2):
                                        ins = nc.tensor.matmul(pO[j][q][:, :], yT[j][:, c * P:(c + 1) * P], w_sb[q][:, c, :],
                                                               start=(c == 0 and not biases[q]), stop=(c == 1))
                                ins.then_inc(s_o, 1)
                        tile_pairs(pe, body)

        def load_nodes(x_sb, src, rows):
            with Stage() as st:
                s_z, s_x = st.sem("s_z"), st.sem("s_x")
                with nc.Block() as block:
                    @block.vector
                    def _(dve):
                        nc.vector.memset(x_sb[:, FULL:NT, :], 0.0).then_inc(s_z, 1)

                    @block.sync
                    def _(sp):
                        sp.dma_start(x_sb[:, 0:FULL, :], src[0:FULL * P, :].rearrange("(t p) c -> p t c", p=P)).then_inc(s_x, 16)
                        sp.wait_ge(s_z, 1)
                        sp.dma_start(x_sb[0:REST, FULL, :], src[FULL * P:N, :]).then_inc(s_x, 16)
                        sp.wait_ge(s_x, 32)

        def rolled(eng, body):
            body(0, True)
            with eng.Fori(1, K // U) as i:
                body(i, False)

        with Stage() as st0:
            a4S = st0.sb("a4S", [P, 4, KP])
            a10S = st0.sb("a10S", [P, NBAS, KP])
            with Stage() as st:
                zf = st.sb("zf", [P, 2 * D])
                padi = st.sb("padi", [1, 2, P], I32)
                frow_i = st.sb("frow_i", [1, ET], I32)
                trow_i = st.sb("trow_i", [1, ET], I32)
                frow = st.sb("frow", [1, ET])
                trow = st.sb("trow", [1, ET])
                kcol_i = st.sb("kcol_i", [P, KB], I32)
                kcol = st.sb("kcol", [P, KB])
                hit = st.sb("hit", [P, ET - 1])
                tk = st.sb("tk", [P, KB])
                tki = st.sb("tki", [P, KB], I32)
                nk = st.sb("nk", [P, KB])
                nkc = st.sb("nkc", [P, KB])
                nki = st.sb("nki", [P, KB], I32)
                base = st.sb("base", [P, KB])
                relK = st.sb("relK", [P, KB, P])
                m1 = st.sb("m1", [P, KB, P])
                gt = st.sb("gt", [MUL, 2, 3, 3 * MUL])
                nodeF = st.sb("nodeF", [P, KP])
                gdst = st.sb("gdst", [P, KB, P], I32)
                gsrc = st.sb("gsrc", [P, KB, P], I32)
                gsf = st.sb("gsf", [P, KB, P])
                gw = st.sb("gw", [P, KB, P])
                g4 = st.sb("g4", [P, 4 * P])
                g10 = st.sb("g10", [P, NBAS * P])
                oh4 = st.sb("oh4", [P, 2, 4, P], BF16)
                deg = st.sb("deg", [P, NT])
                degt = st.sb("degt", [P, NT])
                zb = st.sb("zb", [P, P], BF16)
                nh4 = st.sb("nh4", [P, 2, 4, NT], BF16)
                pS = [st.ps(f"pS{n}", [P, (ET - 1) // 2]) for n in range(2)]
                pT = [st.ps(f"pT{n}", [P, P]) for n in range(4)]
                pC = st.ps("pC", [P, NT])
                s_const, s_zero, s_pad, s_first, s_row = (st.sem(n) for n in ("s_const", "s_zero", "s_pad", "s_first", "s_row"))
                s_ts, s_v, s_tk, s_nd, s_ndd, s_ndr = (st.sem(n) for n in ("s_ts", "s_v", "s_tk", "s_nd", "s_ndd", "s_ndr"))
                s_w1, s_w2, s_gd, s_gs, s_gw = (st.sem(n) for n in ("s_w1", "s_w2", "s_gd", "s_gs", "s_gw"))
                s_g4, s_g10, s_kf, s_tr, s_cp = (st.sem(n) for n in ("s_g4", "s_g10", "s_kf", "s_tr", "s_cp"))
                s_oh, s_cn, s_pc, s_deg = (st.sem(n) for n in ("s_oh", "s_cn", "s_pc", "s_deg"))
                PADS = E // 50

                with nc.Block() as block:
                    @block.sync
                    def _(sp):
                        for dst, src, w in ((dst_pad, a["dst"], 1), (src_pad, a["src"], 1), (w_pad, a["edge_weight"], 1),
                                            (a4_pad, a["edge_attr_4"].rearrange("e c -> (e c)"), 4),
                                            (a10_pad, a["edge_attr_10"].rearrange("e c -> (e c)"), NBAS)):
                            sp.dma_start(dst[0:E * w].rearrange("(a b) -> a b", a=50 * w),
                                         src.rearrange("(a b) -> a b", a=50 * w)).then_inc(s_pad, 16)
                        sp.wait_ge(s_zero, 3)
                        sp.dma_start(dst_pad[E:EPAD].rearrange("(a b) -> a b", a=1), padi[0:1, 0, 0:EPAD - E]).then_inc(s_pad, 16)
                        sp.dma_start(src_pad[E:EPAD].rearrange("(a b) -> a b", a=1), padi[0:1, 1, 0:EPAD - E]).then_inc(s_pad, 16)
                        sp.dma_start(w_pad[E:EPAD].rearrange("(a b) -> a b", a=1), zf[0:1, 0:EPAD - E]).then_inc(s_pad, 16)
                        sp.dma_start(a4_pad[4 * E:4 * EPAD].rearrange("(a b) -> a b", a=4), zf[0:4, 0:EPAD - E]).then_inc(s_pad, 16)
                        sp.dma_start(a10_pad[NBAS * E:NBAS * EPAD].rearrange("(a b) -> a b", a=NBAS), zf[0:NBAS, 0:EPAD - E]).then_inc(s_pad, 16)
                        sp.wait_ge(s_pad, 160)
                        with nc.allow_non_contiguous_dma(reason="one dst of each edge tile"):
                            sp.dma_start(frow_i[0:1, :], dst_pad.rearrange("(a t p) -> a t p", a=1, p=P)[:, :, 0]).then_inc(s_first, 16)
                        sp.wait_ge(s_nd, 1)
                        with nc.allow_non_contiguous_dma(reason="896 step entries"):
                            sp.dma_start(node_i.rearrange("(b p) -> p b", p=P), nki[:, :]).then_inc(s_ndd, 16)
                            sp.dma_start(node_f.rearrange("(b p) -> p b", p=P), nkc[:, :]).then_inc(s_ndd, 16)
                        sp.wait_ge(s_ndd, 32)
                        sp.dma_start(nodeR[0:1, :], node_i.rearrange("(a k) -> a k", a=1)).then_inc(s_ndr, 16)
                        sp.dma_start(nodeF[:, :], node_f.rearrange("(a k) -> a k", a=1).broadcast_to([P, KP])).then_inc(s_ndr, 16)
                        for r in range(2):
                            sp.dma_start(wbig[r * P:(r + 1) * P, :], zf[:, :]).then_inc(s_w1, 16)
                        sp.wait_ge(s_zero, 4)
                        for f, (w0, w1) in enumerate((("L0_gnn_W_li0", "L0_gnn_W_li1"), ("L0_gnn_W_lm0", "L0_gnn_W_lm1"))):
                            for m in range(3):
                                sp.dma_start(gt[:, f, m, m * MUL:(m + 1) * MUL], a[w1]).then_inc(s_w1, 16)
                        sp.wait_ge(s_w1, 128)
                        for f, w0 in enumerate(("L0_gnn_W_li0", "L0_gnn_W_lm0")):
                            sp.dma_start(wbig[0:MUL, f * D:f * D + MUL], a[w0]).then_inc(s_w2, 16)
                            sp.dma_start(wbig[MUL:D, f * D + MUL:(f + 1) * D].rearrange("(u m) c -> u m c", m=3),
                                         gt[:, f, :, :]).then_inc(s_w2, 16)
                        sp.wait_ge(s_w2, 64)
                        sp.wait_ge(s_ndr, 32)

                    @block.gpsimd
                    def _(pool):
                        pool.iota(kcol_i[:, :], [[P, KB]], base=0, channel_multiplier=1).then_inc(s_const, 1)
                        pool.iota(trow_i[:, :], [[1, ET]], base=0, channel_multiplier=0).then_inc(s_const, 1)
                        pool.iota(iota[:, :], [[1, P]], base=0, channel_multiplier=0,
                                  allow_small_or_imprecise_dtypes=True).then_inc(s_const, 1)
                        pool.memset(ident[:, :], 0.0).then_inc(s_const, 1)
                        pool.wait_ge(s_const, 4)
                        pool.affine_select(out=ident[:, :], in_=ident[:, :], compare_op=ALU.not_equal, fill=1.0, base=0,
                                           pattern=[[-1, P]], channel_multiplier=1).then_inc(s_const, 1)
                        pool.wait_ge(s_tk, 1)
                        for b in range(KB):
                            at = bass.IndirectOffsetOnAxis(ap=tki[:, b:b + 1], axis=0)
                            rows = lambda t: t.rearrange("(t q) -> t q", t=ET)
                            pool.indirect_dma_start(gdst[:, b, :], None, rows(dst_pad), at).then_inc(s_gd, 16)
                            pool.indirect_dma_start(gsrc[:, b, :], None, rows(src_pad), at).then_inc(s_gs, 16)
                            pool.indirect_dma_start(gw[:, b, :], None, rows(w_pad), at).then_inc(s_gw, 16)
                        for b in range(KB):
                            if b:
                                pool.wait_ge(s_tr, 3 * KB + 14 * (b - 1) + 4)
                            pool.indirect_dma_start(g4[:, :], None, rows(a4_pad), bass.IndirectOffsetOnAxis(ap=tki[:, b:b + 1], axis=0)).then_inc(s_g4, 16)
                            if b:
                                pool.wait_ge(s_tr, 3 * KB + 14 * b)
                            pool.indirect_dma_start(g10[:, :], None, rows(a10_pad), bass.IndirectOffsetOnAxis(ap=tki[:, b:b + 1], axis=0)).then_inc(s_g10, 16)

                    @block.vector
                    def _(dve):
                        nc.vector.memset(zf[:, :], 0.0).then_inc(s_zero, 1)
                        nc.vector.memset(padi[0:1, 0, :], NOWHERE).then_inc(s_zero, 1)
                        nc.vector.memset(padi[0:1, 1, :], 0).then_inc(s_zero, 1)
                        nc.vector.memset(gt[:, :, :, :], 0.0).then_inc(s_zero, 1)
                        nc.vector.memset(ones[:, :], 1.0).then_inc(s_zero, 1)
                        nc.vector.memset(zb[:, :], 0.0).then_inc(s_zero, 1)
                        link = chain(dve, s_v)
                        dve.wait_ge(s_const, 5)
                        dve.wait_ge(s_first, 16)
                        link(nc.vector.tensor_scalar(frow_i[:, :], frow_i[:, :], 7, None, ALU.arith_shift_right))
                        link(nc.vector.tensor_copy(frow[:, :], frow_i[:, :]))
                        link(nc.vector.tensor_copy(trow[:, :], trow_i[:, :]))
                        link(nc.vector.tensor_tensor(frow[:, :], frow[:, :], trow[:, :], ALU.add))
                        nc.vector.tensor_copy(kcol[:, :], kcol_i[:, :]).then_inc(s_row, 1)
                        dve.wait_ge(s_row, 1)
                        dve.wait_ge(s_ts, 2)
                        for b in range(KB):
                            for n in range(2):
                                link(nc.vector.tensor_scalar(hit[:, n * (ET // 2):(n + 1) * (ET // 2)], pS[n][:, :],
                                                             kcol[:, b:b + 1], None, ALU.is_le))
                            link(nc.vector.tensor_reduce(tk[:, b:b + 1], hit[:, :], AX.X, ALU.add))
                        link(nc.vector.tensor_copy(tki[:, :], tk[:, :]))
                        nc.vector.tensor_tensor(nk[:, :], kcol[:, :], tk[:, :], ALU.subtract).then_inc(s_tk, 1)
                        dve.wait_ge(s_tk, 1)
                        link(nc.vector.tensor_scalar(nkc[:, :], nk[:, :], float(NT - 1), None, ALU.min))
                        link(nc.vector.tensor_scalar(base[:, :], nk[:, :], float(-P), None, ALU.mult))
                        nc.vector.tensor_copy(nki[:, :], nkc[:, :]).then_inc(s_nd, 1)
                        dve.wait_ge(s_gd, 16 * KB)
                        link(nc.vector.tensor_copy(dstK[:, :, :], gdst[:, :, :]))
                        for b in range(KB):
                            last = nc.vector.tensor_scalar(relK[:, b, :], dstK[:, b, :], base[:, b:b + 1], None, ALU.add)
                        link(last)
                        dve.wait_ge(s_gs, 16 * KB)
                        dve.wait_ge(s_gw, 16 * KB)
                        nc.vector.tensor_copy(gsf[:, :, :], gsrc[:, :, :]).then_inc(s_kf, 1)
                        link(nc.vector.tensor_scalar(m1[:, :, :], relK[:, :, :], 0.0, -BIG, ALU.is_lt, ALU.mult))
                        link(nc.vector.tensor_scalar(outK[:, :, :], relK[:, :, :], float(P), -BIG, ALU.is_ge, ALU.mult))
                        link(nc.vector.tensor_tensor(outK[:, :, :], outK[:, :, :], m1[:, :, :], ALU.add))
                        dve.wait_ge(s_ndr, 32)
                        dve.wait_ge(s_cp, 3 * KB)
                        with dve.Fori(0, K // 8) as i:
                            for h in range(2):
                                dve.wait_ge(s_cn, 2 * i + h + 1)
                                nc.vector.tensor_tensor(oh4[:, h, :, :], iota[:, :].unsqueeze(1).broadcast_to([P, 4, P]),
                                                        relS[:, ds(8 * i + 4 * h, 4)].unsqueeze(2).broadcast_to([P, 4, P]), ALU.is_equal)
                                nc.vector.tensor_tensor(nh4[:, h, :, :], iota[:, 0:NT].unsqueeze(1).broadcast_to([P, 4, NT]),
                                                        nodeF[:, ds(8 * i + 4 * h, 4)].unsqueeze(2).broadcast_to([P, 4, NT]),
                                                        ALU.is_equal).then_inc(s_oh, 1)
                        dve.wait_ge(s_pc, 1)
                        nc.vector.tensor_copy(cnt[:, :], pC[:, :]).then_inc(s_pc, 1)
                        dve.wait_ge(s_pc, 2)
                        nc.vector.tensor_scalar(deg[:, :], cnt[:, :], 1.0, None, ALU.max).then_inc(s_deg, 1)
                        dve.wait_ge(s_deg, 2)
                        link(nc.vector.reciprocal(dis[:, :], dis[:, :]))
                        newton_rsqrt(link, dis[:, :], deg[:, :], degt[:, :])

                    @block.tensor
                    def _(pe):
                        pe.wait_ge(s_zero, 6)
                        pe.wait_ge(s_row, 1)
                        for n in range(2):
                            nc.tensor.matmul(pS[n][:, :], ones[0:1, :], frow[0:1, 1 + n * (ET // 2):1 + (n + 1) * (ET // 2)],
                                             start=True, stop=True).then_inc(s_ts, 1)
                        pe.wait_ge(s_kf, 1)
                        count = 0

                        def turn(src):
                            nonlocal count
                            if count >= 4:
                                pe.wait_ge(s_cp, count - 3)
                            nc.tensor.transpose(pT[count % 4][:, :], src, ident[:, :]).then_inc(s_tr, 1)
                            count += 1

                        for g in (relK, gsf, gw):
                            for b in range(KB):
                                turn(g[:, b, :])
                        for b in range(KB):
                            pe.wait_ge(s_g4, 16 * b + 16)
                            for c in range(4):
                                turn(g4[:, :].rearrange("k (e c) -> k c e", c=4)[:, c, :])
                            pe.wait_ge(s_g10, 16 * b + 16)
                            for c in range(NBAS):
                                turn(g10[:, :].rearrange("k (e c) -> k c e", c=NBAS)[:, c, :])
                        nc.tensor.matmul(pC[:, :], zb[:, :], zb[:, 0:NT], start=True, stop=False).then_inc(s_cn, 2)
                        with pe.Fori(0, K // 8) as i:
                            for h in range(2):
                                pe.wait_ge(s_oh, 2 * i + h + 1)
                                for q in range(4):
                                    ins = nc.tensor.matmul(pC[:, :], oh4[:, h, q, :], nh4[:, h, q, :], start=False, stop=False)
                                ins.then_inc(s_cn, 1)
                        nc.tensor.matmul(pC[:, :], zb[:, :], zb[:, 0:NT], start=False, stop=True).then_inc(s_pc, 1)

                    @block.scalar
                    def _(act):
                        count = 0
                        for dst in (relS, srcI, wS):
                            for b in range(KB):
                                act.wait_ge(s_tr, count + 1)
                                nc.scalar.activation(dst[:, b * P:(b + 1) * P], pT[count % 4][:, :], ACT.Copy).then_inc(s_cp, 1)
                                count += 1
                        for b in range(KB):
                            for dst, w in ((a4S, 4), (a10S, NBAS)):
                                for c in range(w):
                                    act.wait_ge(s_tr, count + 1)
                                    nc.scalar.activation(dst[:, c, b * P:(b + 1) * P], pT[count % 4][:, :], ACT.Copy).then_inc(s_cp, 1)
                                    count += 1
                        act.wait_ge(s_deg, 1)
                        nc.scalar.activation(dis[:, :], deg[:, :], ACT.Sqrt).then_inc(s_deg, 1)
            attr = st0.sb("attr", [P, NT])
            sc_f = st0.sb("sc_f", [P, NT])
            sc_m = st0.sb("sc_m", [P, NT])
            sc_o = st0.sb("sc_o", [P, NT])
            with Stage() as st:
                s_a0, s_a, s_c = st.sem("s_a0"), st.sem("s_a"), st.sem("s_c")
                with nc.Block() as block:
                    @block.sync
                    def _(sp):
                        sp.wait_ge(s_a0, 1)
                        vec = a["node_vec1"].rearrange("n o -> (n o)")
                        with nc.allow_non_contiguous_dma(reason="6250 attributes, node on partition"):
                            sp.dma_start(attr[:, 0:FULL], vec[0:FULL * P].rearrange("(t p) -> p t", p=P)).then_inc(s_a, 16)
                            sp.dma_start(attr[0:REST, FULL:FULL + 1], vec[FULL * P:N].rearrange("(p o) -> p o", o=1)).then_inc(s_a, 16)

                    @block.vector
                    def _(dve):
                        nc.vector.memset(attr[:, :], 0.0).then_inc(s_a0, 1)
                        dve.wait_ge(s_a, 32)
                        link = chain(dve, s_c)
                        link(nc.vector.tensor_tensor(sc_f[:, :], attr[:, :], dis[:, :], ALU.mult))
                        link(nc.vector.tensor_scalar(sc_o[:, :], sc_f[:, :], math.cos(math.pi / 8) / math.sqrt(2 * MUL), None, ALU.mult))
                        link(nc.vector.tensor_scalar(sc_f[:, :], sc_f[:, :], 1 / math.sqrt(MUL), None, ALU.mult))
                        link(nc.vector.tensor_scalar(sc_m[:, :], attr[:, :], math.sin(math.pi / 8) / math.sqrt(MUL), None, ALU.mult))

            with Stage() as st:
                x_sb = st.sb("x_in", [P, NT, D])
                rstd, shift = st.sb("rstd0", [P, NT]), st.sb("shift0", [P, NT])
                load_nodes(x_sb, a["x"], N)
                layernorm_stats(x_sb, rstd, shift)

                def act_end(act, n, j, pO, row, aux):
                    return nc.scalar.activation(row[:, :], pO[0][:, 0:D], ACT.Copy, scale=sc_f[:, ds(n, 1)])

                def dve_end(dve, n, j, pO, row, aux, s_ae):
                    xt = tile(x_sb, n)
                    nc.vector.scalar_tensor_tensor(aux[:, 0:MUL], pO[1][:, 0:MUL], sc_m[:, ds(n, 1)], xt[:, 0:MUL],
                                                   ALU.mult, ALU.add)
                    return nc.vector.scalar_tensor_tensor(
                        aux[:, MUL:D].rearrange("p (k m) -> p m k", m=3), pO[1][:, MUL:D].rearrange("p (m k) -> p m k", m=3),
                        sc_m[:, ds(n, 1)], xt[:, MUL:D].rearrange("p (k m) -> p m k", m=3), ALU.mult, ALU.add)

                node_stage(0, x_sb, rstd, shift, [D, D],
                           lambda w, b: [(w[q][:, :, :], wbig[:, q * D:(q + 1) * D].rearrange("(c p) n -> p c n", p=P)) for q in range(2)],
                           [False, False], act_end, dve_end,
                           [(lambda n: table[0][ds(n * P, P), :], lambda row, aux: row[:, :]),
                            (lambda n: base0[ds(n * P, P), :], lambda row, aux: aux[:, :])])

            with Stage() as st:
                acc = st.sb("acc0", [P, NT, 2 * D])
                with Stage() as se:
                    G = [se.sb(f"G{j}", [P, D]) for j in range(U)]
                    ib = se.sb("ib", [P, U], I32)
                    gate = se.sb("gate", [1, 3])
                    w1p = se.sb("w1p", [4 * NBAS, 4, NHID])
                    w1s = se.sb("w1s", [4 * NBAS, NHID])
                    w2s = se.sb("w2s", [NHID, D])
                    a10 = [se.sb(f"a10_{h}", [P, P]) for h in range(2)]
                    a10T = [se.sb(f"a10T_{h}", [4 * NBAS, P]) for h in range(2)]
                    hid = [se.sb(f"hid{j}", [NHID, P]) for j in range(2)]
                    oh = [se.sb(f"oh{j}", [P, 4, P]) for j in range(2)]
                    one = [se.sb(f"one{j}", [P, P]) for j in range(2)]
                    prod = [se.sb(f"prod{j}", [P, 8, MUL]) for j in range(2)]
                    pA = se.ps("pA", [P, P])
                    pH = [se.ps(f"pH{j}", [NHID, P]) for j in range(2)]
                    pE = [se.ps(f"pE{j}", [P, D]) for j in range(2)]
                    pM = [se.ps(f"pM{j}", [P, 8, MUL]) for j in range(2)]
                    s_w, s_z, s_c, s_ib, s_cons = (se.sem(n) for n in ("s_w", "s_z", "s_c", "s_ib", "s_cons"))
                    s_g = [se.sem(f"s_g{j}") for j in range(U)]
                    s_a, s_at, s_ac, s_h, s_hs, s_e = (se.sem(n) for n in ("s_a", "s_at", "s_ac", "s_h", "s_hs", "s_e"))
                    s_one, s_oh, s_m, s_acc, s_gt = (se.sem(n) for n in ("s_one", "s_oh", "s_m", "s_acc", "s_gt"))
                    with nc.Block() as block:
                        @block.sync
                        def _(sp):
                            sp.wait_ge(s_z, 1)
                            for j in range(4):
                                sp.dma_start(w1p[j * NBAS:(j + 1) * NBAS, j, :], a["L0_gnn_W_mlp1"]).then_inc(s_w, 16)
                            for q, c in enumerate((0, 2, 3, 1)):
                                sp.dma_start(w2s[:, q * MUL:(q + 1) * MUL], a["L0_gnn_W_mlp2"][:, c * MUL:(c + 1) * MUL]).then_inc(s_w, 16)

                        @block.gpsimd
                        def _(pool):
                            pool.memset(gate[:, :], 1.0).then_inc(s_gt, 1)
                            pool.wait_ge(s_gt, 1)
                            rolled(pool, lambda i, first: gather_rows(pool, G, ib, gate, table[0], s_ib, s_g, s_gt, i))

                        @block.scalar
                        def _(act):
                            act.wait_ge(s_z, 4)

                            def body(i, first):
                                gather_indices(act, ib, s_ib, s_cons, s_gt, i, first)
                                for h in range(2):
                                    if not first:
                                        act.wait_ge(s_at, 2 * i - 1 + h)
                                    nc.scalar.activation(a10[h][:, 0:4 * NBAS].rearrange("p (k c) -> p k c", k=4),
                                                         a10S[:, :, ds(U * i + 4 * h, 4)].rearrange("p c k -> p k c"),
                                                         ACT.Copy).then_inc(s_a, 1)
                                for j in range(U):
                                    k, h = U * i + j, j // 4
                                    if j % 4 == 0:
                                        act.wait_ge(s_at, 2 * i + h + 1)
                                        if not first:
                                            act.wait_ge(s_h, U * (i - 1) + 4 * h + 4)
                                        nc.scalar.activation(a10T[h][:, :], pA[0:4 * NBAS, :], ACT.Copy).then_inc(s_ac, 1)
                                    act.wait_ge(s_h, k + 1)
                                    if not first or j >= 2:
                                        act.wait_ge(s_e, k - 1)
                                    nc.scalar.activation(hid[j % 2][:, :], pH[j % 2][:, :], ACT.Silu,
                                                         scale=1 / math.sqrt(NBAS)).then_inc(s_hs, 1)
                                    act.wait_ge(s_one, k + 1)
                                    if not first or j >= 2:
                                        act.wait_ge(s_m, k - 1)
                                    for m in range(1, 4):
                                        ins = nc.scalar.activation(oh[j % 2][:, m, :], one[j % 2][:, :], ACT.Copy,
                                                                   scale=a4S[:, m, ds(k, 1)])
                                    ins.then_inc(s_oh, 1)
                            rolled(act, body)

                        @block.vector
                        def _(dve):
                            nc.vector.memset(w1p[:, :, :], 0.0).then_inc(s_z, 1)
                            for h in range(2):
                                nc.vector.memset(a10[h][:, :], 0.0).then_inc(s_z, 1)
                            nc.vector.memset(acc[:, :, :], 0.0).then_inc(s_z, 1)
                            dve.wait_ge(s_w, 16 * 8)
                            dve.wait_ge(s_z, 4)
                            link = chain(dve, s_c)
                            link(nc.vector.tensor_scalar(w2s[:, 0:3 * MUL], w2s[:, 0:3 * MUL], 1 / math.sqrt(NHID), None, ALU.mult))
                            link(nc.vector.tensor_scalar(w2s[:, 3 * MUL:D], w2s[:, 3 * MUL:D], 1 / math.sqrt(3 * NHID), None, ALU.mult))

                            def add(k, j):
                                node = dve.value_load(nodeR[0:1, ds(k, 1)], min_val=0, max_val=NT - 1)
                                dve.wait_ge(s_m, k + 1)
                                if type(k) is not int or k:
                                    dve.wait_ge(s_acc, k)
                                at = tile(acc, node)
                                nc.vector.tensor_tensor(at, at, pM[j % 2][:, :, :].rearrange("p b c -> p (b c)"), ALU.add).then_inc(s_acc, 1)

                            def body(i, first):
                                for j in range(U):
                                    k = U * i + j
                                    if not first or j >= 2:
                                        dve.wait_ge(s_oh, k - 1)
                                        dve.wait_ge(s_m, k - 1)
                                    nc.vector.tensor_scalar(one[j % 2][:, :], iota[:, :], relS[:, ds(k, 1)], None, ALU.is_equal).then_inc(s_one, 1)
                                    nc.vector.tensor_scalar(oh[j % 2][:, 0, :], iota[:, :], relS[:, ds(k, 1)], a4S[:, 0, ds(k, 1)],
                                                            ALU.is_equal, ALU.mult)
                                    dve.wait_ge(s_e, k + 1)
                                    dve.wait_ge(s_g[j], 16 * i + 16)
                                    w = pE[j % 2][:, :].rearrange("p (b c) -> p b c", c=MUL)
                                    g = G[j][:, :].rearrange("p (b c) -> p b c", c=MUL)
                                    nc.vector.tensor_tensor(prod[j % 2][:, 0:8:7, :], w[:, 0:2, :], g[:, 0:1, :].broadcast_to([P, 2, MUL]), ALU.mult)
                                    nc.vector.tensor_tensor(prod[j % 2][:, 1:7, :].rearrange("p (q m) c -> p q m c", q=2),
                                                            w[:, 2:4, :].unsqueeze(2).broadcast_to([P, 2, 3, MUL]),
                                                            g[:, 1:4, :].unsqueeze(1).broadcast_to([P, 2, 3, MUL]), ALU.mult).then_inc(s_cons, 1)
                                    if not first or j:
                                        add(k - 1, (j - 1) % 2)
                            rolled(dve, body)
                            add(K - 1, (K - 1) % 2)

                        @block.tensor
                        def _(pe):
                            pe.wait_ge(s_w, 16 * 8)
                            pe.wait_ge(s_c, 2)

                            def hidden(i, first, j):
                                k, h = U * i + j, j // 4
                                if j % 4 == 0:
                                    pe.wait_ge(s_a, 2 * i + h + 1)
                                    if not first or h:
                                        pe.wait_ge(s_ac, 2 * i + h)
                                    nc.tensor.transpose(pA[:, :], a10[h][:, :], ident[:, :]).then_inc(s_at, 1)
                                    pe.wait_ge(s_ac, 2 * i + h + 1)
                                if not first or j >= 2:
                                    pe.wait_ge(s_hs, k - 1)
                                nc.tensor.matmul(pH[j % 2][:, :], w1p[:, j % 4, :], a10T[h][:, :], start=True, stop=True).then_inc(s_h, 1)

                            def scatter(k, j, early):
                                pe.wait_ge(s_oh, k + 1)
                                pe.wait_ge(s_cons, k + 1)
                                if not early:
                                    pe.wait_ge(s_acc, k - 1)
                                o, p, m = oh[j % 2], prod[j % 2], pM[j % 2]
                                nc.tensor.matmul(m[:, 0:4, :], o[:, 0, :], p[:, 0:4, :], start=True, stop=False)
                                nc.tensor.matmul(m[:, 4:6, :], o[:, 1, :], p[:, 4:8:3, :], start=False, stop=False)
                                for q in range(2):
                                    nc.tensor.matmul(m[:, 4, :], o[:, 2 + q, :], p[:, 5 + q, :], start=False, stop=False)
                                    ins = nc.tensor.matmul(m[:, 6 + q, :], o[:, 2 + q, :], p[:, 7, :], start=False, stop=(q == 1))
                                ins.then_inc(s_m, 1)

                            def body(i, first):
                                for j in range(U):
                                    k = U * i + j
                                    hidden(i, first, j)
                                    if not first or j:
                                        scatter(k - 1, (j - 1) % 2, first and j < 3)
                                    pe.wait_ge(s_hs, k + 1)
                                    if not first or j >= 2:
                                        pe.wait_ge(s_cons, k - 1)
                                    nc.tensor.matmul(pE[j % 2][:, :], hid[j % 2][:, :], w2s[:, :], start=True, stop=True).then_inc(s_e, 1)
                            rolled(pe, body)
                            scatter(K - 1, (K - 1) % 2, False)

                with Stage() as se:
                    wo = se.sb("wo", [P, 2, MUL])
                    ms = [se.sb(f"ms{j}", [P, 8, MUL]) for j in range(2)]
                    mT = [se.sb(f"mT{j}", [P, 2 * D]) for j in range(2)]
                    bs = [se.sb(f"bs{j}", [P, D]) for j in range(2)]
                    xo = [se.sb(f"xo{j}", [P, D]) for j in range(2)]
                    pT = [se.ps(f"pT{j}", [P, 2 * D]) for j in range(2)]
                    pO = [se.ps(f"pO{j}", [P, D]) for j in range(2)]
                    s_w, s_ms, s_t, s_mt, s_o, s_x = (se.sem(n) for n in ("s_w", "s_ms", "s_t", "s_mt", "s_o", "s_x"))
                    s_b = [se.sem(f"s_b{j}") for j in range(2)]
                    s_st = [se.sem(f"s_st{j}") for j in range(2)]

                    with nc.Block() as block:
                        @block.sync
                        def _(sp):
                            sp.dma_start(wo[:, 0, :], a["L0_gnn_W_lo0"]).then_inc(s_w, 16)
                            sp.dma_start(wo[0:MUL, 1, :], a["L0_gnn_W_lo1"][MUL:2 * MUL, :]).then_inc(s_w, 16)
                            sp.dma_start(wo[MUL:P, 1, :], a["L0_gnn_W_lo1"][0:MUL, :]).then_inc(s_w, 16)

                            def body(i, first):
                                for j in range(2):
                                    if not first:
                                        sp.wait_ge(s_x, 2 * i + j - 1)
                                    sp.dma_start(bs[j][:, :], base0[ds((2 * i + j) * P, P), :]).then_inc(s_b[j], 16)
                            tile_pairs(sp, body)

                        @block.scalar
                        def _(act):
                            def body(i, first):
                                for j in range(2):
                                    n = 2 * i + j
                                    if not first:
                                        act.wait_ge(s_t, n - 1)
                                    nc.scalar.activation(ms[j][:, :, :].rearrange("p (c h) k -> p h c k", h=2),
                                                         tile(acc, n).rearrange("p (h c k) -> p h c k", h=2, k=MUL), ACT.Copy,
                                                         scale=sc_o[:, ds(n, 1)]).then_inc(s_ms, 1)
                                for j in range(2):
                                    n = 2 * i + j
                                    act.wait_ge(s_x, n + 1)
                                    act.dma_start(x1[ds(n * P, P), :], xo[j][:, :]).then_inc(s_st[j], 16)
                            tile_pairs(act, body)
                            for j in range(2):
                                act.wait_ge(s_st[j], 16 * (NT // 2))

                        @block.vector
                        def _(dve):
                            def body(i, first):
                                for j in range(2):
                                    n = 2 * i + j
                                    dve.wait_ge(s_t, n + 1)
                                    if not first:
                                        dve.wait_ge(s_o, n - 1)
                                    nc.vector.tensor_copy(mT[j][:, :], pT[j][:, :]).then_inc(s_mt, 1)
                                for j in range(2):
                                    n = 2 * i + j
                                    dve.wait_ge(s_o, n + 1)
                                    dve.wait_ge(s_b[j], 16 * i + 16)
                                    if not first:
                                        dve.wait_ge(s_st[j], 16 * i)
                                    nc.vector.tensor_tensor(xo[j][:, 0:MUL], pO[j][:, 0:MUL], bs[j][:, 0:MUL], ALU.add)
                                    nc.vector.tensor_tensor(xo[j][:, MUL:D].rearrange("p (k m) -> p m k", m=3),
                                                            pO[j][:, MUL:D].rearrange("p (m k) -> p m k", m=3),
                                                            bs[j][:, MUL:D].rearrange("p (k m) -> p m k", m=3), ALU.add).then_inc(s_x, 1)
                            tile_pairs(dve, body)

                        @block.tensor
                        def _(pe):
                            pe.wait_ge(s_w, 48)

                            def body(i, first):
                                for j in range(2):
                                    n = 2 * i + j
                                    pe.wait_ge(s_ms, n + 1)
                                    if not first:
                                        pe.wait_ge(s_mt, n - 1)
                                    for c in range(4):
                                        ins = nc.tensor.transpose(pT[j][:, c * P:(c + 1) * P],
                                                                  ms[j][:, 2 * c:2 * c + 2, :].rearrange("p b k -> p (b k)"), ident[:, :])
                                    ins.then_inc(s_t, 1)
                                for j in range(2):
                                    n = 2 * i + j
                                    pe.wait_ge(s_mt, n + 1)
                                    if not first:
                                        pe.wait_ge(s_x, n - 1)
                                    for c in range(4):
                                        ins = nc.tensor.matmul(pO[j][:, c * MUL:(c + 1) * MUL], mT[j][:, c * P:(c + 1) * P],
                                                               wo[:, min(c, 1), :], start=True, stop=True)
                                    ins.then_inc(s_o, 1)
                            tile_pairs(pe, body)
        x_sb = top.sb("x_sb", [P, NT, D])
        rstd, shift = top.sb("rstd", [P, NT]), top.sb("shift", [P, NT])
        load_nodes(x_sb, x1, N)
        layernorm_stats(x_sb, rstd, shift)
        with Stage() as st1:
            F1 = D // H1
            gS, dS = st1.sb("gS", [P, KP, H1]), st1.sb("dS", [P, KP, H1])
            score = st1.sb("score", [P, NT, 2 * H1])
            with Stage() as st:
                wz = st.sb("wz", [P, 2, D])
                wa = st.sb("wa", [P, 2, 2 * H1])
                att = st.sb("att", [P, H1, 2 * F1])
                wp = st.sb("wp", [P, 2, D])
                s_w, s_c = st.sem("s_w"), st.sem("s_c")
                with nc.Block() as block:
                    @block.sync
                    def _(sp):
                        for h in range(H1):
                            sp.dma_start(wz[:, :, h * F1:(h + 1) * F1], a["L1_gnn_W"][h].rearrange("(c p) f -> p c f", p=P)).then_inc(s_w, 16)
                        sp.dma_start(att[:, :, :].rearrange("p h f -> p (h f)"),
                                     a["L1_gnn_att"].rearrange("(a h) f -> a (h f)", a=1).broadcast_to([P, H1 * 2 * F1])).then_inc(s_w, 16)

                    @block.vector
                    def _(dve):
                        dve.wait_ge(s_w, 16 * (H1 + 1))
                        link = chain(dve, s_c)
                        for half in range(2):
                            for c in range(2):
                                link(nc.vector.tensor_tensor(wp[:, c, :].rearrange("p (h f) -> p h f", h=H1),
                                                             wz[:, c, :].rearrange("p (h f) -> p h f", h=H1),
                                                             att[:, :, half * F1:(half + 1) * F1], ALU.mult))
                                link(nc.vector.tensor_reduce(wa[:, c, half * H1:(half + 1) * H1],
                                                             wp[:, c, :].rearrange("p (h f) -> p h f", h=H1), AX.X, ALU.add))

                def act_end(act, n, j, pO, row, aux):
                    return nc.scalar.activation(row[:, :], pO[0][:, :], ACT.Copy)

                def dve_end(dve, n, j, pO, row, aux, s_ae):
                    return nc.vector.tensor_copy(tile(score, n), pO[1][:, :])

                node_stage(1, x_sb, rstd, shift, [D, 2 * H1], lambda w, b: [], [False, False], act_end, dve_end,
                           [(lambda n: table[1][ds(n * P, P), :], lambda row, aux: row[:, :])], ready={0: wz, 1: wa})
            with Stage() as st:
                sc_d = st.sb("sc_d", [P, NT, H1])
                s_s, s_c = st.sem("s_s"), st.sem("s_c")
                with nc.Block() as block:
                    @block.sync
                    def _(sp):
                        sp.dma_start(small1.rearrange("(t p) h -> p t h", p=P), score[:, :, 0:H1]).then_inc(s_s, 16)
                        sp.wait_ge(s_s, 16)

                    @block.vector
                    def _(dve):
                        nc.vector.tensor_copy(sc_d[:, :, :], score[:, :, H1:2 * H1]).then_inc(s_c, 1)
                edge_scores(small1, sc_d, H1, gS, dS)
            edge_softmax(H1, gS, dS, 0.01, -1000.0, False)
            with Stage() as st:
                acc = st.sb("acc1", [P, NT, D + H1])
                den = st.sb("den", [P, NT, H1])
                s_z, s_c = st.sem("s_z"), st.sem("s_c")
                with nc.Block() as block:
                    @block.vector
                    def _(dve):
                        nc.vector.memset(acc[:, :, :], 0.0).then_inc(s_z, 1)
                edge_sum(table[1], acc, D + H1, H1, gS, None)
                with nc.Block() as block:
                    @block.vector
                    def _(dve):
                        link = chain(dve, s_c)
                        link(nc.vector.tensor_scalar(den[:, :, :], acc[:, :, D:D + H1], 1e-30, None, ALU.max))
                        link(nc.vector.reciprocal(den[:, :, :], den[:, :, :]))
                        heads = acc[:, :, 0:D].rearrange("p t (h f) -> p t h f", h=H1)
                        link(nc.vector.tensor_tensor(heads, heads, den[:, :, :].unsqueeze(3).broadcast_to([P, NT, H1, F1]), ALU.mult))
                        link(nc.vector.tensor_tensor(x_sb[:, :, :], x_sb[:, :, :], acc[:, :, 0:D], ALU.add))

        layernorm_stats(x_sb, rstd, shift)

        def act_end(act, n, j, pO, row, aux):
            return nc.scalar.activation(row[:, :], pO[0][:, :], ACT.Copy)

        def dve_end(dve, n, j, pO, row, aux, s_ae):
            return nc.vector.tensor_tensor(tile(x_sb, n), tile(x_sb, n), pO[1][:, :], ALU.add)

        node_stage(2, x_sb, rstd, shift, [D, D],
                   lambda w, b: [(w[0][:, :, :], a["L2_gnn_w_nbr"].rearrange("(c p) n -> p c n", p=P)),
                                 (w[1][:, :, :], a["L2_gnn_w_own"].rearrange("(c p) n -> p c n", p=P)),
                                 (b[1][0:1, :], a["L2_gnn_bias"].rearrange("(a n) -> a n", a=1))],
                   [False, True], act_end, dve_end, [(lambda n: table[2][ds(n * P, P), :], lambda row, aux: row[:, :])])
        edge_sum(table[2], x_sb, D, 0, None, None)

        layernorm_stats(x_sb, rstd, shift)
        with Stage() as st3:
            F3 = D // H3
            gS, dS = st3.sb("gS", [P, KP, H3]), st3.sb("dS", [P, KP, H3])
            with Stage() as st:
                score = st.sb("score", [P, NT, H3])
                s_l = st.sem("s_l")

                def act_end(act, n, j, pO, row, aux):
                    nc.scalar.activation(aux[:, :], pO[0][:, 0:D], ACT.Copy)
                    return nc.scalar.activation(row[:, :], pO[1][:, :], ACT.Copy)

                def dve_end(dve, n, j, pO, row, aux, s_ae):
                    dve.wait_ge(s_ae, n + 1)
                    nc.vector.tensor_tensor(aux[:, :], aux[:, :], pO[0][:, D:2 * D], ALU.mult).then_inc(s_l, 1)
                    dve.wait_ge(s_l, n + 1)
                    return nc.vector.tensor_reduce(tile(score, n), aux[:, :].rearrange("p (h c) -> p h c", h=H3), AX.X, ALU.add)

                def qkv(w, b):
                    for q, (name, o) in enumerate((("q", 0), ("k", D), ("v", 0))):
                        yield w[q // 2][:, :, o:o + D], a[f"L3_gnn_W{name}"].rearrange("(c p) n -> p c n", p=P)
                        yield b[q // 2][0:1, o:o + D], a[f"L3_gnn_b{name}"].rearrange("(a n) -> a n", a=1)

                node_stage(3, x_sb, rstd, shift, [2 * D, D], qkv, [True, True], act_end, dve_end,
                           [(lambda n: table[3][ds(n * P, P), :], lambda row, aux: row[:, :])])
                with Stage() as se:
                    s_c, s_s = se.sem("s_c"), se.sem("s_s")
                    with nc.Block() as block:
                        @block.vector
                        def _(dve):
                            nc.vector.tensor_scalar(score[:, :, :], score[:, :, :], 1 / math.sqrt(F3), None, ALU.mult).then_inc(s_c, 1)

                        @block.sync
                        def _(sp):
                            sp.wait_ge(s_c, 1)
                            sp.dma_start(small3.rearrange("(t p) h -> p t h", p=P), score[:, :, :]).then_inc(s_s, 16)
                            sp.wait_ge(s_s, 16)
                edge_scores(small3, score, H3, gS, dS)
            edge_softmax(H3, gS, dS, 0.2, None, True)
            acc = st3.sb("acc3", [P, NT, D + 2 * H3])
            with Stage() as st:
                s_z = st.sem("s_z")
                with nc.Block() as block:
                    @block.vector
                    def _(dve):
                        nc.vector.memset(acc[:, :, :], 0.0).then_inc(s_z, 1)
            edge_sum(table[3], acc, D + 2 * H3, H3, gS, dS)

            with Stage() as st:
                own, den = st.sb("own", [P, NT, H3]), st.sb("den", [P, NT, H3])
                alone = st.sb("alone", [P, NT])
                wo = st.sb("wo", [P, 2, D])
                bo = st.sb("bo", [1, D])
                v = [st.sb(f"v{j}", [P, D]) for j in range(2)]
                y = [st.sb(f"y{j}", [P, D]) for j in range(2)]
                vT = [st.sb(f"vT{j}", [P, D]) for j in range(2)]
                pT = [st.ps(f"pT{j}", [P, D]) for j in range(2)]
                pO = [st.ps(f"pO{j}", [P, D]) for j in range(2)]
                s_w, s_c, s_at, s_t, s_tc, s_o, s_r, s_y, s_l = (st.sem(n) for n in ("s_w", "s_c", "s_at", "s_t", "s_tc", "s_o", "s_r", "s_y", "s_l"))
                s_v = [st.sem(f"s_v{j}") for j in range(2)]
                with nc.Block() as block:
                    @block.sync
                    def _(sp):
                        sp.dma_start(wo[:, :, :], a["L3_gnn_Wo"].rearrange("(c p) n -> p c n", p=P)).then_inc(s_w, 16)
                        sp.dma_start(bo[0:1, :], a["L3_gnn_bo"].rearrange("(a n) -> a n", a=1)).then_inc(s_w, 16)

                        def body(i, first):
                            for j in range(2):
                                n = 2 * i + j
                                if not first:
                                    sp.wait_ge(s_t, n - 1)
                                sp.dma_start(v[j][:, :], table[3][ds(n * P, P), :]).then_inc(s_v[j], 16)
                        tile_pairs(sp, body)

                    @block.vector
                    def _(dve):
                        link = chain(dve, s_c)
                        link(nc.vector.tensor_scalar(alone[:, :], cnt[:, :], 0.0, None, ALU.is_equal))
                        link(nc.vector.tensor_tensor(own[:, :, :], acc[:, :, D + H3:D + 2 * H3],
                                                     alone[:, :].unsqueeze(2).broadcast_to([P, NT, H3]), ALU.add))
                        link(nc.vector.tensor_tensor(den[:, :, :], own[:, :, :], acc[:, :, D:D + H3], ALU.add))
                        link(nc.vector.reciprocal(den[:, :, :], den[:, :, :]))
                        heads = lambda t: t.rearrange("p (h c) -> p h c", h=H3)
                        wide = lambda t, n: t[:, ds(n, 1), :].rearrange("p a h -> p h a").broadcast_to([P, H3, F3])

                        def body(i, first):
                            for j in range(2):
                                n = 2 * i + j
                                dve.wait_ge(s_v[j], 16 * i + 16)
                                at = tile(acc[:, :, 0:D], n)
                                nc.vector.tensor_tensor(heads(v[j][:, :]), heads(v[j][:, :]), wide(own, n), ALU.mult).then_inc(s_l, 1)
                                dve.wait_ge(s_l, 2 * n + 1)
                                nc.vector.tensor_tensor(v[j][:, :], v[j][:, :], at, ALU.add).then_inc(s_l, 1)
                                dve.wait_ge(s_l, 2 * n + 2)
                                nc.vector.tensor_tensor(heads(v[j][:, :]), heads(v[j][:, :]), wide(den, n), ALU.mult).then_inc(s_at, 1)
                            for j in range(2):
                                n = 2 * i + j
                                dve.wait_ge(s_o, n + 1)
                                dve.wait_ge(s_y, n + 1)
                                nc.vector.tensor_tensor(tile(acc[:, :, 0:D], n), pO[j][:, :], y[j][:, :], ALU.add).then_inc(s_r, 1)
                        tile_pairs(dve, body)

                    @block.scalar
                    def _(act):
                        def body(i, first):
                            for j in range(2):
                                n = 2 * i + j
                                if not first:
                                    act.wait_ge(s_r, n - 1)
                                nc.scalar.activation(y[j][:, :], tile(x_sb, n), ACT.Relu, bias=shift[:, ds(n, 1)],
                                                     scale=rstd[:, ds(n, 1)]).then_inc(s_y, 1)
                            for j in range(2):
                                n = 2 * i + j
                                act.wait_ge(s_t, n + 1)
                                if not first:
                                    act.wait_ge(s_o, n - 1)
                                nc.scalar.activation(vT[j][:, :], pT[j][:, :], ACT.Copy).then_inc(s_tc, 1)
                        tile_pairs(act, body)

                    @block.tensor
                    def _(pe):
                        pe.wait_ge(s_w, 32)

                        def body(i, first):
                            for j in range(2):
                                n = 2 * i + j
                                pe.wait_ge(s_at, n + 1)
                                if not first:
                                    pe.wait_ge(s_tc, n - 1)
                                for c in range(2):
                                    ins = nc.tensor.transpose(pT[j][:, c * P:(c + 1) * P], v[j][:, c * P:(c + 1) * P], ident[:, :])
                                ins.then_inc(s_t, 1)
                            for j in range(2):
                                n = 2 * i + j
                                pe.wait_ge(s_tc, n + 1)
                                if not first:
                                    pe.wait_ge(s_r, n - 1)
                                nc.tensor.matmul(pO[j][:, :], ones[0:1, :], bo[0:1, :], start=True, stop=False)
                                for c in range(2):
                                    ins = nc.tensor.matmul(pO[j][:, :], vT[j][:, c * P:(c + 1) * P], wo[:, c, :], start=False, stop=(c == 1))
                                ins.then_inc(s_o, 1)
                        tile_pairs(pe, body)

            rsg, brow = st3.sb("rsg", [P, D]), st3.sb("brow", [P, D])
            batch_norm(acc, a["L3_gnn_bn1_g"], a["L3_gnn_bn1_b"], rsg, brow)

            with Stage() as st:
                FB = 2 * D // P
                w1 = st.sb("w1", [P, 2, 2 * D])
                w2 = st.sb("w2", [P, FB, D])
                b1 = st.sb("b1", [P, FB])
                b2 = st.sb("b2", [1, D])
                h1 = [st.sb(f"h1_{j}", [P, D]) for j in range(2)]
                hT = [st.sb(f"hT{j}", [P, D]) for j in range(2)]
                fT = [st.sb(f"fT{j}", [P, FB, P]) for j in range(2)]
                pT = [st.ps(f"pT{j}", [P, D]) for j in range(2)]
                pF = [st.ps(f"pF{j}", [P, FB, P]) for j in range(2)]
                pO = [st.ps(f"pO{j}", [P, D]) for j in range(2)]
                s_w, s_l, s_h, s_t, s_tc, s_f, s_fc, s_o, s_r = (st.sem(n) for n in ("s_w", "s_l", "s_h", "s_t", "s_tc", "s_f", "s_fc", "s_o", "s_r"))
                with nc.Block() as block:
                    @block.sync
                    def _(sp):
                        sp.dma_start(w1[:, :, :], a["L3_gnn_W1"].rearrange("(c p) n -> p c n", p=P)).then_inc(s_w, 16)
                        sp.dma_start(w2[:, :, :], a["L3_gnn_W2"].rearrange("(c p) n -> p c n", p=P)).then_inc(s_w, 16)
                        with nc.allow_non_contiguous_dma(reason="512 biases, feature on partition"):
                            sp.dma_start(b1[:, :], a["L3_gnn_b1"].rearrange("(c p) -> p c", p=P)).then_inc(s_w, 16)
                        sp.dma_start(b2[0:1, :], a["L3_gnn_b2"].rearrange("(a n) -> a n", a=1)).then_inc(s_w, 16)

                    @block.vector
                    def _(dve):
                        def body(i, first):
                            for j in range(2):
                                n = 2 * i + j
                                if not first:
                                    dve.wait_ge(s_t, n - 1)
                                    dve.wait_ge(s_r, n - 1)
                                nc.vector.tensor_tensor(h1[j][:, :], tile(acc[:, :, 0:D], n), rsg[:, :], ALU.mult).then_inc(s_l, 1)
                                dve.wait_ge(s_l, n + 1)
                                nc.vector.tensor_tensor(h1[j][:, :], h1[j][:, :], brow[:, :], ALU.add).then_inc(s_h, 1)
                            for j in range(2):
                                n = 2 * i + j
                                dve.wait_ge(s_o, n + 1)
                                nc.vector.tensor_tensor(tile(acc[:, :, 0:D], n), pO[j][:, :], h1[j][:, :], ALU.add).then_inc(s_r, 1)
                        tile_pairs(dve, body)

                    @block.scalar
                    def _(act):
                        act.wait_ge(s_w, 64)

                        def body(i, first):
                            for j in range(2):
                                n = 2 * i + j
                                act.wait_ge(s_t, n + 1)
                                if not first:
                                    act.wait_ge(s_f, n - 1)
                                nc.scalar.activation(hT[j][:, :], pT[j][:, :], ACT.Copy).then_inc(s_tc, 1)
                            for j in range(2):
                                n = 2 * i + j
                                act.wait_ge(s_f, n + 1)
                                if not first:
                                    act.wait_ge(s_o, n - 1)
                                for q in range(FB):
                                    ins = nc.scalar.activation(fT[j][:, q, :], pF[j][:, q, :], ACT.Relu, bias=b1[:, q:q + 1])
                                ins.then_inc(s_fc, 1)
                        tile_pairs(act, body)

                    @block.tensor
                    def _(pe):
                        pe.wait_ge(s_w, 64)

                        def body(i, first):
                            for j in range(2):
                                n = 2 * i + j
                                pe.wait_ge(s_h, n + 1)
                                if not first:
                                    pe.wait_ge(s_tc, n - 1)
                                for c in range(2):
                                    ins = nc.tensor.transpose(pT[j][:, c * P:(c + 1) * P], h1[j][:, c * P:(c + 1) * P], ident[:, :])
                                ins.then_inc(s_t, 1)
                            for j in range(2):
                                n = 2 * i + j
                                pe.wait_ge(s_tc, n + 1)
                                if not first:
                                    pe.wait_ge(s_fc, n - 1)
                                for q in range(FB):
                                    for c in range(2):
                                        ins = nc.tensor.matmul(pF[j][:, q, :], w1[:, c, q * P:(q + 1) * P], hT[j][:, c * P:(c + 1) * P],
                                                               start=(c == 0), stop=(c == 1))
                                ins.then_inc(s_f, 1)
                            for j in range(2):
                                n = 2 * i + j
                                pe.wait_ge(s_fc, n + 1)
                                if not first:
                                    pe.wait_ge(s_r, n - 1)
                                nc.tensor.matmul(pO[j][:, :], ones[0:1, :], b2[0:1, :], start=True, stop=False)
                                for q in range(FB):
                                    ins = nc.tensor.matmul(pO[j][:, :], fT[j][:, q, :], w2[:, q, :], start=False, stop=(q == FB - 1))
                                ins.then_inc(s_o, 1)
                        tile_pairs(pe, body)

            batch_norm(acc, a["L3_gnn_bn2_g"], a["L3_gnn_bn2_b"], rsg, brow)

            with Stage() as st:
                CH = NT // 5
                s_c, s_out = st.sem("s_c"), st.sem("s_out")
                with nc.Block() as block:
                    @block.vector
                    def _(dve):
                        for q in range(5):
                            link = chain(dve, s_c, 3 * q)
                            at = acc[:, q * CH:(q + 1) * CH, 0:D]
                            xt = x_sb[:, q * CH:(q + 1) * CH, :]
                            link(nc.vector.tensor_tensor(at, at, rsg[:, :].unsqueeze(1).broadcast_to([P, CH, D]), ALU.mult))
                            link(nc.vector.tensor_tensor(xt, xt, brow[:, :].unsqueeze(1).broadcast_to([P, CH, D]), ALU.add))
                            link(nc.vector.tensor_tensor(xt, xt, at, ALU.add))

                    @block.sync
                    def _(sp):
                        for q in range(5):
                            sp.wait_ge(s_c, 3 * q + 3)
                            last = min(FULL, (q + 1) * CH)
                            sp.dma_start(out[q * CH * P:last * P, :].rearrange("(t p) c -> p t c", p=P), x_sb[:, q * CH:last, :]).then_inc(s_out, 16)
                        sp.dma_start(out[FULL * P:N, :], x_sb[0:REST, FULL, :]).then_inc(s_out, 16)
                        sp.wait_ge(s_out, 96)

def kernel(**inputs):
    import concourse.bacc as _bacc
    from concourse import mybir as _mybir
    from concourse.bass_utils import run_bass_kernel_spmd as _run

    nc = _bacc.Bacc("TRN2", target_bir_lowering=False, num_devices=1)
    arrays, args = {}, {}
    for name, value in inputs.items():
        value = np.ascontiguousarray(value)
        arrays[f"in_{name}"] = value
        args[name] = nc.dram_tensor(f"in_{name}", value.shape, _mybir.dt.from_np(value.dtype), kind="ExternalInput").ap()
    out = nc.dram_tensor("out_x", (N, D), _mybir.dt.from_np(np.dtype("float32")), kind="ExternalOutput").ap()
    build(nc, args, out)
    r = _run(nc, [arrays], core_ids=[0])
    return r.results[0]["out_x"]
```

```python
import math

import numpy as np

N = 6250
D = 256
E = 106250
P = 128
NT = 2 * math.ceil(N / P / 2)
NP = NT * P
FULL, REST = N // P, N % P
ET = math.ceil(E / P)
EPAD = ET * P
U = 8
LAG = 3
K = U * math.ceil((ET + math.ceil(N / P) - 1) / U)
KB = math.ceil(K / P)
KP = KB * P
NOWHERE = 16383
BIG = 1.0e38
EPS = 1e-5
MUL = 64
NBAS, NHID = 10, 100
H1, H3 = 4, 8


def build(nc, a, out):
    import concourse.bass as bass
    from concourse import mybir
    from contextlib import ExitStack

    F32, I32, BF16 = mybir.dt.float32, mybir.dt.int32, mybir.dt.bfloat16
    ALU = mybir.AluOpType
    ACT = mybir.ActivationFunctionType
    AX = mybir.AxisListType
    ds = bass.ds

    def dram(name, shape, dt=F32):
        return nc.dram_tensor(name, shape, dt).ap()

    stages = []

    class Stage(ExitStack):

        def __init__(self):
            super().__init__()
            stages.append(self)
            self.tag = f"_{len(stages)}"
            self.sems = []

        def sb(self, name, shape, dt=F32):
            return self.enter_context(nc.sbuf_tensor(name + self.tag, list(shape), dt))

        def ps(self, name, shape):
            bank = self.enter_context(nc.psum_tensor(name + self.tag, [P, 512], F32))
            view = bank[0:shape[0], 0:math.prod(shape[1:])]
            return view if len(shape) == 2 else view.rearrange("p (b c) -> p b c", b=shape[1])

        def sem(self, name):
            handle = nc.alloc_semaphore(name + self.tag)
            self.sems.append(handle)
            return handle

        def __exit__(self, *exc):
            if self.sems and exc[0] is None:
                nc.clear_and_free_semaphores(self.sems)
                nc.all_engine_barrier(sem_only=True)
            return super().__exit__(*exc)

    def chain(eng, sem, base=0):
        count = [0]

        def link(ins):
            count[0] += 1
            ins.then_inc(sem, 1)
            eng.wait_ge(sem, base + count[0])
        return link

    dst_pad, src_pad, w_pad = dram("dst_pad", [EPAD], I32), dram("src_pad", [EPAD], I32), dram("w_pad", [EPAD])
    a4_pad, a10_pad = dram("a4_pad", [EPAD * 4]), dram("a10_pad", [EPAD * NBAS])
    node_i, node_f = dram("step_node_i", [KP], I32), dram("step_node_f", [KP])
    wbig = dram("wbig", [D, 2 * D])
    table = [dram(f"table{n}", [NP, D]) for n in range(4)]
    small1, small3 = dram("small1", [NP, H1]), dram("small3", [NP, H3])
    base0, x1 = dram("base0", [NP, D]), dram("x1", [NP, D])

    top = Stage()
    with top:
        ident = top.sb("ident", [P, P])
        iota = top.sb("iota", [P, P])
        ones = top.sb("ones", [P, P])
        relS = top.sb("relS", [P, KP])
        wS = top.sb("wS", [P, KP])
        srcI = top.sb("srcI", [P, KP], I32)
        dstK = top.sb("dstK", [P, KB, P])
        outK = top.sb("outK", [P, KB, P])
        nodeR = top.sb("nodeR", [1, KP + LAG], I32)
        cnt = top.sb("cnt", [P, NT])
        dis = top.sb("dis", [P, NT])

        def pipelined(eng, count, unroll, peel, *parts):
            def turn(i, skip):
                for j in range(unroll):
                    for lag, do in parts:
                        if not skip or unroll * i + j >= lag:
                            do(unroll * i + j - lag, (j - lag) % unroll)
            for i in range(peel):
                turn(i, True)
            with eng.Fori(peel, count // unroll) as i:
                turn(i, False)
            for j in range(max(lag for lag, _ in parts)):
                for lag, do in parts:
                    if j < lag:
                        do(count + j - lag, (j - lag) % unroll)

        def freed(eng, sem, value):
            if not (type(value) is int and value <= 0):
                eng.wait_ge(sem, value)

        def steps(eng, *parts):
            pipelined(eng, K, U, 1, *parts)

        def tiles(eng, *parts):
            pipelined(eng, NT, 2, 2, *parts)

        def gather_indices(act, ib, s_ib, s_cons, s_gt):
            def do(k, j):
                if j % 4 == 0:
                    freed(act, s_cons, k - 4)
                    if not (type(k) is int and k < U):
                        act.wait_ge(s_gt, (k - j) // 4 + j // 4)
                    nc.scalar.activation(ib[:, j:j + 4], srcI[:, ds(k, 4)], ACT.Copy).then_inc(s_ib, 1)
            return do

        def gather_rows(pool, G, ib, gate, rows, s_ib, s_g, s_gt):
            def do(k, j):
                if j % 4 == 0:
                    pool.wait_ge(s_ib, (k - j) // 4 + j // 4 + 1)
                    h = j // 4
                    pool.tensor_tensor(gate[0:1, h:h + 1], gate[0:1, 2:3], gate[0:1, 2:3], ALU.mult).then_inc(s_gt, 1)
                pool.indirect_dma_start(G[j][:, :], None, rows,
                                        bass.IndirectOffsetOnAxis(ap=ib[:, j:j + 1], axis=0)).then_inc(s_g[j], 16)
            return do

        def gathered(eng, s_g, k, j):
            eng.wait_ge(s_g[j], 2 * (k - j) + 16)

        def step_nodes(eng):
            at = {}

            def node(k, j):
                return at[(j + LAG) % U]

            def load(k, j):
                if j == 0:
                    _, values = nc.values_load_multi_w_load_instructions(nodeR[0:1, ds(k, U)], engines=[eng.engine], min_val=0, max_val=NT - 1)
                    at.update(enumerate(values))
            return load, node

        def adder(dve, acc, pM, R, s_m, s_acc, node):
            def do(k, j):
                dve.wait_ge(s_m, k + 1)
                freed(dve, s_acc, k)
                at = tile(acc, node(k, j))
                nc.vector.tensor_tensor(at, at, pM[j % R][:, :], ALU.add).then_inc(s_acc, 1)
            return do

        def edge_scores(small, node_sc, H, gS, dS):
            with Stage() as se:
                G = [se.sb(f"G{j}", [P, H]) for j in range(U)]
                ib, gate = se.sb("ib", [P, U], I32), se.sb("gate", [1, 3])
                R = 4
                one = [se.sb(f"one{j}", [P, P]) for j in range(R)]
                oneT = [se.sb(f"oneT{j}", [P, P]) for j in range(R)]
                pT = [se.ps(f"pT{j}", [P, P]) for j in range(R)]
                pD = [se.ps(f"pD{j}", [P, H]) for j in range(R)]
                s_ib, s_gt, s_cons, s_one, s_t, s_tc, s_d, s_dc, s_z = (
                    se.sem(n) for n in ("s_ib", "s_gt", "s_cons", "s_one", "s_t", "s_tc", "s_d", "s_dc", "s_z"))
                s_g = [se.sem(f"s_g{j}") for j in range(U)]
                with nc.Block() as block:
                    @block.gpsimd
                    def _(pool):
                        pool.memset(gate[:, :], 1.0).then_inc(s_gt, 1)
                        pool.wait_ge(s_gt, 1)
                        steps(pool, (0, gather_rows(pool, G, ib, gate, small, s_ib, s_g, s_gt)))

                    @block.vector
                    def _(dve):
                        nc.vector.memset(gS[:, K:KP, :], 0.0).then_inc(s_z, 1)
                        nc.vector.memset(dS[:, K:KP, :], 0.0).then_inc(s_z, 1)

                        def mark(k, j):
                            freed(dve, s_t, k - R + 1)
                            nc.vector.tensor_scalar(one[j % R][:, :], iota[:, :], relS[:, ds(k, 1)], None, ALU.is_equal).then_inc(s_one, 1)

                        def keep(k, j):
                            gathered(dve, s_g, k, j)
                            nc.vector.tensor_copy(tile(gS, k), G[j][:, :]).then_inc(s_cons, 1)
                        steps(dve, (0, mark), (0, keep))

                    @block.tensor
                    def _(pe):
                        load, node = step_nodes(pe)

                        def turn(k, j):
                            pe.wait_ge(s_one, k + 1)
                            freed(pe, s_tc, k - R + 1)
                            nc.tensor.transpose(pT[j % R][:, :], one[j % R][:, :], ident[:, :]).then_inc(s_t, 1)

                        def pick(k, j):
                            pe.wait_ge(s_tc, k + 1)
                            freed(pe, s_dc, k - R + 1)
                            nc.tensor.matmul(pD[j % R][:, :], oneT[j % R][:, :], tile(node_sc, node(k, j)), start=True, stop=True).then_inc(s_d, 1)
                        steps(pe, (0, load), (0, turn), (LAG, pick))

                    @block.scalar
                    def _(act):
                        def turned(k, j):
                            act.wait_ge(s_t, k + 1)
                            freed(act, s_d, k - R + 1)
                            nc.scalar.activation(oneT[j % R][:, :], pT[j % R][:, :], ACT.Copy).then_inc(s_tc, 1)

                        def picked(k, j):
                            act.wait_ge(s_d, k + 1)
                            nc.scalar.activation(tile(dS, k), pD[j % R][:, :], ACT.Copy).then_inc(s_dc, 1)
                        steps(act, (0, gather_indices(act, ib, s_ib, s_cons, s_gt)), (0, turned), (LAG + 1, picked))

        def edge_softmax(H, gS, dS, slope, zero_to, loops):
            with Stage() as st:
                W = KB * P
                brk = st.sb("brk", [P, W + 1])
                notfirst, notlast = st.sb("notfirst", [P, KB, P]), st.sb("notlast", [P, KB, P])
                starts = st.sb("starts", [P, KB, P]) if loops else None
                bk = st.sb("bk", [P, KB])
                rF, rL = st.sb("rF", [1, KP]), st.sb("rL", [1, KP])
                join = st.sb("join", [1, KP + 1])
                many, thrF, thrB = st.sb("many", [1, KP]), st.sb("thrF", [1, KP]), st.sb("thrB", [1, KP])
                g_h, d_h = st.sb("g_h", [P, KP]), st.sb("d_h", [P, KP])
                gK, dK = st.sb("gK", [P, W]), st.sb("dK", [P, W])
                e, f, m = st.sb("e", [P, W]), st.sb("f", [P, W]), st.sb("m", [P, W])
                u = st.sb("u", [P, W]) if loops else e
                rowA, rowB = st.sb("rowA", [1, KP]), st.sb("rowB", [1, KP])
                cin = st.sb("cin", [P, 2 * KB])
                col = st.sb("col", [P, 2, KB])
                pX = [st.ps(f"pX{q}", [P, 512]) for q in range(4)]
                pR = st.ps("pR", [P, P])
                pC = st.ps("pC", [P, 2 * KB])
                s_v, s_row, s_rc, s_col, s_f, s_hc, s_tr, s_kc = (st.sem(n) for n in ("s_v", "s_row", "s_rc", "s_col", "s_f", "s_hc", "s_tr", "s_kc"))
                s_th, s_rr, s_ci, s_cc, s_df, s_ex, s_bt, s_bc = (st.sem(n) for n in ("s_th", "s_rr", "s_ci", "s_cc", "s_df", "s_ex", "s_bt", "s_bc"))
                R1 = (KB - 4) * P
                dst2 = dstK[:, :, :].rearrange("k b i -> k (b i)")
                out2 = outK[:, :, :].rearrange("k b i -> k (b i)")

                def to_rows(src, sem):
                    for q in range(2):
                        for b in range(KB):
                            ins = nc.tensor.transpose(pX[2 * q + b // 4][0:1, (b % 4) * P:(b % 4 + 1) * P], src[:, q, b:b + 1], ident[:, :])
                    ins.then_inc(sem, 1)

                def from_row(row, at):
                    for b in range(KB):
                        ins = nc.tensor.transpose(pC[:, at + b:at + b + 1], row[0:1, b * P:(b + 1) * P], ident[0:1, 0:1])
                    return ins

                def row_out(q, row):
                    nc.vector.tensor_copy(row[0:1, 0:512], pX[2 * q][0:1, :])
                    return nc.vector.tensor_copy(row[0:1, 512:KP], pX[2 * q + 1][0:1, 0:R1])

                VN = 10 + (2 if zero_to is not None else 0) + (4 if loops else 0)
                with nc.Block() as block:
                    @block.vector
                    def _(dve):
                        flat = lambda t: t[:, :, :].rearrange("k b i -> k (b i)")
                        link = chain(dve, s_f)
                        link(nc.vector.tensor_tensor(brk[:, 1:W], dst2[:, 1:W], dst2[:, 0:W - 1], ALU.not_equal))
                        link(nc.vector.tensor_scalar(brk[:, 1:W], brk[:, 1:W], -BIG, None, ALU.mult))
                        link(nc.vector.memset(brk[:, 0:W + 1:P], -BIG))
                        for out_, at in ((notfirst, 0), (notlast, P - 1)):
                            link(nc.vector.tensor_tensor(out_[:, :, :], dstK[:, :, :], dstK[:, :, at:at + 1].broadcast_to([P, KB, P]), ALU.not_equal))
                            link(nc.vector.tensor_scalar(out_[:, :, :], out_[:, :, :], -BIG, None, ALU.mult))
                            nc.vector.tensor_copy(col[:, at // (P - 1), :], dstK[:, :, at]).then_inc(s_col, 1)
                        dve.wait_ge(s_row, 1)
                        row_out(0, rF)
                        link(row_out(1, rL))
                        link(nc.vector.tensor_tensor(join[0:1, 1:KP], rF[0:1, 1:KP], rL[0:1, 0:KP - 1], ALU.not_equal))
                        link(nc.vector.tensor_scalar(join[0:1, 1:KP], join[0:1, 1:KP], -BIG, None, ALU.mult))
                        link(nc.vector.memset(join[0:1, 0:KP + 1:KP], -BIG))
                        link(nc.vector.tensor_tensor(many[:, :], rF[:, :], rL[:, :], ALU.not_equal))
                        link(nc.vector.tensor_scalar(many[:, :], many[:, :], -BIG, None, ALU.mult))
                        link(nc.vector.tensor_tensor(thrF[:, :], many[:, :], join[:, 0:KP], ALU.add))
                        nc.vector.tensor_tensor(thrB[:, :], many[:, :], join[:, 1:KP + 1], ALU.add).then_inc(s_rc, 1)
                        dve.wait_ge(s_rc, 1)
                        if loops:
                            dve.wait_ge(s_col, 3)
                            link(nc.vector.tensor_scalar(flat(starts), brk[:, 0:W], 0.0, None, ALU.is_lt))
                            link(nc.vector.tensor_scalar(starts[:, :, 0], pC[:, 0:KB], 0.0, None, ALU.is_lt))

                        with dve.Fori(0, H) as h:
                            link = chain(dve, s_v, VN * h)
                            dve.wait_ge(s_kc, h + 1)
                            link(nc.vector.tensor_tensor(gK[:, :], gK[:, :], dK[:, :], ALU.add))
                            link(nc.vector.scalar_tensor_tensor(e[:, :], gK[:, :], slope, gK[:, :], ALU.mult, ALU.max))
                            if zero_to is not None:
                                link(nc.vector.tensor_scalar(gK[:, :], gK[:, :], 0.0, zero_to, ALU.is_equal, ALU.mult))
                                link(nc.vector.tensor_tensor(e[:, :], e[:, :], gK[:, :], ALU.add))
                            link(nc.vector.tensor_tensor(e[:, :], e[:, :], out2, ALU.add))
                            if loops:
                                link(nc.vector.tensor_scalar(dK[:, :], dK[:, :], 2.0, None, ALU.mult))
                                link(nc.vector.scalar_tensor_tensor(dK[:, :], dK[:, :], slope, dK[:, :], ALU.mult, ALU.max))
                                link(nc.vector.tensor_tensor(dK[:, :], dK[:, :], out2, ALU.add))
                                link(nc.vector.tensor_tensor(u[:, :], e[:, :], dK[:, :], ALU.max))
                            link(nc.vector.tensor_tensor_scan(f[:, :], brk[:, 0:W], u[:, :], -BIG, ALU.add, ALU.max))
                            link(nc.vector.tensor_tensor_scan(m[:, ::-1], brk[:, 1:W + 1][:, ::-1], f[:, ::-1], -BIG, ALU.add, ALU.max))
                            m3 = m[:, :].rearrange("k (b i) -> k b i", b=KB)
                            nc.vector.tensor_copy(col[:, 0, :], m3[:, :, P - 1])
                            nc.vector.tensor_copy(col[:, 1, :], m3[:, :, 0]).then_inc(s_th, 1)
                            dve.wait_ge(s_rr, h + 1)
                            row_out(0, rowA)
                            link(row_out(1, rowB))
                            nc.vector.tensor_tensor_scan(rF[:, :], thrF[:, :], rowA[:, :], -BIG, ALU.add, ALU.max)
                            link(nc.vector.tensor_tensor_scan(rL[:, ::-1], thrB[:, ::-1], rowB[:, ::-1], -BIG, ALU.add, ALU.max))
                            nc.vector.memset(rowA[0:1, 0:1], -BIG)
                            nc.vector.tensor_tensor(rowA[0:1, 1:KP], rF[0:1, 0:KP - 1], join[0:1, 1:KP], ALU.add)
                            nc.vector.memset(rowB[0:1, KP - 1:KP], -BIG)
                            nc.vector.tensor_tensor(rowB[0:1, 0:KP - 1], rL[0:1, 1:KP], join[0:1, 1:KP], ALU.add).then_inc(s_ci, 1)
                            dve.wait_ge(s_cc, h + 1)
                            link(nc.vector.tensor_copy(cin[:, :], pC[:, :]))
                            for q, away in enumerate((notfirst, notlast)):
                                for b in range(KB):
                                    ins = nc.vector.scalar_tensor_tensor(m3[:, b, :], away[:, b, :], cin[:, q * KB + b:q * KB + b + 1],
                                                                         m3[:, b, :], ALU.add, ALU.max)
                                link(ins)
                            ins = nc.vector.tensor_tensor(e[:, :], e[:, :], m[:, :], ALU.subtract)
                            if loops:
                                ins = nc.vector.tensor_tensor(dK[:, :], dK[:, :], m[:, :], ALU.subtract)
                            ins.then_inc(s_df, 1)
                            if loops:
                                dve.wait_ge(s_ex, h + 1)
                                nc.vector.tensor_tensor(dK[:, :], dK[:, :], flat(starts), ALU.mult).then_inc(s_df, 1)

                            dve.wait_ge(s_bt, h + 1)
                            for q, t in enumerate((gS, dS) if loops else (gS,)):
                                nc.vector.tensor_scalar(t[:, 0:512, ds(h, 1)].rearrange("p k a -> p (k a)"), pX[2 * q][:, :], 1.0, None, ALU.mult)
                                ins = nc.vector.tensor_scalar(t[:, 512:KP, ds(h, 1)].rearrange("p k a -> p (k a)"), pX[2 * q + 1][:, 0:R1], 1.0, None, ALU.mult)
                            ins.then_inc(s_bc, 1)

                    DF = 2 if loops else 1

                    @block.scalar
                    def _(act):
                        with act.Fori(0, H) as h:
                            nc.scalar.activation(g_h[:, :], gS[:, :, ds(h, 1)].rearrange("p k a -> p (k a)"), ACT.Copy)
                            nc.scalar.activation(d_h[:, :], dS[:, :, ds(h, 1)].rearrange("p k a -> p (k a)"), ACT.Copy).then_inc(s_hc, 1)
                            act.wait_ge(s_tr, h + 1)
                            nc.scalar.activation(gK[:, 0:512], pX[0][:, :], ACT.Copy)
                            nc.scalar.activation(gK[:, 512:W], pX[1][:, 0:R1], ACT.Copy)
                            nc.scalar.activation(dK[:, 0:512], pX[2][:, :], ACT.Copy)
                            nc.scalar.activation(dK[:, 512:W], pX[3][:, 0:R1], ACT.Copy).then_inc(s_kc, 1)
                            act.wait_ge(s_df, DF * h + 1)
                            ins = nc.scalar.activation(e[:, :], e[:, :], ACT.Exp)
                            if loops:
                                ins = nc.scalar.activation(dK[:, :], dK[:, :], ACT.Exp)
                            ins.then_inc(s_ex, 1)
                            act.wait_ge(s_bc, h + 1)

                    @block.tensor
                    def _(pe):
                        pe.wait_ge(s_col, 2)
                        to_rows(col, s_row)
                        pe.wait_ge(s_rc, 1)
                        if loops:
                            from_row(join, 0).then_inc(s_col, 1)

                        def turn(src, q):
                            for b in range(KB):
                                ins = nc.tensor.transpose(pX[2 * q + b // 4][:, (b % 4) * P:(b % 4 + 1) * P], src[:, b * P:(b + 1) * P], ident[:, :])
                            return ins

                        with pe.Fori(0, H) as h:
                            pe.wait_ge(s_hc, h + 1)
                            turn(g_h, 0)
                            turn(d_h, 1).then_inc(s_tr, 1)
                            pe.wait_ge(s_th, h + 1)
                            to_rows(col, s_rr)
                            pe.wait_ge(s_ci, h + 1)
                            nc.tensor.transpose(pR[:, 0:P], ident[:, :], ident[:, :])
                            from_row(rowA, 0)
                            from_row(rowB, KB).then_inc(s_cc, 1)
                            if loops:
                                pe.wait_ge(s_df, DF * h + 2)
                                turn(e, 0)
                                turn(dK, 1).then_inc(s_bt, 1)
                            else:
                                pe.wait_ge(s_ex, h + 1)
                                turn(e, 0).then_inc(s_bt, 1)

        def edge_sum(rows, acc, W, heads, gS, dS):
            with Stage() as se:
                G = [se.sb(f"G{j}", [P, D]) for j in range(U)]
                ib, gate = se.sb("ib", [P, U], I32), se.sb("gate", [1, 3])
                R = 4
                one = [se.sb(f"one{j}", [P, P]) for j in range(R)]
                msg = [se.sb(f"msg{j}", [P, W]) for j in range(R)] if heads else None
                pM = [se.ps(f"pM{j}", [P, W]) for j in range(R)]
                s_ib, s_gt, s_one, s_ex, s_m, s_acc = (se.sem(n) for n in ("s_ib", "s_gt", "s_one", "s_ex", "s_m", "s_acc"))
                s_g = [se.sem(f"s_g{j}") for j in range(U)]
                s_cons = s_one if heads else s_m
                with nc.Block() as block:
                    @block.gpsimd
                    def _(pool):
                        pool.memset(gate[:, :], 1.0).then_inc(s_gt, 1)
                        pool.wait_ge(s_gt, 1)
                        steps(pool, (0, gather_rows(pool, G, ib, gate, rows, s_ib, s_g, s_gt)))

                    @block.scalar
                    def _(act):
                        def weights(k, j):
                            freed(act, s_m, k - R + 1)
                            ins = nc.scalar.activation(msg[j % R][:, D:D + heads], tile(gS, k), ACT.Copy)
                            if dS is not None:
                                ins = nc.scalar.activation(msg[j % R][:, D + heads:W], tile(dS, k), ACT.Copy)
                            ins.then_inc(s_ex, 1)
                        steps(act, (0, gather_indices(act, ib, s_ib, s_cons, s_gt)), *([(0, weights)] if heads else []))

                    @block.vector
                    def _(dve):
                        load, node = step_nodes(dve)

                        def mark(k, j):
                            freed(dve, s_m, k - R + 1)
                            if heads:
                                nc.vector.tensor_scalar(one[j % R][:, :], iota[:, :], relS[:, ds(k, 1)], None, ALU.is_equal)
                                gathered(dve, s_g, k, j)
                                nc.vector.tensor_tensor(msg[j % R][:, 0:D].rearrange("p (h c) -> p h c", h=heads),
                                                        G[j][:, :].rearrange("p (h c) -> p h c", h=heads),
                                                        gS[:, ds(k, 1), :].rearrange("p a h -> p h a").broadcast_to([P, heads, D // heads]),
                                                        ALU.mult).then_inc(s_one, 1)
                            else:
                                nc.vector.tensor_scalar(one[j % R][:, :], iota[:, :], relS[:, ds(k, 1)], wS[:, ds(k, 1)],
                                                        ALU.is_equal, ALU.mult).then_inc(s_one, 1)
                        steps(dve, (0, load), (0, mark), (LAG, adder(dve, acc, pM, R, s_m, s_acc, node)))

                    @block.tensor
                    def _(pe):
                        def scatter(k, j):
                            pe.wait_ge(s_one, k + 1)
                            if heads:
                                pe.wait_ge(s_ex, k + 1)
                            else:
                                gathered(pe, s_g, k, j)
                            freed(pe, s_acc, k - R + 1)
                            nc.tensor.matmul(pM[j % R][:, :], one[j % R][:, :], (msg[j % R] if heads else G[j])[:, :],
                                             start=True, stop=True).then_inc(s_m, 1)
                        steps(pe, (0, scatter))

        def batch_norm(acc, gain, bias, rsg, brow):
            with Stage() as st:
                lane = st.sb("lane", [P, 1])
                live = st.sb("live", [P, 1])
                part = st.sb("part", [P, D])
                mean, var, vt = st.sb("mean", [P, D]), st.sb("var", [P, D]), st.sb("vt", [P, D])
                sq = [st.sb(f"sq{j}", [P, D]) for j in range(2)]
                grow = st.sb("grow", [P, D])
                pS = st.ps("pS", [P, D])
                s_l, s_b, s_c, s_p, s_s, s_rt, s_q, s_a = (st.sem(n) for n in ("s_l", "s_b", "s_c", "s_p", "s_s", "s_rt", "s_q", "s_a"))
                nodes = lambda t: t[:, 0:FULL + 1, 0:D]
                with nc.Block() as block:
                    @block.gpsimd
                    def _(pool):
                        pool.iota(lane[:, :], [[0, 1]], base=0, channel_multiplier=1, allow_small_or_imprecise_dtypes=True).then_inc(s_l, 1)

                    @block.sync
                    def _(sp):
                        sp.dma_start(grow[:, :], gain.rearrange("(a n) -> a n", a=1).broadcast_to([P, D])).then_inc(s_b, 16)
                        sp.dma_start(brow[:, :], bias.rearrange("(a n) -> a n", a=1).broadcast_to([P, D])).then_inc(s_b, 16)

                    @block.vector
                    def _(dve):
                        link = chain(dve, s_c)
                        dve.wait_ge(s_l, 1)
                        link(nc.vector.tensor_scalar(live[:, :], lane[:, :], float(REST), None, ALU.is_lt))
                        link(nc.vector.tensor_scalar(acc[:, FULL, 0:D], acc[:, FULL, 0:D], live[:, :], None, ALU.mult))
                        nc.vector.tensor_reduce(part[:, :], nodes(acc).rearrange("p t c -> p c t"), AX.X, ALU.add).then_inc(s_p, 1)
                        dve.wait_ge(s_s, 1)
                        link(nc.vector.tensor_scalar(mean[:, :], pS[:, :], 1 / N, None, ALU.mult))
                        link(nc.vector.tensor_tensor(nodes(acc), nodes(acc), mean[:, :].unsqueeze(1).broadcast_to([P, FULL + 1, D]), ALU.subtract))
                        link(nc.vector.tensor_scalar(acc[:, FULL, 0:D], acc[:, FULL, 0:D], live[:, :], None, ALU.mult))
                        nc.vector.memset(part[:, :], 0.0).then_inc(s_q, 1)

                        def add_square(n, j):
                            dve.wait_ge(s_a, n + 1)
                            dve.wait_ge(s_q, n + 1)
                            nc.vector.tensor_tensor(part[:, :], part[:, :], sq[j][:, :], ALU.add).then_inc(s_q, 1)
                        with dve.Fori(0, FULL // 2) as i:
                            add_square(2 * i, 0)
                            add_square(2 * i + 1, 1)
                        add_square(FULL, 0)
                        dve.wait_ge(s_s, 2)
                        nc.vector.tensor_scalar(var[:, :], pS[:, :], 1 / N, EPS, ALU.mult, ALU.add).then_inc(s_rt, 1)
                        dve.wait_ge(s_rt, 2)
                        link(nc.vector.reciprocal(rsg[:, :], rsg[:, :]))
                        newton_rsqrt(link, rsg[:, :], var[:, :], vt[:, :])
                        dve.wait_ge(s_b, 32)
                        link(nc.vector.tensor_tensor(rsg[:, :], rsg[:, :], grow[:, :], ALU.mult))

                    @block.scalar
                    def _(act):
                        act.wait_ge(s_q, 1)

                        def square(n, j, early=False):
                            if not early:
                                act.wait_ge(s_q, n)
                            nc.scalar.activation(sq[j][:, :], tile(acc[:, :, 0:D], n), ACT.Square).then_inc(s_a, 1)
                        square(0, 0, True)
                        square(1, 1, True)
                        with act.Fori(1, FULL // 2) as i:
                            square(2 * i, 0)
                            square(2 * i + 1, 1)
                        square(FULL, 0)
                        act.wait_ge(s_rt, 1)
                        nc.scalar.activation(rsg[:, :], var[:, :], ACT.Sqrt).then_inc(s_rt, 1)

                    @block.tensor
                    def _(pe):
                        for sem, value in ((s_p, 1), (s_q, FULL + 2)):
                            pe.wait_ge(sem, value)
                            nc.tensor.matmul(pS[:, :], ones[:, :], part[:, :], start=True, stop=True).then_inc(s_s, 1)

        def tile_pairs(eng, body):
            body(0, True)
            with eng.Fori(1, NT // 2) as i:
                body(i, False)

        def newton_rsqrt(link, r, v, t):
            link(nc.vector.tensor_tensor(t, r, r, ALU.mult))
            link(nc.vector.tensor_tensor(t, t, v, ALU.mult))
            link(nc.vector.tensor_scalar(t, t, -0.5, 1.5, ALU.mult, ALU.add))
            link(nc.vector.tensor_tensor(r, r, t, ALU.mult))

        def tile(t, n):
            return t[:, ds(n, 1), :].rearrange("p a c -> p (a c)")

        def layernorm_stats(x_sb, rstd, shift):
            with Stage() as st:
                bn = st.sb("bn", [P, NT, 6])
                mean, dif, ve = st.sb("mean", [P, NT]), st.sb("dif", [P, NT]), st.sb("ve", [P, NT])
                s_bn, s_ve, s_rt, s_ch = (st.sem(n) for n in ("s_bn", "s_ve", "s_rt", "s_ch"))
                with nc.Block() as block:
                    @block.vector
                    def _(dve):
                        with dve.Fori(0, NT // 2) as i:
                            for j in range(2):
                                ins = nc.vector.bn_stats(tile(bn, 2 * i + j), tile(x_sb, 2 * i + j))
                            ins.then_inc(s_bn, 1)
                        dve.wait_ge(s_bn, NT // 2)
                        link = chain(dve, s_ch)
                        link(nc.vector.tensor_tensor(mean[:, :], bn[:, :, 1], bn[:, :, 4], ALU.add))
                        link(nc.vector.tensor_tensor(dif[:, :], bn[:, :, 1], bn[:, :, 4], ALU.subtract))
                        link(nc.vector.tensor_tensor(ve[:, :], bn[:, :, 2], bn[:, :, 5], ALU.add))
                        link(nc.vector.tensor_tensor(dif[:, :], dif[:, :], dif[:, :], ALU.mult))
                        link(nc.vector.tensor_scalar(ve[:, :], ve[:, :], 1 / D, EPS, ALU.mult, ALU.add))
                        nc.vector.scalar_tensor_tensor(ve[:, :], dif[:, :], 0.25, ve[:, :], ALU.mult, ALU.add).then_inc(s_ve, 1)
                        dve.wait_ge(s_rt, 1)
                        link(nc.vector.reciprocal(rstd[:, :], rstd[:, :]))
                        newton_rsqrt(link, rstd[:, :], ve[:, :], dif[:, :])
                        link(nc.vector.scalar_tensor_tensor(shift[:, :], mean[:, :], -0.5, rstd[:, :], ALU.mult, ALU.mult))

                    @block.scalar
                    def _(act):
                        act.wait_ge(s_ve, 1)
                        nc.scalar.activation(rstd[:, :], ve[:, :], ACT.Sqrt).then_inc(s_rt, 1)

        def node_stage(layer, x_sb, rstd, shift, wide, load, biases, act_end, dve_end, store, ready=None):
            with Stage() as st:
                y = [st.sb(f"y{j}", [P, D]) for j in range(2)]
                yT = [st.sb(f"yT{j}", [P, D]) for j in range(2)]
                ready = ready or {}
                w_sb = [ready[q] if q in ready else st.sb(f"w_sb{q}", [P, 2, w]) for q, w in enumerate(wide)]
                b_sb = [st.sb(f"b_sb{q}", [1, w]) if biases[q] else None for q, w in enumerate(wide)]
                pT = [st.ps(f"pT{j}", [P, D]) for j in range(2)]
                pO = [[st.ps(f"pO{j}_{q}", [P, w]) for q, w in enumerate(wide)] for j in range(2)]
                row = [st.sb(f"row{j}", [P, D]) for j in range(2)]
                aux = [st.sb(f"aux{j}", [P, D]) for j in range(2)]
                s_w, s_y, s_t, s_yt, s_o, s_ae, s_de = (st.sem(n) for n in ("s_w", "s_y", "s_t", "s_yt", "s_o", "s_ae", "s_de"))
                s_st = [st.sem(f"s_st{j}") for j in range(2)]
                loads = []
                n_st = len(store)

                with nc.Block() as block:
                    @block.sync
                    def _(sp):
                        for dst, src in load(w_sb, b_sb):
                            loads.append(sp.dma_start(dst, src).then_inc(s_w, 16))

                        def body(i, first):
                            for j in range(2):
                                sp.wait_ge(s_ae, 2 * i + j + 1)
                                sp.wait_ge(s_de, 2 * i + j + 1)
                                for dst, src in store:
                                    sp.dma_start(dst(2 * i + j), src(row[j], aux[j])).then_inc(s_st[j], 16)
                        tile_pairs(sp, body)
                        for j in range(2):
                            sp.wait_ge(s_st[j], 16 * n_st * (NT // 2))

                    @block.scalar
                    def _(act):
                        def body(i, first):
                            for j in range(2):
                                n = 2 * i + j
                                if not first:
                                    act.wait_ge(s_t, n - 1)
                                nc.scalar.activation(y[j][:, :], tile(x_sb, n), ACT.Relu, bias=shift[:, ds(n, 1)],
                                                     scale=rstd[:, ds(n, 1)]).then_inc(s_y, 1)
                            for j in range(2):
                                n = 2 * i + j
                                act.wait_ge(s_o, n + 1)
                                if not first:
                                    act.wait_ge(s_st[j], 16 * n_st * i)
                                act_end(act, n, j, pO[j], row[j], aux[j]).then_inc(s_ae, 1)
                        tile_pairs(act, body)

                    @block.vector
                    def _(dve):
                        def body(i, first):
                            for j in range(2):
                                n = 2 * i + j
                                dve.wait_ge(s_t, n + 1)
                                if not first:
                                    dve.wait_ge(s_o, n - 1)
                                nc.vector.tensor_copy(yT[j][:, :], pT[j][:, :]).then_inc(s_yt, 1)
                            for j in range(2):
                                n = 2 * i + j
                                dve.wait_ge(s_o, n + 1)
                                if not first:
                                    dve.wait_ge(s_st[j], 16 * n_st * i)
                                dve_end(dve, n, j, pO[j], row[j], aux[j], s_ae).then_inc(s_de, 1)
                        tile_pairs(dve, body)

                    @block.tensor
                    def _(pe):
                        pe.wait_ge(s_w, 16 * len(loads))

                        def body(i, first):
                            for j in range(2):
                                n = 2 * i + j
                                pe.wait_ge(s_y, n + 1)
                                if not first:
                                    pe.wait_ge(s_yt, n - 1)
                                for c in range(2):
                                    ins = nc.tensor.transpose(pT[j][:, c * P:(c + 1) * P], y[j][:, c * P:(c + 1) * P], ident[:, :])
                                ins.then_inc(s_t, 1)
                            for j in range(2):
                                n = 2 * i + j
                                pe.wait_ge(s_yt, n + 1)
                                if not first:
                                    pe.wait_ge(s_ae, n - 1)
                                    pe.wait_ge(s_de, n - 1)
                                for q, w in enumerate(wide):
                                    if biases[q]:
                                        nc.tensor.matmul(pO[j][q][:, :], ones[0:1, :], b_sb[q][0:1, :], start=True, stop=False)
                                    for c in range(2):
                                        ins = nc.tensor.matmul(pO[j][q][:, :], yT[j][:, c * P:(c + 1) * P], w_sb[q][:, c, :],
                                                               start=(c == 0 and not biases[q]), stop=(c == 1))
                                ins.then_inc(s_o, 1)
                        tile_pairs(pe, body)

        def load_nodes(x_sb, src, rows):
            with Stage() as st:
                s_z, s_x = st.sem("s_z"), st.sem("s_x")
                with nc.Block() as block:
                    @block.vector
                    def _(dve):
                        nc.vector.memset(x_sb[:, FULL:NT, :], 0.0).then_inc(s_z, 1)

                    @block.sync
                    def _(sp):
                        sp.dma_start(x_sb[:, 0:FULL, :], src[0:FULL * P, :].rearrange("(t p) c -> p t c", p=P)).then_inc(s_x, 16)
                        sp.wait_ge(s_z, 1)
                        sp.dma_start(x_sb[0:REST, FULL, :], src[FULL * P:N, :]).then_inc(s_x, 16)
                        sp.wait_ge(s_x, 32)

        with Stage() as st0:
            a4S = st0.sb("a4S", [P, 4, KP])
            a10S = st0.sb("a10S", [P, NBAS, KP])
            with Stage() as st:
                zf = st.sb("zf", [P, 2 * D])
                padi = st.sb("padi", [1, 2, P], I32)
                frow_i = st.sb("frow_i", [1, ET], I32)
                trow_i = st.sb("trow_i", [1, ET], I32)
                frow = st.sb("frow", [1, ET])
                trow = st.sb("trow", [1, ET])
                kcol_i = st.sb("kcol_i", [P, KB], I32)
                kcol = st.sb("kcol", [P, KB])
                hit = st.sb("hit", [P, ET - 1])
                tk = st.sb("tk", [P, KB])
                tki = st.sb("tki", [P, KB], I32)
                nk = st.sb("nk", [P, KB])
                nkc = st.sb("nkc", [P, KB])
                nki = st.sb("nki", [P, KB], I32)
                base = st.sb("base", [P, KB])
                relK = st.sb("relK", [P, KB, P])
                m1 = st.sb("m1", [P, KB, P])
                gt = st.sb("gt", [MUL, 2, 3, 3 * MUL])
                nodeF = st.sb("nodeF", [P, KP])
                gdst = st.sb("gdst", [P, KB, P], I32)
                gsrc = st.sb("gsrc", [P, KB, P], I32)
                gsf = st.sb("gsf", [P, KB, P])
                gw = st.sb("gw", [P, KB, P])
                g4 = st.sb("g4", [P, 4 * P])
                g10 = st.sb("g10", [P, NBAS * P])
                oh4 = st.sb("oh4", [P, 2, 4, P], BF16)
                deg = st.sb("deg", [P, NT])
                degt = st.sb("degt", [P, NT])
                zb = st.sb("zb", [P, P], BF16)
                nh4 = st.sb("nh4", [P, 2, 4, NT], BF16)
                pS = [st.ps(f"pS{n}", [P, (ET - 1) // 2]) for n in range(2)]
                pT = [st.ps(f"pT{n}", [P, P]) for n in range(4)]
                pC = st.ps("pC", [P, NT])
                s_const, s_zero, s_pad, s_first, s_row = (st.sem(n) for n in ("s_const", "s_zero", "s_pad", "s_first", "s_row"))
                s_ts, s_v, s_tk, s_nd, s_ndd, s_ndr = (st.sem(n) for n in ("s_ts", "s_v", "s_tk", "s_nd", "s_ndd", "s_ndr"))
                s_w1, s_w2, s_gd, s_gs, s_gw = (st.sem(n) for n in ("s_w1", "s_w2", "s_gd", "s_gs", "s_gw"))
                s_g4, s_g10, s_kf, s_tr, s_cp = (st.sem(n) for n in ("s_g4", "s_g10", "s_kf", "s_tr", "s_cp"))
                s_oh, s_cn, s_pc, s_deg = (st.sem(n) for n in ("s_oh", "s_cn", "s_pc", "s_deg"))
                PADS = E // 50

                with nc.Block() as block:
                    @block.sync
                    def _(sp):
                        for dst, src, w in ((dst_pad, a["dst"], 1), (src_pad, a["src"], 1), (w_pad, a["edge_weight"], 1),
                                            (a4_pad, a["edge_attr_4"].rearrange("e c -> (e c)"), 4),
                                            (a10_pad, a["edge_attr_10"].rearrange("e c -> (e c)"), NBAS)):
                            sp.dma_start(dst[0:E * w].rearrange("(a b) -> a b", a=50 * w),
                                         src.rearrange("(a b) -> a b", a=50 * w)).then_inc(s_pad, 16)
                        sp.wait_ge(s_zero, 3)
                        sp.dma_start(dst_pad[E:EPAD].rearrange("(a b) -> a b", a=1), padi[0:1, 0, 0:EPAD - E]).then_inc(s_pad, 16)
                        sp.dma_start(src_pad[E:EPAD].rearrange("(a b) -> a b", a=1), padi[0:1, 1, 0:EPAD - E]).then_inc(s_pad, 16)
                        sp.dma_start(w_pad[E:EPAD].rearrange("(a b) -> a b", a=1), zf[0:1, 0:EPAD - E]).then_inc(s_pad, 16)
                        sp.dma_start(a4_pad[4 * E:4 * EPAD].rearrange("(a b) -> a b", a=4), zf[0:4, 0:EPAD - E]).then_inc(s_pad, 16)
                        sp.dma_start(a10_pad[NBAS * E:NBAS * EPAD].rearrange("(a b) -> a b", a=NBAS), zf[0:NBAS, 0:EPAD - E]).then_inc(s_pad, 16)
                        sp.wait_ge(s_pad, 160)
                        with nc.allow_non_contiguous_dma(reason="one dst of each edge tile"):
                            sp.dma_start(frow_i[0:1, :], dst_pad.rearrange("(a t p) -> a t p", a=1, p=P)[:, :, 0]).then_inc(s_first, 16)
                        sp.wait_ge(s_nd, 1)
                        with nc.allow_non_contiguous_dma(reason="896 step entries"):
                            sp.dma_start(node_i.rearrange("(b p) -> p b", p=P), nki[:, :]).then_inc(s_ndd, 16)
                            sp.dma_start(node_f.rearrange("(b p) -> p b", p=P), nkc[:, :]).then_inc(s_ndd, 16)
                        sp.wait_ge(s_ndd, 32)
                        sp.wait_ge(s_zero, 7)
                        sp.dma_start(nodeR[0:1, LAG:KP + LAG], node_i.rearrange("(a k) -> a k", a=1)).then_inc(s_ndr, 16)
                        sp.dma_start(nodeF[:, :], node_f.rearrange("(a k) -> a k", a=1).broadcast_to([P, KP])).then_inc(s_ndr, 16)
                        for r in range(2):
                            sp.dma_start(wbig[r * P:(r + 1) * P, :], zf[:, :]).then_inc(s_w1, 16)
                        sp.wait_ge(s_zero, 4)
                        for f, (w0, w1) in enumerate((("L0_gnn_W_li0", "L0_gnn_W_li1"), ("L0_gnn_W_lm0", "L0_gnn_W_lm1"))):
                            for m in range(3):
                                sp.dma_start(gt[:, f, m, m * MUL:(m + 1) * MUL], a[w1]).then_inc(s_w1, 16)
                        sp.wait_ge(s_w1, 128)
                        for f, w0 in enumerate(("L0_gnn_W_li0", "L0_gnn_W_lm0")):
                            sp.dma_start(wbig[0:MUL, f * D:f * D + MUL], a[w0]).then_inc(s_w2, 16)
                            sp.dma_start(wbig[MUL:D, f * D + MUL:(f + 1) * D].rearrange("(u m) c -> u m c", m=3),
                                         gt[:, f, :, :]).then_inc(s_w2, 16)
                        sp.wait_ge(s_w2, 64)
                        sp.wait_ge(s_ndr, 32)

                    @block.gpsimd
                    def _(pool):
                        pool.iota(kcol_i[:, :], [[P, KB]], base=0, channel_multiplier=1).then_inc(s_const, 1)
                        pool.iota(trow_i[:, :], [[1, ET]], base=0, channel_multiplier=0).then_inc(s_const, 1)
                        pool.iota(iota[:, :], [[1, P]], base=0, channel_multiplier=0,
                                  allow_small_or_imprecise_dtypes=True).then_inc(s_const, 1)
                        pool.memset(ident[:, :], 0.0).then_inc(s_const, 1)
                        pool.wait_ge(s_const, 4)
                        pool.affine_select(out=ident[:, :], in_=ident[:, :], compare_op=ALU.not_equal, fill=1.0, base=0,
                                           pattern=[[-1, P]], channel_multiplier=1).then_inc(s_const, 1)
                        pool.wait_ge(s_tk, 1)
                        for b in range(KB):
                            at = bass.IndirectOffsetOnAxis(ap=tki[:, b:b + 1], axis=0)
                            rows = lambda t: t.rearrange("(t q) -> t q", t=ET)
                            pool.indirect_dma_start(gdst[:, b, :], None, rows(dst_pad), at).then_inc(s_gd, 16)
                            pool.indirect_dma_start(gsrc[:, b, :], None, rows(src_pad), at).then_inc(s_gs, 16)
                            pool.indirect_dma_start(gw[:, b, :], None, rows(w_pad), at).then_inc(s_gw, 16)
                        for b in range(KB):
                            if b:
                                pool.wait_ge(s_tr, 3 * KB + 14 * (b - 1) + 4)
                            pool.indirect_dma_start(g4[:, :], None, rows(a4_pad), bass.IndirectOffsetOnAxis(ap=tki[:, b:b + 1], axis=0)).then_inc(s_g4, 16)
                            if b:
                                pool.wait_ge(s_tr, 3 * KB + 14 * b)
                            pool.indirect_dma_start(g10[:, :], None, rows(a10_pad), bass.IndirectOffsetOnAxis(ap=tki[:, b:b + 1], axis=0)).then_inc(s_g10, 16)

                    @block.vector
                    def _(dve):
                        nc.vector.memset(zf[:, :], 0.0).then_inc(s_zero, 1)
                        nc.vector.memset(padi[0:1, 0, :], NOWHERE).then_inc(s_zero, 1)
                        nc.vector.memset(padi[0:1, 1, :], 0).then_inc(s_zero, 1)
                        nc.vector.memset(gt[:, :, :, :], 0.0).then_inc(s_zero, 1)
                        nc.vector.memset(ones[:, :], 1.0).then_inc(s_zero, 1)
                        nc.vector.memset(zb[:, :], 0.0).then_inc(s_zero, 1)
                        nc.vector.memset(nodeR[0:1, 0:LAG], 0).then_inc(s_zero, 1)
                        link = chain(dve, s_v)
                        dve.wait_ge(s_const, 5)
                        dve.wait_ge(s_first, 16)
                        link(nc.vector.tensor_scalar(frow_i[:, :], frow_i[:, :], 7, None, ALU.arith_shift_right))
                        link(nc.vector.tensor_copy(frow[:, :], frow_i[:, :]))
                        link(nc.vector.tensor_copy(trow[:, :], trow_i[:, :]))
                        link(nc.vector.tensor_tensor(frow[:, :], frow[:, :], trow[:, :], ALU.add))
                        nc.vector.tensor_copy(kcol[:, :], kcol_i[:, :]).then_inc(s_row, 1)
                        dve.wait_ge(s_row, 1)
                        dve.wait_ge(s_ts, 2)
                        for b in range(KB):
                            for n in range(2):
                                link(nc.vector.tensor_scalar(hit[:, n * (ET // 2):(n + 1) * (ET // 2)], pS[n][:, :],
                                                             kcol[:, b:b + 1], None, ALU.is_le))
                            link(nc.vector.tensor_reduce(tk[:, b:b + 1], hit[:, :], AX.X, ALU.add))
                        link(nc.vector.tensor_copy(tki[:, :], tk[:, :]))
                        nc.vector.tensor_tensor(nk[:, :], kcol[:, :], tk[:, :], ALU.subtract).then_inc(s_tk, 1)
                        dve.wait_ge(s_tk, 1)
                        link(nc.vector.tensor_scalar(nkc[:, :], nk[:, :], float(NT - 1), None, ALU.min))
                        link(nc.vector.tensor_scalar(base[:, :], nk[:, :], float(-P), None, ALU.mult))
                        nc.vector.tensor_copy(nki[:, :], nkc[:, :]).then_inc(s_nd, 1)
                        dve.wait_ge(s_gd, 16 * KB)
                        link(nc.vector.tensor_copy(dstK[:, :, :], gdst[:, :, :]))
                        for b in range(KB):
                            last = nc.vector.tensor_scalar(relK[:, b, :], dstK[:, b, :], base[:, b:b + 1], None, ALU.add)
                        link(last)
                        dve.wait_ge(s_gs, 16 * KB)
                        dve.wait_ge(s_gw, 16 * KB)
                        nc.vector.tensor_copy(gsf[:, :, :], gsrc[:, :, :]).then_inc(s_kf, 1)
                        link(nc.vector.tensor_scalar(m1[:, :, :], relK[:, :, :], 0.0, -BIG, ALU.is_lt, ALU.mult))
                        link(nc.vector.tensor_scalar(outK[:, :, :], relK[:, :, :], float(P), -BIG, ALU.is_ge, ALU.mult))
                        link(nc.vector.tensor_tensor(outK[:, :, :], outK[:, :, :], m1[:, :, :], ALU.add))
                        dve.wait_ge(s_ndr, 32)
                        dve.wait_ge(s_cp, 3 * KB)
                        with dve.Fori(0, K // 8) as i:
                            for h in range(2):
                                dve.wait_ge(s_cn, 2 * i + h + 1)
                                nc.vector.tensor_tensor(oh4[:, h, :, :], iota[:, :].unsqueeze(1).broadcast_to([P, 4, P]),
                                                        relS[:, ds(8 * i + 4 * h, 4)].unsqueeze(2).broadcast_to([P, 4, P]), ALU.is_equal)
                                nc.vector.tensor_tensor(nh4[:, h, :, :], iota[:, 0:NT].unsqueeze(1).broadcast_to([P, 4, NT]),
                                                        nodeF[:, ds(8 * i + 4 * h, 4)].unsqueeze(2).broadcast_to([P, 4, NT]),
                                                        ALU.is_equal).then_inc(s_oh, 1)
                        dve.wait_ge(s_pc, 1)
                        nc.vector.tensor_copy(cnt[:, :], pC[:, :]).then_inc(s_pc, 1)
                        dve.wait_ge(s_pc, 2)
                        nc.vector.tensor_scalar(deg[:, :], cnt[:, :], 1.0, None, ALU.max).then_inc(s_deg, 1)
                        dve.wait_ge(s_deg, 2)
                        link(nc.vector.reciprocal(dis[:, :], dis[:, :]))
                        newton_rsqrt(link, dis[:, :], deg[:, :], degt[:, :])

                    @block.tensor
                    def _(pe):
                        pe.wait_ge(s_zero, 6)
                        pe.wait_ge(s_row, 1)
                        for n in range(2):
                            nc.tensor.matmul(pS[n][:, :], ones[0:1, :], frow[0:1, 1 + n * (ET // 2):1 + (n + 1) * (ET // 2)],
                                             start=True, stop=True).then_inc(s_ts, 1)
                        pe.wait_ge(s_kf, 1)
                        count = 0

                        def turn(src):
                            nonlocal count
                            if count >= 4:
                                pe.wait_ge(s_cp, count - 3)
                            nc.tensor.transpose(pT[count % 4][:, :], src, ident[:, :]).then_inc(s_tr, 1)
                            count += 1

                        for g in (relK, gsf, gw):
                            for b in range(KB):
                                turn(g[:, b, :])
                        for b in range(KB):
                            pe.wait_ge(s_g4, 16 * b + 16)
                            for c in range(4):
                                turn(g4[:, :].rearrange("k (e c) -> k c e", c=4)[:, c, :])
                            pe.wait_ge(s_g10, 16 * b + 16)
                            for c in range(NBAS):
                                turn(g10[:, :].rearrange("k (e c) -> k c e", c=NBAS)[:, c, :])
                        nc.tensor.matmul(pC[:, :], zb[:, :], zb[:, 0:NT], start=True, stop=False).then_inc(s_cn, 2)
                        with pe.Fori(0, K // 8) as i:
                            for h in range(2):
                                pe.wait_ge(s_oh, 2 * i + h + 1)
                                for q in range(4):
                                    ins = nc.tensor.matmul(pC[:, :], oh4[:, h, q, :], nh4[:, h, q, :], start=False, stop=False)
                                ins.then_inc(s_cn, 1)
                        nc.tensor.matmul(pC[:, :], zb[:, :], zb[:, 0:NT], start=False, stop=True).then_inc(s_pc, 1)

                    @block.scalar
                    def _(act):
                        count = 0
                        for dst in (relS, srcI, wS):
                            for b in range(KB):
                                act.wait_ge(s_tr, count + 1)
                                nc.scalar.activation(dst[:, b * P:(b + 1) * P], pT[count % 4][:, :], ACT.Copy).then_inc(s_cp, 1)
                                count += 1
                        for b in range(KB):
                            for dst, w in ((a4S, 4), (a10S, NBAS)):
                                for c in range(w):
                                    act.wait_ge(s_tr, count + 1)
                                    nc.scalar.activation(dst[:, c, b * P:(b + 1) * P], pT[count % 4][:, :], ACT.Copy).then_inc(s_cp, 1)
                                    count += 1
                        act.wait_ge(s_deg, 1)
                        nc.scalar.activation(dis[:, :], deg[:, :], ACT.Sqrt).then_inc(s_deg, 1)
            attr = st0.sb("attr", [P, NT])
            sc_f = st0.sb("sc_f", [P, NT])
            sc_m = st0.sb("sc_m", [P, NT])
            sc_o = st0.sb("sc_o", [P, NT])
            with Stage() as st:
                s_a0, s_a, s_c = st.sem("s_a0"), st.sem("s_a"), st.sem("s_c")
                with nc.Block() as block:
                    @block.sync
                    def _(sp):
                        sp.wait_ge(s_a0, 1)
                        vec = a["node_vec1"].rearrange("n o -> (n o)")
                        with nc.allow_non_contiguous_dma(reason="6250 attributes, node on partition"):
                            sp.dma_start(attr[:, 0:FULL], vec[0:FULL * P].rearrange("(t p) -> p t", p=P)).then_inc(s_a, 16)
                            sp.dma_start(attr[0:REST, FULL:FULL + 1], vec[FULL * P:N].rearrange("(p o) -> p o", o=1)).then_inc(s_a, 16)

                    @block.vector
                    def _(dve):
                        nc.vector.memset(attr[:, :], 0.0).then_inc(s_a0, 1)
                        dve.wait_ge(s_a, 32)
                        link = chain(dve, s_c)
                        link(nc.vector.tensor_tensor(sc_f[:, :], attr[:, :], dis[:, :], ALU.mult))
                        link(nc.vector.tensor_scalar(sc_o[:, :], sc_f[:, :], math.cos(math.pi / 8) / math.sqrt(2 * MUL), None, ALU.mult))
                        link(nc.vector.tensor_scalar(sc_f[:, :], sc_f[:, :], 1 / math.sqrt(MUL), None, ALU.mult))
                        link(nc.vector.tensor_scalar(sc_m[:, :], attr[:, :], math.sin(math.pi / 8) / math.sqrt(MUL), None, ALU.mult))

            with Stage() as st:
                x_sb = st.sb("x_in", [P, NT, D])
                rstd, shift = st.sb("rstd0", [P, NT]), st.sb("shift0", [P, NT])
                load_nodes(x_sb, a["x"], N)
                layernorm_stats(x_sb, rstd, shift)

                def act_end(act, n, j, pO, row, aux):
                    return nc.scalar.activation(row[:, :], pO[0][:, 0:D], ACT.Copy, scale=sc_f[:, ds(n, 1)])

                def dve_end(dve, n, j, pO, row, aux, s_ae):
                    xt = tile(x_sb, n)
                    nc.vector.scalar_tensor_tensor(aux[:, 0:MUL], pO[1][:, 0:MUL], sc_m[:, ds(n, 1)], xt[:, 0:MUL],
                                                   ALU.mult, ALU.add)
                    return nc.vector.scalar_tensor_tensor(
                        aux[:, MUL:D].rearrange("p (k m) -> p m k", m=3), pO[1][:, MUL:D].rearrange("p (m k) -> p m k", m=3),
                        sc_m[:, ds(n, 1)], xt[:, MUL:D].rearrange("p (k m) -> p m k", m=3), ALU.mult, ALU.add)

                node_stage(0, x_sb, rstd, shift, [D, D],
                           lambda w, b: [(w[q][:, :, :], wbig[:, q * D:(q + 1) * D].rearrange("(c p) n -> p c n", p=P)) for q in range(2)],
                           [False, False], act_end, dve_end,
                           [(lambda n: table[0][ds(n * P, P), :], lambda row, aux: row[:, :]),
                            (lambda n: base0[ds(n * P, P), :], lambda row, aux: aux[:, :])])

            with Stage() as st:
                acc = st.sb("acc0", [P, NT, 2 * D])
                with Stage() as se:
                    G = [se.sb(f"G{j}", [P, D]) for j in range(U)]
                    ib = se.sb("ib", [P, U], I32)
                    gate = se.sb("gate", [1, 3])
                    w1p = se.sb("w1p", [4 * NBAS, 4, NHID])
                    w2s = se.sb("w2s", [NHID, D])
                    a10 = [se.sb(f"a10_{h}", [P, P]) for h in range(2)]
                    a10T = [se.sb(f"a10T_{h}", [4 * NBAS, P]) for h in range(2)]
                    hid = [se.sb(f"hid{j}", [NHID, P]) for j in range(2)]
                    oh = [se.sb(f"oh{j}", [P, 4, P]) for j in range(4)]
                    one = [se.sb(f"one{j}", [P, P]) for j in range(2)]
                    prod = [se.sb(f"prod{j}", [P, 8, MUL]) for j in range(2)]
                    pA = se.ps("pA", [P, P])
                    pH = [se.ps(f"pH{j}", [NHID, P]) for j in range(2)]
                    pE = [se.ps(f"pE{j}", [P, D]) for j in range(2)]
                    pM = [se.ps(f"pM{j}", [P, 8, MUL]) for j in range(2)]
                    s_w, s_z, s_c, s_ib, s_cons = (se.sem(n) for n in ("s_w", "s_z", "s_c", "s_ib", "s_cons"))
                    s_g = [se.sem(f"s_g{j}") for j in range(U)]
                    s_a, s_at, s_ac, s_h, s_hs, s_e = (se.sem(n) for n in ("s_a", "s_at", "s_ac", "s_h", "s_hs", "s_e"))
                    s_one, s_oh, s_oh0, s_m, s_acc, s_gt = (se.sem(n) for n in ("s_one", "s_oh", "s_oh0", "s_m", "s_acc", "s_gt"))
                    with nc.Block() as block:
                        @block.sync
                        def _(sp):
                            sp.wait_ge(s_z, 1)
                            for j in range(4):
                                sp.dma_start(w1p[j * NBAS:(j + 1) * NBAS, j, :], a["L0_gnn_W_mlp1"]).then_inc(s_w, 16)
                            for q, c in enumerate((0, 2, 3, 1)):
                                sp.dma_start(w2s[:, q * MUL:(q + 1) * MUL], a["L0_gnn_W_mlp2"][:, c * MUL:(c + 1) * MUL]).then_inc(s_w, 16)

                        @block.gpsimd
                        def _(pool):
                            pool.memset(gate[:, :], 1.0).then_inc(s_gt, 1)
                            pool.wait_ge(s_gt, 1)
                            steps(pool, (0, gather_rows(pool, G, ib, gate, table[0], s_ib, s_g, s_gt)))

                        @block.scalar
                        def _(act):
                            act.wait_ge(s_z, 4)

                            def features(k, q, h):
                                freed(act, s_at, q - 1)
                                nc.scalar.activation(a10[h][:, 0:4 * NBAS].rearrange("p (k c) -> p k c", k=4),
                                                     a10S[:, :, ds(k, 4)].rearrange("p c k -> p k c"), ACT.Copy).then_inc(s_a, 1)

                            def turned(q, h):
                                act.wait_ge(s_at, q + 1)
                                freed(act, s_h, 4 * q - 4)
                                nc.scalar.activation(a10T[h][:, :], pA[0:4 * NBAS, :], ACT.Copy).then_inc(s_ac, 1)

                            def next_quad(k, j):
                                if j % 4 in (0, 3):
                                    q = (k - j) // 4 + j // 4 + 1
                                    if j % 4 == 0:
                                        features(k + 4, q, 1 - j // 4)
                                    else:
                                        turned(q, 1 - j // 4)

                            def silu(k, j):
                                act.wait_ge(s_h, k + 1)
                                freed(act, s_e, k - 1)
                                nc.scalar.activation(hid[j % 2][:, :], pH[j % 2][:, :], ACT.Silu,
                                                     scale=1 / math.sqrt(NBAS)).then_inc(s_hs, 1)

                            def vectors(k, j):
                                act.wait_ge(s_one, k + 1)
                                freed(act, s_m, k - 3)
                                for m in range(1, 4):
                                    ins = nc.scalar.activation(oh[j % 4][:, m, :], one[j % 2][:, :], ACT.Copy,
                                                               scale=a4S[:, m, ds(k, 1)])
                                ins.then_inc(s_oh, 1)
                            features(0, 0, 0)
                            turned(0, 0)
                            steps(act, (0, gather_indices(act, ib, s_ib, s_cons, s_gt)), (0, silu), (0, vectors), (0, next_quad))

                        @block.vector
                        def _(dve):
                            nc.vector.memset(w1p[:, :, :], 0.0).then_inc(s_z, 1)
                            for h in range(2):
                                nc.vector.memset(a10[h][:, :], 0.0).then_inc(s_z, 1)
                            nc.vector.memset(acc[:, :, :], 0.0).then_inc(s_z, 1)
                            dve.wait_ge(s_w, 16 * 8)
                            dve.wait_ge(s_z, 4)
                            link = chain(dve, s_c)
                            link(nc.vector.tensor_scalar(w2s[:, 0:3 * MUL], w2s[:, 0:3 * MUL], 1 / math.sqrt(NHID), None, ALU.mult))
                            link(nc.vector.tensor_scalar(w2s[:, 3 * MUL:D], w2s[:, 3 * MUL:D], 1 / math.sqrt(3 * NHID), None, ALU.mult))
                            load, node = step_nodes(dve)

                            def mark(k, j):
                                freed(dve, s_oh, k - 1)
                                nc.vector.tensor_scalar(one[j % 2][:, :], iota[:, :], relS[:, ds(k, 1)], None, ALU.is_equal).then_inc(s_one, 1)
                                freed(dve, s_m, k - 3)
                                nc.vector.tensor_scalar(oh[j % 4][:, 0, :], iota[:, :], relS[:, ds(k, 1)], a4S[:, 0, ds(k, 1)],
                                                        ALU.is_equal, ALU.mult).then_inc(s_oh0, 1)

                            def products(k, j):
                                dve.wait_ge(s_e, k + 1)
                                gathered(dve, s_g, k, j)
                                freed(dve, s_m, k - 1)
                                w = pE[j % 2][:, :].rearrange("p (b c) -> p b c", c=MUL)
                                g = G[j][:, :].rearrange("p (b c) -> p b c", c=MUL)
                                nc.vector.tensor_tensor(prod[j % 2][:, 0:8:7, :], w[:, 0:2, :], g[:, 0:1, :].broadcast_to([P, 2, MUL]), ALU.mult)
                                nc.vector.tensor_tensor(prod[j % 2][:, 1:7, :].rearrange("p (q m) c -> p q m c", q=2),
                                                        w[:, 2:4, :].unsqueeze(2).broadcast_to([P, 2, 3, MUL]),
                                                        g[:, 1:4, :].unsqueeze(1).broadcast_to([P, 2, 3, MUL]), ALU.mult).then_inc(s_cons, 1)
                            flat = [t.rearrange("p b c -> p (b c)") for t in pM]
                            steps(dve, (0, load), (0, mark), (1, products), (LAG, adder(dve, acc, flat, 2, s_m, s_acc, node)))

                        @block.tensor
                        def _(pe):
                            pe.wait_ge(s_w, 16 * 8)
                            pe.wait_ge(s_c, 2)

                            def turn(q, h):
                                pe.wait_ge(s_a, q + 1)
                                freed(pe, s_ac, q)
                                nc.tensor.transpose(pA[:, :], a10[h][:, :], ident[:, :]).then_inc(s_at, 1)

                            def next_quad(k, j):
                                if j % 4 == 2:
                                    turn((k - j) // 4 + j // 4 + 1, 1 - j // 4)

                            def hidden(k, j):
                                if j % 4 == 0:
                                    pe.wait_ge(s_ac, (k - j) // 4 + j // 4 + 1)
                                freed(pe, s_hs, k - 1)
                                nc.tensor.matmul(pH[j % 2][:, :], w1p[:, j % 4, :], a10T[j // 4][:, :], start=True, stop=True).then_inc(s_h, 1)

                            def edge_weights(k, j):
                                pe.wait_ge(s_hs, k + 1)
                                freed(pe, s_cons, k - 1)
                                nc.tensor.matmul(pE[j % 2][:, :], hid[j % 2][:, :], w2s[:, :], start=True, stop=True).then_inc(s_e, 1)

                            def scatter(k, j):
                                pe.wait_ge(s_oh, k + 1)
                                pe.wait_ge(s_oh0, k + 1)
                                pe.wait_ge(s_cons, k + 1)
                                freed(pe, s_acc, k - 1)
                                o, p, m = oh[j % 4], prod[j % 2], pM[j % 2]
                                nc.tensor.matmul(m[:, 0:4, :], o[:, 0, :], p[:, 0:4, :], start=True, stop=False)
                                nc.tensor.matmul(m[:, 4:6, :], o[:, 1, :], p[:, 4:8:3, :], start=False, stop=False)
                                for q in range(2):
                                    nc.tensor.matmul(m[:, 4, :], o[:, 2 + q, :], p[:, 5 + q, :], start=False, stop=False)
                                    ins = nc.tensor.matmul(m[:, 6 + q, :], o[:, 2 + q, :], p[:, 7, :], start=False, stop=(q == 1))
                                ins.then_inc(s_m, 1)
                            turn(0, 0)
                            steps(pe, (0, hidden), (1, edge_weights), (2, scatter), (0, next_quad))

                with Stage() as se:
                    wo = se.sb("wo", [P, 2, MUL])
                    ms = [se.sb(f"ms{j}", [P, 8, MUL]) for j in range(2)]
                    mT = [se.sb(f"mT{j}", [P, 2 * D]) for j in range(2)]
                    bs = [se.sb(f"bs{j}", [P, D]) for j in range(2)]
                    xo = [se.sb(f"xo{j}", [P, D]) for j in range(2)]
                    pT = [se.ps(f"pT{j}", [P, 2 * D]) for j in range(2)]
                    pO = [se.ps(f"pO{j}", [P, D]) for j in range(2)]
                    s_w, s_ms, s_t, s_mt, s_o, s_x = (se.sem(n) for n in ("s_w", "s_ms", "s_t", "s_mt", "s_o", "s_x"))
                    s_b = [se.sem(f"s_b{j}") for j in range(2)]
                    s_st = [se.sem(f"s_st{j}") for j in range(2)]

                    with nc.Block() as block:
                        @block.sync
                        def _(sp):
                            sp.dma_start(wo[:, 0, :], a["L0_gnn_W_lo0"]).then_inc(s_w, 16)
                            sp.dma_start(wo[0:MUL, 1, :], a["L0_gnn_W_lo1"][MUL:2 * MUL, :]).then_inc(s_w, 16)
                            sp.dma_start(wo[MUL:P, 1, :], a["L0_gnn_W_lo1"][0:MUL, :]).then_inc(s_w, 16)

                            def body(i, first):
                                for j in range(2):
                                    if not first:
                                        sp.wait_ge(s_x, 2 * i + j - 1)
                                    sp.dma_start(bs[j][:, :], base0[ds((2 * i + j) * P, P), :]).then_inc(s_b[j], 16)
                            tile_pairs(sp, body)

                        @block.scalar
                        def _(act):
                            def body(i, first):
                                for j in range(2):
                                    n = 2 * i + j
                                    if not first:
                                        act.wait_ge(s_t, n - 1)
                                    nc.scalar.activation(ms[j][:, :, :].rearrange("p (c h) k -> p h c k", h=2),
                                                         tile(acc, n).rearrange("p (h c k) -> p h c k", h=2, k=MUL), ACT.Copy,
                                                         scale=sc_o[:, ds(n, 1)]).then_inc(s_ms, 1)
                                for j in range(2):
                                    n = 2 * i + j
                                    act.wait_ge(s_x, n + 1)
                                    act.dma_start(x1[ds(n * P, P), :], xo[j][:, :]).then_inc(s_st[j], 16)
                            tile_pairs(act, body)
                            for j in range(2):
                                act.wait_ge(s_st[j], 16 * (NT // 2))

                        @block.vector
                        def _(dve):
                            def body(i, first):
                                for j in range(2):
                                    n = 2 * i + j
                                    dve.wait_ge(s_t, n + 1)
                                    if not first:
                                        dve.wait_ge(s_o, n - 1)
                                    nc.vector.tensor_copy(mT[j][:, :], pT[j][:, :]).then_inc(s_mt, 1)
                                for j in range(2):
                                    n = 2 * i + j
                                    dve.wait_ge(s_o, n + 1)
                                    dve.wait_ge(s_b[j], 16 * i + 16)
                                    if not first:
                                        dve.wait_ge(s_st[j], 16 * i)
                                    nc.vector.tensor_tensor(xo[j][:, 0:MUL], pO[j][:, 0:MUL], bs[j][:, 0:MUL], ALU.add)
                                    nc.vector.tensor_tensor(xo[j][:, MUL:D].rearrange("p (k m) -> p m k", m=3),
                                                            pO[j][:, MUL:D].rearrange("p (m k) -> p m k", m=3),
                                                            bs[j][:, MUL:D].rearrange("p (k m) -> p m k", m=3), ALU.add).then_inc(s_x, 1)
                            tile_pairs(dve, body)

                        @block.tensor
                        def _(pe):
                            pe.wait_ge(s_w, 48)

                            def body(i, first):
                                for j in range(2):
                                    n = 2 * i + j
                                    pe.wait_ge(s_ms, n + 1)
                                    if not first:
                                        pe.wait_ge(s_mt, n - 1)
                                    for c in range(4):
                                        ins = nc.tensor.transpose(pT[j][:, c * P:(c + 1) * P],
                                                                  ms[j][:, 2 * c:2 * c + 2, :].rearrange("p b k -> p (b k)"), ident[:, :])
                                    ins.then_inc(s_t, 1)
                                for j in range(2):
                                    n = 2 * i + j
                                    pe.wait_ge(s_mt, n + 1)
                                    if not first:
                                        pe.wait_ge(s_x, n - 1)
                                    for c in range(4):
                                        ins = nc.tensor.matmul(pO[j][:, c * MUL:(c + 1) * MUL], mT[j][:, c * P:(c + 1) * P],
                                                               wo[:, min(c, 1), :], start=True, stop=True)
                                    ins.then_inc(s_o, 1)
                            tile_pairs(pe, body)
        x_sb = top.sb("x_sb", [P, NT, D])
        rstd, shift = top.sb("rstd", [P, NT]), top.sb("shift", [P, NT])
        load_nodes(x_sb, x1, N)
        layernorm_stats(x_sb, rstd, shift)
        with Stage() as st1:
            F1 = D // H1
            gS, dS = st1.sb("gS", [P, KP, H1]), st1.sb("dS", [P, KP, H1])
            score = st1.sb("score", [P, NT, 2 * H1])
            with Stage() as st:
                wz = st.sb("wz", [P, 2, D])
                wa = st.sb("wa", [P, 2, 2 * H1])
                att = st.sb("att", [P, H1, 2 * F1])
                wp = st.sb("wp", [P, 2, D])
                s_w, s_c = st.sem("s_w"), st.sem("s_c")
                with nc.Block() as block:
                    @block.sync
                    def _(sp):
                        for h in range(H1):
                            sp.dma_start(wz[:, :, h * F1:(h + 1) * F1], a["L1_gnn_W"][h].rearrange("(c p) f -> p c f", p=P)).then_inc(s_w, 16)
                        sp.dma_start(att[:, :, :].rearrange("p h f -> p (h f)"),
                                     a["L1_gnn_att"].rearrange("(a h) f -> a (h f)", a=1).broadcast_to([P, H1 * 2 * F1])).then_inc(s_w, 16)

                    @block.vector
                    def _(dve):
                        dve.wait_ge(s_w, 16 * (H1 + 1))
                        link = chain(dve, s_c)
                        for half in range(2):
                            for c in range(2):
                                link(nc.vector.tensor_tensor(wp[:, c, :].rearrange("p (h f) -> p h f", h=H1),
                                                             wz[:, c, :].rearrange("p (h f) -> p h f", h=H1),
                                                             att[:, :, half * F1:(half + 1) * F1], ALU.mult))
                                link(nc.vector.tensor_reduce(wa[:, c, half * H1:(half + 1) * H1],
                                                             wp[:, c, :].rearrange("p (h f) -> p h f", h=H1), AX.X, ALU.add))

                def act_end(act, n, j, pO, row, aux):
                    return nc.scalar.activation(row[:, :], pO[0][:, :], ACT.Copy)

                def dve_end(dve, n, j, pO, row, aux, s_ae):
                    return nc.vector.tensor_copy(tile(score, n), pO[1][:, :])

                node_stage(1, x_sb, rstd, shift, [D, 2 * H1], lambda w, b: [], [False, False], act_end, dve_end,
                           [(lambda n: table[1][ds(n * P, P), :], lambda row, aux: row[:, :])], ready={0: wz, 1: wa})
            with Stage() as st:
                sc_d = st.sb("sc_d", [P, NT, H1])
                s_s, s_c = st.sem("s_s"), st.sem("s_c")
                with nc.Block() as block:
                    @block.sync
                    def _(sp):
                        sp.dma_start(small1.rearrange("(t p) h -> p t h", p=P), score[:, :, 0:H1]).then_inc(s_s, 16)
                        sp.wait_ge(s_s, 16)

                    @block.vector
                    def _(dve):
                        nc.vector.tensor_copy(sc_d[:, :, :], score[:, :, H1:2 * H1]).then_inc(s_c, 1)
                edge_scores(small1, sc_d, H1, gS, dS)
            edge_softmax(H1, gS, dS, 0.01, -1000.0, False)
            with Stage() as st:
                acc = st.sb("acc1", [P, NT, D + H1])
                den = st.sb("den", [P, NT, H1])
                s_z, s_c = st.sem("s_z"), st.sem("s_c")
                with nc.Block() as block:
                    @block.vector
                    def _(dve):
                        nc.vector.memset(acc[:, :, :], 0.0).then_inc(s_z, 1)
                edge_sum(table[1], acc, D + H1, H1, gS, None)
                with nc.Block() as block:
                    @block.vector
                    def _(dve):
                        link = chain(dve, s_c)
                        link(nc.vector.tensor_scalar(den[:, :, :], acc[:, :, D:D + H1], 1e-30, None, ALU.max))
                        link(nc.vector.reciprocal(den[:, :, :], den[:, :, :]))
                        heads = acc[:, :, 0:D].rearrange("p t (h f) -> p t h f", h=H1)
                        link(nc.vector.tensor_tensor(heads, heads, den[:, :, :].unsqueeze(3).broadcast_to([P, NT, H1, F1]), ALU.mult))
                        link(nc.vector.tensor_tensor(x_sb[:, :, :], x_sb[:, :, :], acc[:, :, 0:D], ALU.add))

        layernorm_stats(x_sb, rstd, shift)

        def act_end(act, n, j, pO, row, aux):
            return nc.scalar.activation(row[:, :], pO[0][:, :], ACT.Copy)

        def dve_end(dve, n, j, pO, row, aux, s_ae):
            return nc.vector.tensor_tensor(tile(x_sb, n), tile(x_sb, n), pO[1][:, :], ALU.add)

        node_stage(2, x_sb, rstd, shift, [D, D],
                   lambda w, b: [(w[0][:, :, :], a["L2_gnn_w_nbr"].rearrange("(c p) n -> p c n", p=P)),
                                 (w[1][:, :, :], a["L2_gnn_w_own"].rearrange("(c p) n -> p c n", p=P)),
                                 (b[1][0:1, :], a["L2_gnn_bias"].rearrange("(a n) -> a n", a=1))],
                   [False, True], act_end, dve_end, [(lambda n: table[2][ds(n * P, P), :], lambda row, aux: row[:, :])])
        edge_sum(table[2], x_sb, D, 0, None, None)

        layernorm_stats(x_sb, rstd, shift)
        with Stage() as st3:
            F3 = D // H3
            gS, dS = st3.sb("gS", [P, KP, H3]), st3.sb("dS", [P, KP, H3])
            with Stage() as st:
                score = st.sb("score", [P, NT, H3])
                s_l = st.sem("s_l")

                def act_end(act, n, j, pO, row, aux):
                    nc.scalar.activation(aux[:, :], pO[0][:, 0:D], ACT.Copy)
                    return nc.scalar.activation(row[:, :], pO[1][:, :], ACT.Copy)

                def dve_end(dve, n, j, pO, row, aux, s_ae):
                    dve.wait_ge(s_ae, n + 1)
                    nc.vector.tensor_tensor(aux[:, :], aux[:, :], pO[0][:, D:2 * D], ALU.mult).then_inc(s_l, 1)
                    dve.wait_ge(s_l, n + 1)
                    return nc.vector.tensor_reduce(tile(score, n), aux[:, :].rearrange("p (h c) -> p h c", h=H3), AX.X, ALU.add)

                def qkv(w, b):
                    for q, (name, o) in enumerate((("q", 0), ("k", D), ("v", 0))):
                        yield w[q // 2][:, :, o:o + D], a[f"L3_gnn_W{name}"].rearrange("(c p) n -> p c n", p=P)
                        yield b[q // 2][0:1, o:o + D], a[f"L3_gnn_b{name}"].rearrange("(a n) -> a n", a=1)

                node_stage(3, x_sb, rstd, shift, [2 * D, D], qkv, [True, True], act_end, dve_end,
                           [(lambda n: table[3][ds(n * P, P), :], lambda row, aux: row[:, :])])
                with Stage() as se:
                    s_c, s_s = se.sem("s_c"), se.sem("s_s")
                    with nc.Block() as block:
                        @block.vector
                        def _(dve):
                            nc.vector.tensor_scalar(score[:, :, :], score[:, :, :], 1 / math.sqrt(F3), None, ALU.mult).then_inc(s_c, 1)

                        @block.sync
                        def _(sp):
                            sp.wait_ge(s_c, 1)
                            sp.dma_start(small3.rearrange("(t p) h -> p t h", p=P), score[:, :, :]).then_inc(s_s, 16)
                            sp.wait_ge(s_s, 16)
                edge_scores(small3, score, H3, gS, dS)
            edge_softmax(H3, gS, dS, 0.2, None, True)
            acc = st3.sb("acc3", [P, NT, D + 2 * H3])
            with Stage() as st:
                s_z = st.sem("s_z")
                with nc.Block() as block:
                    @block.vector
                    def _(dve):
                        nc.vector.memset(acc[:, :, :], 0.0).then_inc(s_z, 1)
            edge_sum(table[3], acc, D + 2 * H3, H3, gS, dS)

            with Stage() as st:
                own, den = st.sb("own", [P, NT, H3]), st.sb("den", [P, NT, H3])
                alone = st.sb("alone", [P, NT])
                wo = st.sb("wo", [P, 2, D])
                bo = st.sb("bo", [1, D])
                v = [st.sb(f"v{j}", [P, D]) for j in range(2)]
                y = [st.sb(f"y{j}", [P, D]) for j in range(2)]
                vT = [st.sb(f"vT{j}", [P, D]) for j in range(2)]
                pT = [st.ps(f"pT{j}", [P, D]) for j in range(2)]
                pO = [st.ps(f"pO{j}", [P, D]) for j in range(2)]
                s_w, s_c, s_at, s_t, s_tc, s_o, s_r, s_y, s_l = (st.sem(n) for n in ("s_w", "s_c", "s_at", "s_t", "s_tc", "s_o", "s_r", "s_y", "s_l"))
                s_v = [st.sem(f"s_v{j}") for j in range(2)]
                with nc.Block() as block:
                    @block.sync
                    def _(sp):
                        sp.dma_start(wo[:, :, :], a["L3_gnn_Wo"].rearrange("(c p) n -> p c n", p=P)).then_inc(s_w, 16)
                        sp.dma_start(bo[0:1, :], a["L3_gnn_bo"].rearrange("(a n) -> a n", a=1)).then_inc(s_w, 16)

                        def body(i, first):
                            for j in range(2):
                                n = 2 * i + j
                                if not first:
                                    sp.wait_ge(s_t, n - 1)
                                sp.dma_start(v[j][:, :], table[3][ds(n * P, P), :]).then_inc(s_v[j], 16)
                        tile_pairs(sp, body)

                    @block.vector
                    def _(dve):
                        link = chain(dve, s_c)
                        link(nc.vector.tensor_scalar(alone[:, :], cnt[:, :], 0.0, None, ALU.is_equal))
                        link(nc.vector.tensor_tensor(own[:, :, :], acc[:, :, D + H3:D + 2 * H3],
                                                     alone[:, :].unsqueeze(2).broadcast_to([P, NT, H3]), ALU.add))
                        link(nc.vector.tensor_tensor(den[:, :, :], own[:, :, :], acc[:, :, D:D + H3], ALU.add))
                        link(nc.vector.reciprocal(den[:, :, :], den[:, :, :]))
                        heads = lambda t: t.rearrange("p (h c) -> p h c", h=H3)
                        wide = lambda t, n: t[:, ds(n, 1), :].rearrange("p a h -> p h a").broadcast_to([P, H3, F3])

                        def body(i, first):
                            for j in range(2):
                                n = 2 * i + j
                                dve.wait_ge(s_v[j], 16 * i + 16)
                                at = tile(acc[:, :, 0:D], n)
                                nc.vector.tensor_tensor(heads(v[j][:, :]), heads(v[j][:, :]), wide(own, n), ALU.mult).then_inc(s_l, 1)
                                dve.wait_ge(s_l, 2 * n + 1)
                                nc.vector.tensor_tensor(v[j][:, :], v[j][:, :], at, ALU.add).then_inc(s_l, 1)
                                dve.wait_ge(s_l, 2 * n + 2)
                                nc.vector.tensor_tensor(heads(v[j][:, :]), heads(v[j][:, :]), wide(den, n), ALU.mult).then_inc(s_at, 1)
                            for j in range(2):
                                n = 2 * i + j
                                dve.wait_ge(s_o, n + 1)
                                dve.wait_ge(s_y, n + 1)
                                nc.vector.tensor_tensor(tile(acc[:, :, 0:D], n), pO[j][:, :], y[j][:, :], ALU.add).then_inc(s_r, 1)
                        tile_pairs(dve, body)

                    @block.scalar
                    def _(act):
                        def body(i, first):
                            for j in range(2):
                                n = 2 * i + j
                                if not first:
                                    act.wait_ge(s_r, n - 1)
                                nc.scalar.activation(y[j][:, :], tile(x_sb, n), ACT.Relu, bias=shift[:, ds(n, 1)],
                                                     scale=rstd[:, ds(n, 1)]).then_inc(s_y, 1)
                            for j in range(2):
                                n = 2 * i + j
                                act.wait_ge(s_t, n + 1)
                                if not first:
                                    act.wait_ge(s_o, n - 1)
                                nc.scalar.activation(vT[j][:, :], pT[j][:, :], ACT.Copy).then_inc(s_tc, 1)
                        tile_pairs(act, body)

                    @block.tensor
                    def _(pe):
                        pe.wait_ge(s_w, 32)

                        def body(i, first):
                            for j in range(2):
                                n = 2 * i + j
                                pe.wait_ge(s_at, n + 1)
                                if not first:
                                    pe.wait_ge(s_tc, n - 1)
                                for c in range(2):
                                    ins = nc.tensor.transpose(pT[j][:, c * P:(c + 1) * P], v[j][:, c * P:(c + 1) * P], ident[:, :])
                                ins.then_inc(s_t, 1)
                            for j in range(2):
                                n = 2 * i + j
                                pe.wait_ge(s_tc, n + 1)
                                if not first:
                                    pe.wait_ge(s_r, n - 1)
                                nc.tensor.matmul(pO[j][:, :], ones[0:1, :], bo[0:1, :], start=True, stop=False)
                                for c in range(2):
                                    ins = nc.tensor.matmul(pO[j][:, :], vT[j][:, c * P:(c + 1) * P], wo[:, c, :], start=False, stop=(c == 1))
                                ins.then_inc(s_o, 1)
                        tile_pairs(pe, body)

            rsg, brow = st3.sb("rsg", [P, D]), st3.sb("brow", [P, D])
            batch_norm(acc, a["L3_gnn_bn1_g"], a["L3_gnn_bn1_b"], rsg, brow)

            with Stage() as st:
                FB = 2 * D // P
                w1 = st.sb("w1", [P, 2, 2 * D])
                w2 = st.sb("w2", [P, FB, D])
                b1 = st.sb("b1", [P, FB])
                b2 = st.sb("b2", [1, D])
                h1 = [st.sb(f"h1_{j}", [P, D]) for j in range(2)]
                hT = [st.sb(f"hT{j}", [P, D]) for j in range(2)]
                fT = [st.sb(f"fT{j}", [P, FB, P]) for j in range(2)]
                pT = [st.ps(f"pT{j}", [P, D]) for j in range(2)]
                pF = [st.ps(f"pF{j}", [P, FB, P]) for j in range(2)]
                pO = [st.ps(f"pO{j}", [P, D]) for j in range(2)]
                s_w, s_l, s_h, s_t, s_tc, s_f, s_fc, s_o, s_r = (st.sem(n) for n in ("s_w", "s_l", "s_h", "s_t", "s_tc", "s_f", "s_fc", "s_o", "s_r"))
                with nc.Block() as block:
                    @block.sync
                    def _(sp):
                        sp.dma_start(w1[:, :, :], a["L3_gnn_W1"].rearrange("(c p) n -> p c n", p=P)).then_inc(s_w, 16)
                        sp.dma_start(w2[:, :, :], a["L3_gnn_W2"].rearrange("(c p) n -> p c n", p=P)).then_inc(s_w, 16)
                        with nc.allow_non_contiguous_dma(reason="512 biases, feature on partition"):
                            sp.dma_start(b1[:, :], a["L3_gnn_b1"].rearrange("(c p) -> p c", p=P)).then_inc(s_w, 16)
                        sp.dma_start(b2[0:1, :], a["L3_gnn_b2"].rearrange("(a n) -> a n", a=1)).then_inc(s_w, 16)

                    @block.vector
                    def _(dve):
                        def body(i, first):
                            for j in range(2):
                                n = 2 * i + j
                                if not first:
                                    dve.wait_ge(s_t, n - 1)
                                    dve.wait_ge(s_r, n - 1)
                                nc.vector.tensor_tensor(h1[j][:, :], tile(acc[:, :, 0:D], n), rsg[:, :], ALU.mult).then_inc(s_l, 1)
                                dve.wait_ge(s_l, n + 1)
                                nc.vector.tensor_tensor(h1[j][:, :], h1[j][:, :], brow[:, :], ALU.add).then_inc(s_h, 1)
                            for j in range(2):
                                n = 2 * i + j
                                dve.wait_ge(s_o, n + 1)
                                nc.vector.tensor_tensor(tile(acc[:, :, 0:D], n), pO[j][:, :], h1[j][:, :], ALU.add).then_inc(s_r, 1)
                        tile_pairs(dve, body)

                    @block.scalar
                    def _(act):
                        act.wait_ge(s_w, 64)

                        def body(i, first):
                            for j in range(2):
                                n = 2 * i + j
                                act.wait_ge(s_t, n + 1)
                                if not first:
                                    act.wait_ge(s_f, n - 1)
                                nc.scalar.activation(hT[j][:, :], pT[j][:, :], ACT.Copy).then_inc(s_tc, 1)
                            for j in range(2):
                                n = 2 * i + j
                                act.wait_ge(s_f, n + 1)
                                if not first:
                                    act.wait_ge(s_o, n - 1)
                                for q in range(FB):
                                    ins = nc.scalar.activation(fT[j][:, q, :], pF[j][:, q, :], ACT.Relu, bias=b1[:, q:q + 1])
                                ins.then_inc(s_fc, 1)
                        tile_pairs(act, body)

                    @block.tensor
                    def _(pe):
                        pe.wait_ge(s_w, 64)

                        def body(i, first):
                            for j in range(2):
                                n = 2 * i + j
                                pe.wait_ge(s_h, n + 1)
                                if not first:
                                    pe.wait_ge(s_tc, n - 1)
                                for c in range(2):
                                    ins = nc.tensor.transpose(pT[j][:, c * P:(c + 1) * P], h1[j][:, c * P:(c + 1) * P], ident[:, :])
                                ins.then_inc(s_t, 1)
                            for j in range(2):
                                n = 2 * i + j
                                pe.wait_ge(s_tc, n + 1)
                                if not first:
                                    pe.wait_ge(s_fc, n - 1)
                                for q in range(FB):
                                    for c in range(2):
                                        ins = nc.tensor.matmul(pF[j][:, q, :], w1[:, c, q * P:(q + 1) * P], hT[j][:, c * P:(c + 1) * P],
                                                               start=(c == 0), stop=(c == 1))
                                ins.then_inc(s_f, 1)
                            for j in range(2):
                                n = 2 * i + j
                                pe.wait_ge(s_fc, n + 1)
                                if not first:
                                    pe.wait_ge(s_r, n - 1)
                                nc.tensor.matmul(pO[j][:, :], ones[0:1, :], b2[0:1, :], start=True, stop=False)
                                for q in range(FB):
                                    ins = nc.tensor.matmul(pO[j][:, :], fT[j][:, q, :], w2[:, q, :], start=False, stop=(q == FB - 1))
                                ins.then_inc(s_o, 1)
                        tile_pairs(pe, body)

            batch_norm(acc, a["L3_gnn_bn2_g"], a["L3_gnn_bn2_b"], rsg, brow)

            with Stage() as st:
                CH = NT // 5
                s_c, s_out = st.sem("s_c"), st.sem("s_out")
                with nc.Block() as block:
                    @block.vector
                    def _(dve):
                        for q in range(5):
                            link = chain(dve, s_c, 3 * q)
                            at = acc[:, q * CH:(q + 1) * CH, 0:D]
                            xt = x_sb[:, q * CH:(q + 1) * CH, :]
                            link(nc.vector.tensor_tensor(at, at, rsg[:, :].unsqueeze(1).broadcast_to([P, CH, D]), ALU.mult))
                            link(nc.vector.tensor_tensor(xt, xt, brow[:, :].unsqueeze(1).broadcast_to([P, CH, D]), ALU.add))
                            link(nc.vector.tensor_tensor(xt, xt, at, ALU.add))

                    @block.sync
                    def _(sp):
                        for q in range(5):
                            sp.wait_ge(s_c, 3 * q + 3)
                            last = min(FULL, (q + 1) * CH)
                            sp.dma_start(out[q * CH * P:last * P, :].rearrange("(t p) c -> p t c", p=P), x_sb[:, q * CH:last, :]).then_inc(s_out, 16)
                        sp.dma_start(out[FULL * P:N, :], x_sb[0:REST, FULL, :]).then_inc(s_out, 16)
                        sp.wait_ge(s_out, 96)

def kernel(**inputs):
    import concourse.bacc as _bacc
    from concourse import mybir as _mybir
    from concourse.bass_utils import run_bass_kernel_spmd as _run

    nc = _bacc.Bacc("TRN2", target_bir_lowering=False, num_devices=1)
    arrays, args = {}, {}
    for name, value in inputs.items():
        value = np.ascontiguousarray(value)
        arrays[f"in_{name}"] = value
        args[name] = nc.dram_tensor(f"in_{name}", value.shape, _mybir.dt.from_np(value.dtype), kind="ExternalInput").ap()
    out = nc.dram_tensor("out_x", (N, D), _mybir.dt.from_np(np.dtype("float32")), kind="ExternalOutput").ap()
    build(nc, args, out)
    r = _run(nc, [arrays], core_ids=[0])
    return r.results[0]["out_x"]
```

```python
import math

import numpy as np

N = 6250
D = 256
E = 106250
P = 128
NT = 2 * math.ceil(N / P / 2)
NP = NT * P
FULL, REST = N // P, N % P
ET = math.ceil(E / P)
EPAD = ET * P
U, U2 = 8, 16
LAG = 3
K = U2 * math.ceil((ET + math.ceil(N / P) - 1) / U2)
KB = math.ceil(K / P)
KP = KB * P
NOWHERE = 16383
BIG = 1.0e38
EPS = 1e-5
MUL = 64
NBAS, NHID = 10, 100
H1, H3 = 4, 8


def build(nc, a, out):
    import concourse.bass as bass
    from concourse import mybir
    from contextlib import ExitStack

    F32, I32, BF16 = mybir.dt.float32, mybir.dt.int32, mybir.dt.bfloat16
    ALU = mybir.AluOpType
    ACT = mybir.ActivationFunctionType
    AX = mybir.AxisListType
    ds = bass.ds

    def dram(name, shape, dt=F32):
        return nc.dram_tensor(name, shape, dt).ap()

    stages = []

    class Stage(ExitStack):

        def __init__(self):
            super().__init__()
            stages.append(self)
            self.tag = f"_{len(stages)}"
            self.sems = []

        def sb(self, name, shape, dt=F32):
            return self.enter_context(nc.sbuf_tensor(name + self.tag, list(shape), dt))

        def ps(self, name, shape):
            bank = self.enter_context(nc.psum_tensor(name + self.tag, [P, 512], F32))
            view = bank[0:shape[0], 0:math.prod(shape[1:])]
            return view if len(shape) == 2 else view.rearrange("p (b c) -> p b c", b=shape[1])

        def sem(self, name):
            handle = nc.alloc_semaphore(name + self.tag)
            self.sems.append(handle)
            return handle

        def __exit__(self, *exc):
            if self.sems and exc[0] is None:
                nc.clear_and_free_semaphores(self.sems)
                nc.all_engine_barrier(sem_only=True)
            return super().__exit__(*exc)

    def chain(eng, sem, base=0):
        count = [0]

        def link(ins):
            count[0] += 1
            ins.then_inc(sem, 1)
            eng.wait_ge(sem, base + count[0])
        return link

    dst_pad, src_pad, w_pad = dram("dst_pad", [EPAD], I32), dram("src_pad", [EPAD], I32), dram("w_pad", [EPAD])
    a4_pad, a10_pad = dram("a4_pad", [EPAD * 4]), dram("a10_pad", [EPAD * NBAS])
    node_i, node_f = dram("step_node_i", [KP], I32), dram("step_node_f", [KP])
    wbig = dram("wbig", [D, 2 * D])
    table = [dram(f"table{n}", [NP, D]) for n in range(4)]
    small1, small3 = dram("small1", [NP, H1]), dram("small3", [NP, H3])
    base0, x1 = dram("base0", [NP, D]), dram("x1", [NP, D])

    top = Stage()
    with top:
        ident = top.sb("ident", [P, P])
        iota = top.sb("iota", [P, P])
        ones = top.sb("ones", [P, P])
        relS = top.sb("relS", [P, KP])
        wS = top.sb("wS", [P, KP])
        srcI = top.sb("srcI", [P, KP], I32)
        dstK = top.sb("dstK", [P, KB, P])
        outK = top.sb("outK", [P, KB, P])
        nodeR = top.sb("nodeR", [1, KP + LAG], I32)
        cnt = top.sb("cnt", [P, NT])
        dis = top.sb("dis", [P, NT])

        AHEAD = -1

        def pipelined(eng, count, unroll, peel, *parts):
            def turn(i, skip):
                for j in range(unroll):
                    for lag, do in parts:
                        late = max(lag, 0)
                        if not skip or unroll * i + j >= late:
                            do(unroll * i + j - late, (j - late) % unroll)
            for i in range(peel):
                turn(i, True)
            with eng.Fori(peel, count // unroll) as i:
                turn(i, False)
            done = count // unroll * unroll
            for j in range(count - done + max(lag for lag, _ in parts)):
                for lag, do in parts:
                    if lag == AHEAD and j == 0:
                        do(done, 0)
                    if lag >= 0 and done + j - lag < count:
                        do(done + j - lag, (j - lag) % unroll)

        def freed(eng, sem, value):
            if not (type(value) is int and value <= 0):
                eng.wait_ge(sem, value)

        def steps(eng, u, *parts):
            pipelined(eng, K, u, 1, *parts)

        def tiles(eng, *parts):
            pipelined(eng, NT, 2, 2, *parts)

        def tiles4(eng, *parts):
            pipelined(eng, NT, 4, 1, *parts)

        def gather_indices(act, u, ahead, ib, s_ib, s_cons, s_gt):
            def fetch(k, j):
                nc.scalar.activation(ib[:, j:j + 4], srcI[:, ds(k, 4)], ACT.Copy).then_inc(s_ib, 1)
            for k in range(0, ahead, 4):
                fetch(k, k)

            def do(k, j):
                if j % 4 == 0:
                    freed(act, s_cons, k + ahead - u + 4)
                    if not (type(k) is int and k < u - ahead):
                        act.wait_ge(s_gt, (k + ahead - u + 8) // 4)
                    fetch(k + ahead, (j + ahead) % u)
            return do

        def gather_rows(pool, u, G, ib, gate, rows, s_ib, s_g, s_gt):
            pool.memset(gate[:, :], 1.0).then_inc(s_gt, 1)
            pool.wait_ge(s_gt, 1)

            def do(k, j):
                if j % 4 == 0:
                    pool.wait_ge(s_ib, (k - j) // 4 + j // 4 + 1)
                    h = j // 4
                    pool.tensor_tensor(gate[0:1, h:h + 1], gate[0:1, 4:5], gate[0:1, 4:5], ALU.mult).then_inc(s_gt, 1)
                pool.indirect_dma_start(G[j][:, :], None, rows,
                                        bass.IndirectOffsetOnAxis(ap=ib[:, j:j + 1], axis=0)).then_inc(s_g[j], 16)
            steps(pool, u, (0, do))

        def gathered(eng, u, s_g, k, j):
            eng.wait_ge(s_g[j], (k - j) // (u // 8) * 2 + 16)

        def step_nodes(eng, u):
            at = {}

            def node(k, j):
                return at[(j + LAG) % u]

            def load(k, j):
                if j % 8 == 0:
                    _, values = nc.values_load_multi_w_load_instructions(nodeR[0:1, ds(k, 8)], engines=[eng.engine], min_val=0, max_val=NT - 1)
                    at.update((j + q, v) for q, v in enumerate(values))
            return load, node

        def adder(dve, acc, pM, R, s_m, s_acc, node):
            def do(k, j):
                dve.wait_ge(s_m, k + 1)
                freed(dve, s_acc, k)
                at = tile(acc, node(k, j))
                nc.vector.tensor_tensor(at, at, pM[j % R][:, :], ALU.add).then_inc(s_acc, 1)
            return do

        def edge_scores(small, node_sc, H, gS, dS):
            with Stage() as se:
                G = [se.sb(f"G{j}", [P, H]) for j in range(U2)]
                ib, gate = se.sb("ib", [P, U2], I32), se.sb("gate", [1, 5])
                R = 4
                one = [se.sb(f"one{j}", [P, P]) for j in range(R)]
                oneT = [se.sb(f"oneT{j}", [P, P]) for j in range(R)]
                pT = [se.ps(f"pT{j}", [P, P]) for j in range(R)]
                pD = [se.ps(f"pD{j}", [P, H]) for j in range(R)]
                s_ib, s_gt, s_cons, s_one, s_t, s_tc, s_d, s_dc, s_z = (
                    se.sem(n) for n in ("s_ib", "s_gt", "s_cons", "s_one", "s_t", "s_tc", "s_d", "s_dc", "s_z"))
                s_g = [se.sem(f"s_g{j}") for j in range(U2)]
                with nc.Block() as block:
                    @block.gpsimd
                    def _(pool):
                        gather_rows(pool, U2, G, ib, gate, small, s_ib, s_g, s_gt)

                    @block.vector
                    def _(dve):
                        nc.vector.memset(gS[:, K:KP, :], 0.0).then_inc(s_z, 1)
                        nc.vector.memset(dS[:, K:KP, :], 0.0).then_inc(s_z, 1)

                        def mark(k, j):
                            freed(dve, s_t, k - R + 1)
                            nc.vector.tensor_scalar(one[j % R][:, :], iota[:, :], relS[:, ds(k, 1)], None, ALU.is_equal).then_inc(s_one, 1)

                        def keep(k, j):
                            gathered(dve, U2, s_g, k, j)
                            nc.vector.tensor_copy(tile(gS, k), G[j][:, :]).then_inc(s_cons, 1)
                        steps(dve, U2, (0, mark), (0, keep))

                    @block.tensor
                    def _(pe):
                        load, node = step_nodes(pe, U2)

                        def turn(k, j):
                            pe.wait_ge(s_one, k + 1)
                            freed(pe, s_tc, k - R + 1)
                            nc.tensor.transpose(pT[j % R][:, :], one[j % R][:, :], ident[:, :]).then_inc(s_t, 1)

                        def pick(k, j):
                            pe.wait_ge(s_tc, k + 1)
                            freed(pe, s_dc, k - R + 1)
                            nc.tensor.matmul(pD[j % R][:, :], oneT[j % R][:, :], tile(node_sc, node(k, j)), start=True, stop=True).then_inc(s_d, 1)
                        steps(pe, U2, (AHEAD, load), (0, turn), (LAG, pick))

                    @block.scalar
                    def _(act):
                        def turned(k, j):
                            act.wait_ge(s_t, k + 1)
                            freed(act, s_d, k - R + 1)
                            nc.scalar.activation(oneT[j % R][:, :], pT[j % R][:, :], ACT.Copy).then_inc(s_tc, 1)

                        def picked(k, j):
                            act.wait_ge(s_d, k + 1)
                            nc.scalar.activation(tile(dS, k), pD[j % R][:, :], ACT.Copy).then_inc(s_dc, 1)
                        steps(act, U2, (0, gather_indices(act, U2, U2 // 2, ib, s_ib, s_cons, s_gt)), (0, turned), (LAG + 1, picked))

        def edge_softmax(H, gS, dS, slope, zero_to, loops):
            with Stage() as st:
                W = KB * P
                brk = st.sb("brk", [P, W + 1])
                notfirst, notlast = st.sb("notfirst", [P, KB, P]), st.sb("notlast", [P, KB, P])
                starts = st.sb("starts", [P, KB, P]) if loops else None
                bk = st.sb("bk", [P, KB])
                rF, rL = st.sb("rF", [1, KP]), st.sb("rL", [1, KP])
                join = st.sb("join", [1, KP + 1])
                many, thrF, thrB = st.sb("many", [1, KP]), st.sb("thrF", [1, KP]), st.sb("thrB", [1, KP])
                g_h, d_h = st.sb("g_h", [P, KP]), st.sb("d_h", [P, KP])
                gK, dK = st.sb("gK", [P, W]), st.sb("dK", [P, W])
                e, f, m = st.sb("e", [P, W]), st.sb("f", [P, W]), st.sb("m", [P, W])
                u = st.sb("u", [P, W]) if loops else e
                rowA, rowB = st.sb("rowA", [1, KP]), st.sb("rowB", [1, KP])
                cin = st.sb("cin", [P, 2 * KB])
                col = st.sb("col", [P, 2, KB])
                pX = [st.ps(f"pX{q}", [P, 512]) for q in range(4)]
                pR = st.ps("pR", [P, P])
                pC = st.ps("pC", [P, 2 * KB])
                s_v, s_row, s_rc, s_col, s_f, s_hc, s_tr, s_kc = (st.sem(n) for n in ("s_v", "s_row", "s_rc", "s_col", "s_f", "s_hc", "s_tr", "s_kc"))
                s_th, s_rr, s_ci, s_cc, s_df, s_ex, s_bt, s_bc = (st.sem(n) for n in ("s_th", "s_rr", "s_ci", "s_cc", "s_df", "s_ex", "s_bt", "s_bc"))
                R1 = (KB - 4) * P
                dst2 = dstK[:, :, :].rearrange("k b i -> k (b i)")
                out2 = outK[:, :, :].rearrange("k b i -> k (b i)")

                def to_rows(src, sem):
                    for q in range(2):
                        for b in range(KB):
                            ins = nc.tensor.transpose(pX[2 * q + b // 4][0:1, (b % 4) * P:(b % 4 + 1) * P], src[:, q, b:b + 1], ident[:, :])
                    ins.then_inc(sem, 1)

                def from_row(row, at):
                    for b in range(KB):
                        ins = nc.tensor.transpose(pC[:, at + b:at + b + 1], row[0:1, b * P:(b + 1) * P], ident[0:1, 0:1])
                    return ins

                def row_out(q, row):
                    nc.vector.tensor_copy(row[0:1, 0:512], pX[2 * q][0:1, :])
                    return nc.vector.tensor_copy(row[0:1, 512:KP], pX[2 * q + 1][0:1, 0:R1])

                VN = 10 + (2 if zero_to is not None else 0) + (4 if loops else 0)
                with nc.Block() as block:
                    @block.vector
                    def _(dve):
                        flat = lambda t: t[:, :, :].rearrange("k b i -> k (b i)")
                        link = chain(dve, s_f)
                        link(nc.vector.tensor_tensor(brk[:, 1:W], dst2[:, 1:W], dst2[:, 0:W - 1], ALU.not_equal))
                        link(nc.vector.tensor_scalar(brk[:, 1:W], brk[:, 1:W], -BIG, None, ALU.mult))
                        link(nc.vector.memset(brk[:, 0:W + 1:P], -BIG))
                        for out_, at in ((notfirst, 0), (notlast, P - 1)):
                            link(nc.vector.tensor_tensor(out_[:, :, :], dstK[:, :, :], dstK[:, :, at:at + 1].broadcast_to([P, KB, P]), ALU.not_equal))
                            link(nc.vector.tensor_scalar(out_[:, :, :], out_[:, :, :], -BIG, None, ALU.mult))
                            nc.vector.tensor_copy(col[:, at // (P - 1), :], dstK[:, :, at]).then_inc(s_col, 1)
                        dve.wait_ge(s_row, 1)
                        row_out(0, rF)
                        link(row_out(1, rL))
                        link(nc.vector.tensor_tensor(join[0:1, 1:KP], rF[0:1, 1:KP], rL[0:1, 0:KP - 1], ALU.not_equal))
                        link(nc.vector.tensor_scalar(join[0:1, 1:KP], join[0:1, 1:KP], -BIG, None, ALU.mult))
                        link(nc.vector.memset(join[0:1, 0:KP + 1:KP], -BIG))
                        link(nc.vector.tensor_tensor(many[:, :], rF[:, :], rL[:, :], ALU.not_equal))
                        link(nc.vector.tensor_scalar(many[:, :], many[:, :], -BIG, None, ALU.mult))
                        link(nc.vector.tensor_tensor(thrF[:, :], many[:, :], join[:, 0:KP], ALU.add))
                        nc.vector.tensor_tensor(thrB[:, :], many[:, :], join[:, 1:KP + 1], ALU.add).then_inc(s_rc, 1)
                        dve.wait_ge(s_rc, 1)
                        if loops:
                            dve.wait_ge(s_col, 3)
                            link(nc.vector.tensor_scalar(flat(starts), brk[:, 0:W], 0.0, None, ALU.is_lt))
                            link(nc.vector.tensor_scalar(starts[:, :, 0], pC[:, 0:KB], 0.0, None, ALU.is_lt))

                        with dve.Fori(0, H) as h:
                            link = chain(dve, s_v, VN * h)
                            dve.wait_ge(s_kc, h + 1)
                            link(nc.vector.tensor_tensor(gK[:, :], gK[:, :], dK[:, :], ALU.add))
                            link(nc.vector.scalar_tensor_tensor(e[:, :], gK[:, :], slope, gK[:, :], ALU.mult, ALU.max))
                            if zero_to is not None:
                                link(nc.vector.tensor_scalar(gK[:, :], gK[:, :], 0.0, zero_to, ALU.is_equal, ALU.mult))
                                link(nc.vector.tensor_tensor(e[:, :], e[:, :], gK[:, :], ALU.add))
                            link(nc.vector.tensor_tensor(e[:, :], e[:, :], out2, ALU.add))
                            if loops:
                                link(nc.vector.tensor_scalar(dK[:, :], dK[:, :], 2.0, None, ALU.mult))
                                link(nc.vector.scalar_tensor_tensor(dK[:, :], dK[:, :], slope, dK[:, :], ALU.mult, ALU.max))
                                link(nc.vector.tensor_tensor(dK[:, :], dK[:, :], out2, ALU.add))
                                link(nc.vector.tensor_tensor(u[:, :], e[:, :], dK[:, :], ALU.max))
                            link(nc.vector.tensor_tensor_scan(f[:, :], brk[:, 0:W], u[:, :], -BIG, ALU.add, ALU.max))
                            link(nc.vector.tensor_tensor_scan(m[:, ::-1], brk[:, 1:W + 1][:, ::-1], f[:, ::-1], -BIG, ALU.add, ALU.max))
                            m3 = m[:, :].rearrange("k (b i) -> k b i", b=KB)
                            nc.vector.tensor_copy(col[:, 0, :], m3[:, :, P - 1])
                            nc.vector.tensor_copy(col[:, 1, :], m3[:, :, 0]).then_inc(s_th, 1)
                            dve.wait_ge(s_rr, h + 1)
                            row_out(0, rowA)
                            link(row_out(1, rowB))
                            nc.vector.tensor_tensor_scan(rF[:, :], thrF[:, :], rowA[:, :], -BIG, ALU.add, ALU.max)
                            link(nc.vector.tensor_tensor_scan(rL[:, ::-1], thrB[:, ::-1], rowB[:, ::-1], -BIG, ALU.add, ALU.max))
                            nc.vector.memset(rowA[0:1, 0:1], -BIG)
                            nc.vector.tensor_tensor(rowA[0:1, 1:KP], rF[0:1, 0:KP - 1], join[0:1, 1:KP], ALU.add)
                            nc.vector.memset(rowB[0:1, KP - 1:KP], -BIG)
                            nc.vector.tensor_tensor(rowB[0:1, 0:KP - 1], rL[0:1, 1:KP], join[0:1, 1:KP], ALU.add).then_inc(s_ci, 1)
                            dve.wait_ge(s_cc, h + 1)
                            link(nc.vector.tensor_copy(cin[:, :], pC[:, :]))
                            for q, away in enumerate((notfirst, notlast)):
                                for b in range(KB):
                                    ins = nc.vector.scalar_tensor_tensor(m3[:, b, :], away[:, b, :], cin[:, q * KB + b:q * KB + b + 1],
                                                                         m3[:, b, :], ALU.add, ALU.max)
                                link(ins)
                            ins = nc.vector.tensor_tensor(e[:, :], e[:, :], m[:, :], ALU.subtract)
                            if loops:
                                ins = nc.vector.tensor_tensor(dK[:, :], dK[:, :], m[:, :], ALU.subtract)
                            ins.then_inc(s_df, 1)
                            if loops:
                                dve.wait_ge(s_ex, h + 1)
                                nc.vector.tensor_tensor(dK[:, :], dK[:, :], flat(starts), ALU.mult).then_inc(s_df, 1)

                            dve.wait_ge(s_bt, h + 1)
                            for q, t in enumerate((gS, dS) if loops else (gS,)):
                                nc.vector.tensor_scalar(t[:, 0:512, ds(h, 1)].rearrange("p k a -> p (k a)"), pX[2 * q][:, :], 1.0, None, ALU.mult)
                                ins = nc.vector.tensor_scalar(t[:, 512:KP, ds(h, 1)].rearrange("p k a -> p (k a)"), pX[2 * q + 1][:, 0:R1], 1.0, None, ALU.mult)
                            ins.then_inc(s_bc, 1)

                    DF = 2 if loops else 1

                    @block.scalar
                    def _(act):
                        with act.Fori(0, H) as h:
                            nc.scalar.activation(g_h[:, :], gS[:, :, ds(h, 1)].rearrange("p k a -> p (k a)"), ACT.Copy)
                            nc.scalar.activation(d_h[:, :], dS[:, :, ds(h, 1)].rearrange("p k a -> p (k a)"), ACT.Copy).then_inc(s_hc, 1)
                            act.wait_ge(s_tr, h + 1)
                            nc.scalar.activation(gK[:, 0:512], pX[0][:, :], ACT.Copy)
                            nc.scalar.activation(gK[:, 512:W], pX[1][:, 0:R1], ACT.Copy)
                            nc.scalar.activation(dK[:, 0:512], pX[2][:, :], ACT.Copy)
                            nc.scalar.activation(dK[:, 512:W], pX[3][:, 0:R1], ACT.Copy).then_inc(s_kc, 1)
                            act.wait_ge(s_df, DF * h + 1)
                            ins = nc.scalar.activation(e[:, :], e[:, :], ACT.Exp)
                            if loops:
                                ins = nc.scalar.activation(dK[:, :], dK[:, :], ACT.Exp)
                            ins.then_inc(s_ex, 1)
                            act.wait_ge(s_bc, h + 1)

                    @block.tensor
                    def _(pe):
                        pe.wait_ge(s_col, 2)
                        to_rows(col, s_row)
                        pe.wait_ge(s_rc, 1)
                        if loops:
                            from_row(join, 0).then_inc(s_col, 1)

                        def turn(src, q):
                            for b in range(KB):
                                ins = nc.tensor.transpose(pX[2 * q + b // 4][:, (b % 4) * P:(b % 4 + 1) * P], src[:, b * P:(b + 1) * P], ident[:, :])
                            return ins

                        with pe.Fori(0, H) as h:
                            pe.wait_ge(s_hc, h + 1)
                            turn(g_h, 0)
                            turn(d_h, 1).then_inc(s_tr, 1)
                            pe.wait_ge(s_th, h + 1)
                            to_rows(col, s_rr)
                            pe.wait_ge(s_ci, h + 1)
                            nc.tensor.transpose(pR[:, 0:P], ident[:, :], ident[:, :])
                            from_row(rowA, 0)
                            from_row(rowB, KB).then_inc(s_cc, 1)
                            if loops:
                                pe.wait_ge(s_df, DF * h + 2)
                                turn(e, 0)
                                turn(dK, 1).then_inc(s_bt, 1)
                            else:
                                pe.wait_ge(s_ex, h + 1)
                                turn(e, 0).then_inc(s_bt, 1)

        def edge_sum(u, rows, acc, W, heads, gS, dS):
            with Stage() as se:
                G = [se.sb(f"G{j}", [P, D]) for j in range(u)]
                ib, gate = se.sb("ib", [P, u], I32), se.sb("gate", [1, 5])
                R = 4
                one = [se.sb(f"one{j}", [P, P]) for j in range(R)]
                msg = [se.sb(f"msg{j}", [P, W]) for j in range(R)] if heads else None
                pM = [se.ps(f"pM{j}", [P, W]) for j in range(R)]
                s_ib, s_gt, s_one, s_ex, s_m, s_acc = (se.sem(n) for n in ("s_ib", "s_gt", "s_one", "s_ex", "s_m", "s_acc"))
                s_g = [se.sem(f"s_g{j}") for j in range(u)]
                s_cons = s_one if heads else s_m
                with nc.Block() as block:
                    @block.gpsimd
                    def _(pool):
                        gather_rows(pool, u, G, ib, gate, rows, s_ib, s_g, s_gt)

                    @block.scalar
                    def _(act):
                        def weights(k, j):
                            freed(act, s_m, k - R + 1)
                            ins = nc.scalar.activation(msg[j % R][:, D:D + heads], tile(gS, k), ACT.Copy)
                            if dS is not None:
                                ins = nc.scalar.activation(msg[j % R][:, D + heads:W], tile(dS, k), ACT.Copy)
                            ins.then_inc(s_ex, 1)
                        steps(act, u, (0, gather_indices(act, u, u // 2, ib, s_ib, s_cons, s_gt)), *([(0, weights)] if heads else []))

                    @block.vector
                    def _(dve):
                        load, node = step_nodes(dve, u)

                        def mark(k, j):
                            freed(dve, s_m, k - R + 1)
                            if heads:
                                nc.vector.tensor_scalar(one[j % R][:, :], iota[:, :], relS[:, ds(k, 1)], None, ALU.is_equal)
                                gathered(dve, u, s_g, k, j)
                                nc.vector.tensor_tensor(msg[j % R][:, 0:D].rearrange("p (h c) -> p h c", h=heads),
                                                        G[j][:, :].rearrange("p (h c) -> p h c", h=heads),
                                                        gS[:, ds(k, 1), :].rearrange("p a h -> p h a").broadcast_to([P, heads, D // heads]),
                                                        ALU.mult).then_inc(s_one, 1)
                            else:
                                nc.vector.tensor_scalar(one[j % R][:, :], iota[:, :], relS[:, ds(k, 1)], wS[:, ds(k, 1)],
                                                        ALU.is_equal, ALU.mult).then_inc(s_one, 1)
                        steps(dve, u, (AHEAD, load), (0, mark), (LAG, adder(dve, acc, pM, R, s_m, s_acc, node)))

                    @block.tensor
                    def _(pe):
                        def scatter(k, j):
                            pe.wait_ge(s_one, k + 1)
                            if heads:
                                pe.wait_ge(s_ex, k + 1)
                            else:
                                gathered(pe, u, s_g, k, j)
                            freed(pe, s_acc, k - R + 1)
                            nc.tensor.matmul(pM[j % R][:, :], one[j % R][:, :], (msg[j % R] if heads else G[j])[:, :],
                                             start=True, stop=True).then_inc(s_m, 1)
                        steps(pe, u, (0, scatter))

        def batch_norm(acc, gain, bias, rsg, brow):
            with Stage() as st:
                lane = st.sb("lane", [P, 1])
                live = st.sb("live", [P, 1])
                part = st.sb("part", [P, D])
                mean, var, vt = st.sb("mean", [P, D]), st.sb("var", [P, D]), st.sb("vt", [P, D])
                sq = [st.sb(f"sq{j}", [P, D]) for j in range(2)]
                grow = st.sb("grow", [P, D])
                pS = st.ps("pS", [P, D])
                s_l, s_b, s_c, s_p, s_s, s_rt, s_q, s_a = (st.sem(n) for n in ("s_l", "s_b", "s_c", "s_p", "s_s", "s_rt", "s_q", "s_a"))
                nodes = lambda t: t[:, 0:FULL + 1, 0:D]
                with nc.Block() as block:
                    @block.gpsimd
                    def _(pool):
                        pool.iota(lane[:, :], [[0, 1]], base=0, channel_multiplier=1, allow_small_or_imprecise_dtypes=True).then_inc(s_l, 1)

                    @block.sync
                    def _(sp):
                        sp.dma_start(grow[:, :], gain.rearrange("(a n) -> a n", a=1).broadcast_to([P, D])).then_inc(s_b, 16)
                        sp.dma_start(brow[:, :], bias.rearrange("(a n) -> a n", a=1).broadcast_to([P, D])).then_inc(s_b, 16)

                    @block.vector
                    def _(dve):
                        link = chain(dve, s_c)
                        dve.wait_ge(s_l, 1)
                        link(nc.vector.tensor_scalar(live[:, :], lane[:, :], float(REST), None, ALU.is_lt))
                        link(nc.vector.tensor_scalar(acc[:, FULL, 0:D], acc[:, FULL, 0:D], live[:, :], None, ALU.mult))
                        nc.vector.tensor_reduce(part[:, :], nodes(acc).rearrange("p t c -> p c t"), AX.X, ALU.add).then_inc(s_p, 1)
                        dve.wait_ge(s_s, 1)
                        link(nc.vector.tensor_scalar(mean[:, :], pS[:, :], 1 / N, None, ALU.mult))
                        link(nc.vector.tensor_tensor(nodes(acc), nodes(acc), mean[:, :].unsqueeze(1).broadcast_to([P, FULL + 1, D]), ALU.subtract))
                        link(nc.vector.tensor_scalar(acc[:, FULL, 0:D], acc[:, FULL, 0:D], live[:, :], None, ALU.mult))
                        nc.vector.memset(part[:, :], 0.0).then_inc(s_q, 1)

                        def add_square(n, j):
                            dve.wait_ge(s_a, n + 1)
                            dve.wait_ge(s_q, n + 1)
                            nc.vector.tensor_tensor(part[:, :], part[:, :], sq[j][:, :], ALU.add).then_inc(s_q, 1)
                        with dve.Fori(0, FULL // 2) as i:
                            add_square(2 * i, 0)
                            add_square(2 * i + 1, 1)
                        add_square(FULL, 0)
                        dve.wait_ge(s_s, 2)
                        nc.vector.tensor_scalar(var[:, :], pS[:, :], 1 / N, EPS, ALU.mult, ALU.add).then_inc(s_rt, 1)
                        dve.wait_ge(s_rt, 2)
                        link(nc.vector.reciprocal(rsg[:, :], rsg[:, :]))
                        newton_rsqrt(link, rsg[:, :], var[:, :], vt[:, :])
                        dve.wait_ge(s_b, 32)
                        link(nc.vector.tensor_tensor(rsg[:, :], rsg[:, :], grow[:, :], ALU.mult))

                    @block.scalar
                    def _(act):
                        act.wait_ge(s_q, 1)

                        def square(n, j, early=False):
                            if not early:
                                act.wait_ge(s_q, n)
                            nc.scalar.activation(sq[j][:, :], tile(acc[:, :, 0:D], n), ACT.Square).then_inc(s_a, 1)
                        square(0, 0, True)
                        square(1, 1, True)
                        with act.Fori(1, FULL // 2) as i:
                            square(2 * i, 0)
                            square(2 * i + 1, 1)
                        square(FULL, 0)
                        act.wait_ge(s_rt, 1)
                        nc.scalar.activation(rsg[:, :], var[:, :], ACT.Sqrt).then_inc(s_rt, 1)

                    @block.tensor
                    def _(pe):
                        for sem, value in ((s_p, 1), (s_q, FULL + 2)):
                            pe.wait_ge(sem, value)
                            nc.tensor.matmul(pS[:, :], ones[:, :], part[:, :], start=True, stop=True).then_inc(s_s, 1)

        def newton_rsqrt(link, r, v, t):
            link(nc.vector.tensor_tensor(t, r, r, ALU.mult))
            link(nc.vector.tensor_tensor(t, t, v, ALU.mult))
            link(nc.vector.tensor_scalar(t, t, -0.5, 1.5, ALU.mult, ALU.add))
            link(nc.vector.tensor_tensor(r, r, t, ALU.mult))

        def tile(t, n):
            return t[:, ds(n, 1), :].rearrange("p a c -> p (a c)")

        def layernorm_stats(x_sb, rstd, shift):
            with Stage() as st:
                bn = st.sb("bn", [P, NT, 6])
                mean, dif, ve = st.sb("mean", [P, NT]), st.sb("dif", [P, NT]), st.sb("ve", [P, NT])
                s_bn, s_ve, s_rt, s_ch = (st.sem(n) for n in ("s_bn", "s_ve", "s_rt", "s_ch"))
                with nc.Block() as block:
                    @block.vector
                    def _(dve):
                        with dve.Fori(0, NT // 2) as i:
                            for j in range(2):
                                ins = nc.vector.bn_stats(tile(bn, 2 * i + j), tile(x_sb, 2 * i + j))
                            ins.then_inc(s_bn, 1)
                        dve.wait_ge(s_bn, NT // 2)
                        link = chain(dve, s_ch)
                        link(nc.vector.tensor_tensor(mean[:, :], bn[:, :, 1], bn[:, :, 4], ALU.add))
                        link(nc.vector.tensor_tensor(dif[:, :], bn[:, :, 1], bn[:, :, 4], ALU.subtract))
                        link(nc.vector.tensor_tensor(ve[:, :], bn[:, :, 2], bn[:, :, 5], ALU.add))
                        link(nc.vector.tensor_tensor(dif[:, :], dif[:, :], dif[:, :], ALU.mult))
                        link(nc.vector.tensor_scalar(ve[:, :], ve[:, :], 1 / D, EPS, ALU.mult, ALU.add))
                        nc.vector.scalar_tensor_tensor(ve[:, :], dif[:, :], 0.25, ve[:, :], ALU.mult, ALU.add).then_inc(s_ve, 1)
                        dve.wait_ge(s_rt, 1)
                        link(nc.vector.reciprocal(rstd[:, :], rstd[:, :]))
                        newton_rsqrt(link, rstd[:, :], ve[:, :], dif[:, :])
                        link(nc.vector.scalar_tensor_tensor(shift[:, :], mean[:, :], -0.5, rstd[:, :], ALU.mult, ALU.mult))

                    @block.scalar
                    def _(act):
                        act.wait_ge(s_ve, 1)
                        nc.scalar.activation(rstd[:, :], ve[:, :], ACT.Sqrt).then_inc(s_rt, 1)

        def node_stage(layer, x_sb, rstd, shift, wide, load, biases, act_end, dve_end, store, ready=None):
            with Stage() as st:
                y = [st.sb(f"y{j}", [P, D]) for j in range(2)]
                yT = [st.sb(f"yT{j}", [P, D]) for j in range(2)]
                ready = ready or {}
                w_sb = [ready[q] if q in ready else st.sb(f"w_sb{q}", [P, 2, w]) for q, w in enumerate(wide)]
                b_sb = [st.sb(f"b_sb{q}", [1, w]) if biases[q] else None for q, w in enumerate(wide)]
                pT = [st.ps(f"pT{j}", [P, D]) for j in range(2)]
                pO = [[st.ps(f"pO{j}_{q}", [P, w]) for q, w in enumerate(wide)] for j in range(2)]
                row = [st.sb(f"row{j}", [P, D]) for j in range(2)]
                aux = [st.sb(f"aux{j}", [P, D]) for j in range(2)]
                s_w, s_y, s_t, s_yt, s_o, s_ae, s_de = (st.sem(n) for n in ("s_w", "s_y", "s_t", "s_yt", "s_o", "s_ae", "s_de"))
                s_st = [st.sem(f"s_st{j}") for j in range(2)]
                loads = []
                n_st = len(store)

                with nc.Block() as block:
                    @block.sync
                    def _(sp):
                        for dst, src in load(w_sb, b_sb):
                            loads.append(sp.dma_start(dst, src).then_inc(s_w, 16))

                        def out_rows(n, j):
                            sp.wait_ge(s_ae, n + 1)
                            sp.wait_ge(s_de, n + 1)
                            for dst, src in store:
                                sp.dma_start(dst(n), src(row[j], aux[j])).then_inc(s_st[j], 16)
                        tiles(sp, (0, out_rows))
                        for j in range(2):
                            sp.wait_ge(s_st[j], 16 * n_st * (NT // 2))

                    @block.scalar
                    def _(act):
                        def norm(n, j):
                            freed(act, s_t, n - 1)
                            nc.scalar.activation(y[j][:, :], tile(x_sb, n), ACT.Relu, bias=shift[:, ds(n, 1)],
                                                 scale=rstd[:, ds(n, 1)]).then_inc(s_y, 1)

                        def end(n, j):
                            act.wait_ge(s_o, n + 1)
                            freed(act, s_st[j], 8 * n_st * (n - j))
                            act_end(act, n, j, pO[j], row[j], aux[j]).then_inc(s_ae, 1)
                        tiles(act, (0, norm), (2, end))

                    @block.vector
                    def _(dve):
                        def turned(n, j):
                            dve.wait_ge(s_t, n + 1)
                            freed(dve, s_o, n - 1)
                            nc.vector.tensor_copy(yT[j][:, :], pT[j][:, :]).then_inc(s_yt, 1)

                        def end(n, j):
                            dve.wait_ge(s_o, n + 1)
                            freed(dve, s_st[j], 8 * n_st * (n - j))
                            dve_end(dve, n, j, pO[j], row[j], aux[j], s_ae).then_inc(s_de, 1)
                        tiles(dve, (0, turned), (2, end))

                    @block.tensor
                    def _(pe):
                        pe.wait_ge(s_w, 16 * len(loads))

                        def turn(n, j):
                            pe.wait_ge(s_y, n + 1)
                            freed(pe, s_yt, n - 1)
                            for c in range(2):
                                ins = nc.tensor.transpose(pT[j][:, c * P:(c + 1) * P], y[j][:, c * P:(c + 1) * P], ident[:, :])
                            ins.then_inc(s_t, 1)

                        def multiply(n, j):
                            pe.wait_ge(s_yt, n + 1)
                            freed(pe, s_ae, n - 1)
                            freed(pe, s_de, n - 1)
                            for q, w in enumerate(wide):
                                if biases[q]:
                                    nc.tensor.matmul(pO[j][q][:, :], ones[0:1, :], b_sb[q][0:1, :], start=True, stop=False)
                                for c in range(2):
                                    ins = nc.tensor.matmul(pO[j][q][:, :], yT[j][:, c * P:(c + 1) * P], w_sb[q][:, c, :],
                                                           start=(c == 0 and not biases[q]), stop=(c == 1))
                            ins.then_inc(s_o, 1)
                        tiles(pe, (0, turn), (1, multiply))

        def load_nodes(x_sb, src, rows):
            with Stage() as st:
                s_z, s_x = st.sem("s_z"), st.sem("s_x")
                with nc.Block() as block:
                    @block.vector
                    def _(dve):
                        nc.vector.memset(x_sb[:, FULL:NT, :], 0.0).then_inc(s_z, 1)

                    @block.sync
                    def _(sp):
                        sp.dma_start(x_sb[:, 0:FULL, :], src[0:FULL * P, :].rearrange("(t p) c -> p t c", p=P)).then_inc(s_x, 16)
                        sp.wait_ge(s_z, 1)
                        sp.dma_start(x_sb[0:REST, FULL, :], src[FULL * P:N, :]).then_inc(s_x, 16)
                        sp.wait_ge(s_x, 32)

        with Stage() as st0:
            a4S = st0.sb("a4S", [P, 4, KP])
            a10S = st0.sb("a10S", [P, NBAS, KP])
            with Stage() as st:
                zf = st.sb("zf", [P, 2 * D])
                padi = st.sb("padi", [1, 2, P], I32)
                frow_i = st.sb("frow_i", [1, ET], I32)
                trow_i = st.sb("trow_i", [1, ET], I32)
                frow = st.sb("frow", [1, ET])
                trow = st.sb("trow", [1, ET])
                kcol_i = st.sb("kcol_i", [P, KB], I32)
                kcol = st.sb("kcol", [P, KB])
                hit = st.sb("hit", [P, ET - 1])
                tk = st.sb("tk", [P, KB])
                tki = st.sb("tki", [P, KB], I32)
                nk = st.sb("nk", [P, KB])
                nkc = st.sb("nkc", [P, KB])
                nki = st.sb("nki", [P, KB], I32)
                base = st.sb("base", [P, KB])
                relK = st.sb("relK", [P, KB, P])
                m1 = st.sb("m1", [P, KB, P])
                gt = st.sb("gt", [MUL, 2, 3, 3 * MUL])
                nodeF = st.sb("nodeF", [P, KP])
                gdst = st.sb("gdst", [P, KB, P], I32)
                gsrc = st.sb("gsrc", [P, KB, P], I32)
                gsf = st.sb("gsf", [P, KB, P])
                gw = st.sb("gw", [P, KB, P])
                g4 = st.sb("g4", [P, 4 * P])
                g10 = st.sb("g10", [P, NBAS * P])
                oh4 = st.sb("oh4", [P, 2, 4, P], BF16)
                deg = st.sb("deg", [P, NT])
                degt = st.sb("degt", [P, NT])
                zb = st.sb("zb", [P, P], BF16)
                nh4 = st.sb("nh4", [P, 2, 4, NT], BF16)
                pS = [st.ps(f"pS{n}", [P, (ET - 1) // 2]) for n in range(2)]
                pT = [st.ps(f"pT{n}", [P, P]) for n in range(4)]
                pC = st.ps("pC", [P, NT])
                s_const, s_zero, s_pad, s_first, s_row = (st.sem(n) for n in ("s_const", "s_zero", "s_pad", "s_first", "s_row"))
                s_ts, s_v, s_tk, s_nd, s_ndd, s_ndr = (st.sem(n) for n in ("s_ts", "s_v", "s_tk", "s_nd", "s_ndd", "s_ndr"))
                s_w1, s_w2, s_gd, s_gs, s_gw = (st.sem(n) for n in ("s_w1", "s_w2", "s_gd", "s_gs", "s_gw"))
                s_g4, s_g10, s_kf, s_tr, s_cp = (st.sem(n) for n in ("s_g4", "s_g10", "s_kf", "s_tr", "s_cp"))
                s_oh, s_cn, s_pc, s_deg = (st.sem(n) for n in ("s_oh", "s_cn", "s_pc", "s_deg"))
                PADS = E // 50

                with nc.Block() as block:
                    @block.sync
                    def _(sp):
                        for dst, src, w in ((dst_pad, a["dst"], 1), (src_pad, a["src"], 1), (w_pad, a["edge_weight"], 1),
                                            (a4_pad, a["edge_attr_4"].rearrange("e c -> (e c)"), 4),
                                            (a10_pad, a["edge_attr_10"].rearrange("e c -> (e c)"), NBAS)):
                            sp.dma_start(dst[0:E * w].rearrange("(a b) -> a b", a=50 * w),
                                         src.rearrange("(a b) -> a b", a=50 * w)).then_inc(s_pad, 16)
                        sp.wait_ge(s_zero, 3)
                        sp.dma_start(dst_pad[E:EPAD].rearrange("(a b) -> a b", a=1), padi[0:1, 0, 0:EPAD - E]).then_inc(s_pad, 16)
                        sp.dma_start(src_pad[E:EPAD].rearrange("(a b) -> a b", a=1), padi[0:1, 1, 0:EPAD - E]).then_inc(s_pad, 16)
                        sp.dma_start(w_pad[E:EPAD].rearrange("(a b) -> a b", a=1), zf[0:1, 0:EPAD - E]).then_inc(s_pad, 16)
                        sp.dma_start(a4_pad[4 * E:4 * EPAD].rearrange("(a b) -> a b", a=4), zf[0:4, 0:EPAD - E]).then_inc(s_pad, 16)
                        sp.dma_start(a10_pad[NBAS * E:NBAS * EPAD].rearrange("(a b) -> a b", a=NBAS), zf[0:NBAS, 0:EPAD - E]).then_inc(s_pad, 16)
                        sp.wait_ge(s_pad, 160)
                        with nc.allow_non_contiguous_dma(reason="one dst of each edge tile"):
                            sp.dma_start(frow_i[0:1, :], dst_pad.rearrange("(a t p) -> a t p", a=1, p=P)[:, :, 0]).then_inc(s_first, 16)
                        sp.wait_ge(s_nd, 1)
                        with nc.allow_non_contiguous_dma(reason="896 step entries"):
                            sp.dma_start(node_i.rearrange("(b p) -> p b", p=P), nki[:, :]).then_inc(s_ndd, 16)
                            sp.dma_start(node_f.rearrange("(b p) -> p b", p=P), nkc[:, :]).then_inc(s_ndd, 16)
                        sp.wait_ge(s_ndd, 32)
                        sp.wait_ge(s_zero, 7)
                        sp.dma_start(nodeR[0:1, LAG:KP + LAG], node_i.rearrange("(a k) -> a k", a=1)).then_inc(s_ndr, 16)
                        sp.dma_start(nodeF[:, :], node_f.rearrange("(a k) -> a k", a=1).broadcast_to([P, KP])).then_inc(s_ndr, 16)
                        for r in range(2):
                            sp.dma_start(wbig[r * P:(r + 1) * P, :], zf[:, :]).then_inc(s_w1, 16)
                        sp.wait_ge(s_zero, 4)
                        for f, (w0, w1) in enumerate((("L0_gnn_W_li0", "L0_gnn_W_li1"), ("L0_gnn_W_lm0", "L0_gnn_W_lm1"))):
                            for m in range(3):
                                sp.dma_start(gt[:, f, m, m * MUL:(m + 1) * MUL], a[w1]).then_inc(s_w1, 16)
                        sp.wait_ge(s_w1, 128)
                        for f, w0 in enumerate(("L0_gnn_W_li0", "L0_gnn_W_lm0")):
                            sp.dma_start(wbig[0:MUL, f * D:f * D + MUL], a[w0]).then_inc(s_w2, 16)
                            sp.dma_start(wbig[MUL:D, f * D + MUL:(f + 1) * D].rearrange("(u m) c -> u m c", m=3),
                                         gt[:, f, :, :]).then_inc(s_w2, 16)
                        sp.wait_ge(s_w2, 64)
                        sp.wait_ge(s_ndr, 32)

                    @block.gpsimd
                    def _(pool):
                        pool.iota(kcol_i[:, :], [[P, KB]], base=0, channel_multiplier=1).then_inc(s_const, 1)
                        pool.iota(trow_i[:, :], [[1, ET]], base=0, channel_multiplier=0).then_inc(s_const, 1)
                        pool.iota(iota[:, :], [[1, P]], base=0, channel_multiplier=0,
                                  allow_small_or_imprecise_dtypes=True).then_inc(s_const, 1)
                        pool.memset(ident[:, :], 0.0).then_inc(s_const, 1)
                        pool.wait_ge(s_const, 4)
                        pool.affine_select(out=ident[:, :], in_=ident[:, :], compare_op=ALU.not_equal, fill=1.0, base=0,
                                           pattern=[[-1, P]], channel_multiplier=1).then_inc(s_const, 1)
                        pool.wait_ge(s_tk, 1)
                        for b in range(KB):
                            at = bass.IndirectOffsetOnAxis(ap=tki[:, b:b + 1], axis=0)
                            rows = lambda t: t.rearrange("(t q) -> t q", t=ET)
                            pool.indirect_dma_start(gdst[:, b, :], None, rows(dst_pad), at).then_inc(s_gd, 16)
                            pool.indirect_dma_start(gsrc[:, b, :], None, rows(src_pad), at).then_inc(s_gs, 16)
                            pool.indirect_dma_start(gw[:, b, :], None, rows(w_pad), at).then_inc(s_gw, 16)
                        for b in range(KB):
                            if b:
                                pool.wait_ge(s_tr, 3 * KB + 14 * (b - 1) + 4)
                            pool.indirect_dma_start(g4[:, :], None, rows(a4_pad), bass.IndirectOffsetOnAxis(ap=tki[:, b:b + 1], axis=0)).then_inc(s_g4, 16)
                            if b:
                                pool.wait_ge(s_tr, 3 * KB + 14 * b)
                            pool.indirect_dma_start(g10[:, :], None, rows(a10_pad), bass.IndirectOffsetOnAxis(ap=tki[:, b:b + 1], axis=0)).then_inc(s_g10, 16)

                    @block.vector
                    def _(dve):
                        nc.vector.memset(zf[:, :], 0.0).then_inc(s_zero, 1)
                        nc.vector.memset(padi[0:1, 0, :], NOWHERE).then_inc(s_zero, 1)
                        nc.vector.memset(padi[0:1, 1, :], 0).then_inc(s_zero, 1)
                        nc.vector.memset(gt[:, :, :, :], 0.0).then_inc(s_zero, 1)
                        nc.vector.memset(ones[:, :], 1.0).then_inc(s_zero, 1)
                        nc.vector.memset(zb[:, :], 0.0).then_inc(s_zero, 1)
                        nc.vector.memset(nodeR[0:1, 0:LAG], 0).then_inc(s_zero, 1)
                        link = chain(dve, s_v)
                        dve.wait_ge(s_const, 5)
                        dve.wait_ge(s_first, 16)
                        link(nc.vector.tensor_scalar(frow_i[:, :], frow_i[:, :], 7, None, ALU.arith_shift_right))
                        link(nc.vector.tensor_copy(frow[:, :], frow_i[:, :]))
                        link(nc.vector.tensor_copy(trow[:, :], trow_i[:, :]))
                        link(nc.vector.tensor_tensor(frow[:, :], frow[:, :], trow[:, :], ALU.add))
                        nc.vector.tensor_copy(kcol[:, :], kcol_i[:, :]).then_inc(s_row, 1)
                        dve.wait_ge(s_row, 1)
                        dve.wait_ge(s_ts, 2)
                        for b in range(KB):
                            for n in range(2):
                                link(nc.vector.tensor_scalar(hit[:, n * (ET // 2):(n + 1) * (ET // 2)], pS[n][:, :],
                                                             kcol[:, b:b + 1], None, ALU.is_le))
                            link(nc.vector.tensor_reduce(tk[:, b:b + 1], hit[:, :], AX.X, ALU.add))
                        link(nc.vector.tensor_copy(tki[:, :], tk[:, :]))
                        nc.vector.tensor_tensor(nk[:, :], kcol[:, :], tk[:, :], ALU.subtract).then_inc(s_tk, 1)
                        dve.wait_ge(s_tk, 1)
                        link(nc.vector.tensor_scalar(nkc[:, :], nk[:, :], float(NT - 1), None, ALU.min))
                        link(nc.vector.tensor_scalar(base[:, :], nk[:, :], float(-P), None, ALU.mult))
                        nc.vector.tensor_copy(nki[:, :], nkc[:, :]).then_inc(s_nd, 1)
                        dve.wait_ge(s_gd, 16 * KB)
                        link(nc.vector.tensor_copy(dstK[:, :, :], gdst[:, :, :]))
                        for b in range(KB):
                            last = nc.vector.tensor_scalar(relK[:, b, :], dstK[:, b, :], base[:, b:b + 1], None, ALU.add)
                        link(last)
                        dve.wait_ge(s_gs, 16 * KB)
                        dve.wait_ge(s_gw, 16 * KB)
                        nc.vector.tensor_copy(gsf[:, :, :], gsrc[:, :, :]).then_inc(s_kf, 1)
                        link(nc.vector.tensor_scalar(m1[:, :, :], relK[:, :, :], 0.0, -BIG, ALU.is_lt, ALU.mult))
                        link(nc.vector.tensor_scalar(outK[:, :, :], relK[:, :, :], float(P), -BIG, ALU.is_ge, ALU.mult))
                        link(nc.vector.tensor_tensor(outK[:, :, :], outK[:, :, :], m1[:, :, :], ALU.add))
                        dve.wait_ge(s_ndr, 32)
                        dve.wait_ge(s_cp, 3 * KB)
                        with dve.Fori(0, K // 8) as i:
                            for h in range(2):
                                dve.wait_ge(s_cn, 2 * i + h + 1)
                                nc.vector.tensor_tensor(oh4[:, h, :, :], iota[:, :].unsqueeze(1).broadcast_to([P, 4, P]),
                                                        relS[:, ds(8 * i + 4 * h, 4)].unsqueeze(2).broadcast_to([P, 4, P]), ALU.is_equal)
                                nc.vector.tensor_tensor(nh4[:, h, :, :], iota[:, 0:NT].unsqueeze(1).broadcast_to([P, 4, NT]),
                                                        nodeF[:, ds(8 * i + 4 * h, 4)].unsqueeze(2).broadcast_to([P, 4, NT]),
                                                        ALU.is_equal).then_inc(s_oh, 1)
                        dve.wait_ge(s_pc, 1)
                        nc.vector.tensor_copy(cnt[:, :], pC[:, :]).then_inc(s_pc, 1)
                        dve.wait_ge(s_pc, 2)
                        nc.vector.tensor_scalar(deg[:, :], cnt[:, :], 1.0, None, ALU.max).then_inc(s_deg, 1)
                        dve.wait_ge(s_deg, 2)
                        link(nc.vector.reciprocal(dis[:, :], dis[:, :]))
                        newton_rsqrt(link, dis[:, :], deg[:, :], degt[:, :])

                    @block.tensor
                    def _(pe):
                        pe.wait_ge(s_zero, 6)
                        pe.wait_ge(s_row, 1)
                        for n in range(2):
                            nc.tensor.matmul(pS[n][:, :], ones[0:1, :], frow[0:1, 1 + n * (ET // 2):1 + (n + 1) * (ET // 2)],
                                             start=True, stop=True).then_inc(s_ts, 1)
                        pe.wait_ge(s_kf, 1)
                        count = 0

                        def turn(src):
                            nonlocal count
                            if count >= 4:
                                pe.wait_ge(s_cp, count - 3)
                            nc.tensor.transpose(pT[count % 4][:, :], src, ident[:, :]).then_inc(s_tr, 1)
                            count += 1

                        for g in (relK, gsf, gw):
                            for b in range(KB):
                                turn(g[:, b, :])
                        for b in range(KB):
                            pe.wait_ge(s_g4, 16 * b + 16)
                            for c in range(4):
                                turn(g4[:, :].rearrange("k (e c) -> k c e", c=4)[:, c, :])
                            pe.wait_ge(s_g10, 16 * b + 16)
                            for c in range(NBAS):
                                turn(g10[:, :].rearrange("k (e c) -> k c e", c=NBAS)[:, c, :])
                        nc.tensor.matmul(pC[:, :], zb[:, :], zb[:, 0:NT], start=True, stop=False).then_inc(s_cn, 2)
                        with pe.Fori(0, K // 8) as i:
                            for h in range(2):
                                pe.wait_ge(s_oh, 2 * i + h + 1)
                                for q in range(4):
                                    ins = nc.tensor.matmul(pC[:, :], oh4[:, h, q, :], nh4[:, h, q, :], start=False, stop=False)
                                ins.then_inc(s_cn, 1)
                        nc.tensor.matmul(pC[:, :], zb[:, :], zb[:, 0:NT], start=False, stop=True).then_inc(s_pc, 1)

                    @block.scalar
                    def _(act):
                        count = 0
                        for dst in (relS, srcI, wS):
                            for b in range(KB):
                                act.wait_ge(s_tr, count + 1)
                                nc.scalar.activation(dst[:, b * P:(b + 1) * P], pT[count % 4][:, :], ACT.Copy).then_inc(s_cp, 1)
                                count += 1
                        for b in range(KB):
                            for dst, w in ((a4S, 4), (a10S, NBAS)):
                                for c in range(w):
                                    act.wait_ge(s_tr, count + 1)
                                    nc.scalar.activation(dst[:, c, b * P:(b + 1) * P], pT[count % 4][:, :], ACT.Copy).then_inc(s_cp, 1)
                                    count += 1
                        act.wait_ge(s_deg, 1)
                        nc.scalar.activation(dis[:, :], deg[:, :], ACT.Sqrt).then_inc(s_deg, 1)
            attr = st0.sb("attr", [P, NT])
            sc_f = st0.sb("sc_f", [P, NT])
            sc_m = st0.sb("sc_m", [P, NT])
            sc_o = st0.sb("sc_o", [P, NT])
            with Stage() as st:
                s_a0, s_a, s_c = st.sem("s_a0"), st.sem("s_a"), st.sem("s_c")
                with nc.Block() as block:
                    @block.sync
                    def _(sp):
                        sp.wait_ge(s_a0, 1)
                        vec = a["node_vec1"].rearrange("n o -> (n o)")
                        with nc.allow_non_contiguous_dma(reason="6250 attributes, node on partition"):
                            sp.dma_start(attr[:, 0:FULL], vec[0:FULL * P].rearrange("(t p) -> p t", p=P)).then_inc(s_a, 16)
                            sp.dma_start(attr[0:REST, FULL:FULL + 1], vec[FULL * P:N].rearrange("(p o) -> p o", o=1)).then_inc(s_a, 16)

                    @block.vector
                    def _(dve):
                        nc.vector.memset(attr[:, :], 0.0).then_inc(s_a0, 1)
                        dve.wait_ge(s_a, 32)
                        link = chain(dve, s_c)
                        link(nc.vector.tensor_tensor(sc_f[:, :], attr[:, :], dis[:, :], ALU.mult))
                        link(nc.vector.tensor_scalar(sc_o[:, :], sc_f[:, :], math.cos(math.pi / 8) / math.sqrt(2 * MUL), None, ALU.mult))
                        link(nc.vector.tensor_scalar(sc_f[:, :], sc_f[:, :], 1 / math.sqrt(MUL), None, ALU.mult))
                        link(nc.vector.tensor_scalar(sc_m[:, :], attr[:, :], math.sin(math.pi / 8) / math.sqrt(MUL), None, ALU.mult))

            with Stage() as st:
                x_sb = st.sb("x_in", [P, NT, D])
                rstd, shift = st.sb("rstd0", [P, NT]), st.sb("shift0", [P, NT])
                load_nodes(x_sb, a["x"], N)
                layernorm_stats(x_sb, rstd, shift)

                def act_end(act, n, j, pO, row, aux):
                    return nc.scalar.activation(row[:, :], pO[0][:, 0:D], ACT.Copy, scale=sc_f[:, ds(n, 1)])

                def dve_end(dve, n, j, pO, row, aux, s_ae):
                    xt = tile(x_sb, n)
                    nc.vector.scalar_tensor_tensor(aux[:, 0:MUL], pO[1][:, 0:MUL], sc_m[:, ds(n, 1)], xt[:, 0:MUL],
                                                   ALU.mult, ALU.add)
                    return nc.vector.scalar_tensor_tensor(
                        aux[:, MUL:D].rearrange("p (k m) -> p m k", m=3), pO[1][:, MUL:D].rearrange("p (m k) -> p m k", m=3),
                        sc_m[:, ds(n, 1)], xt[:, MUL:D].rearrange("p (k m) -> p m k", m=3), ALU.mult, ALU.add)

                node_stage(0, x_sb, rstd, shift, [D, D],
                           lambda w, b: [(w[q][:, :, :], wbig[:, q * D:(q + 1) * D].rearrange("(c p) n -> p c n", p=P)) for q in range(2)],
                           [False, False], act_end, dve_end,
                           [(lambda n: table[0][ds(n * P, P), :], lambda row, aux: row[:, :]),
                            (lambda n: base0[ds(n * P, P), :], lambda row, aux: aux[:, :])])

            with Stage() as st:
                acc = st.sb("acc0", [P, NT, 2 * D])
                with Stage() as se:
                    G = [se.sb(f"G{j}", [P, D]) for j in range(U)]
                    ib = se.sb("ib", [P, U], I32)
                    gate = se.sb("gate", [1, 5])
                    w1p = se.sb("w1p", [4 * NBAS, 4, NHID])
                    w2s = se.sb("w2s", [NHID, D])
                    a10 = [se.sb(f"a10_{h}", [P, P]) for h in range(2)]
                    a10T = [se.sb(f"a10T_{h}", [4 * NBAS, P]) for h in range(2)]
                    hid = [se.sb(f"hid{j}", [NHID, P]) for j in range(2)]
                    oh = [se.sb(f"oh{j}", [P, 4, P]) for j in range(4)]
                    one = [se.sb(f"one{j}", [P, P]) for j in range(2)]
                    prod = [se.sb(f"prod{j}", [P, 8, MUL]) for j in range(2)]
                    pA = se.ps("pA", [P, P])
                    pH = [se.ps(f"pH{j}", [NHID, P]) for j in range(2)]
                    pE = [se.ps(f"pE{j}", [P, D]) for j in range(2)]
                    pM = [se.ps(f"pM{j}", [P, 8, MUL]) for j in range(2)]
                    s_w, s_z, s_c, s_ib, s_cons = (se.sem(n) for n in ("s_w", "s_z", "s_c", "s_ib", "s_cons"))
                    s_g = [se.sem(f"s_g{j}") for j in range(U)]
                    s_a, s_at, s_ac, s_h, s_hs, s_e = (se.sem(n) for n in ("s_a", "s_at", "s_ac", "s_h", "s_hs", "s_e"))
                    s_one, s_oh, s_oh0, s_m, s_acc, s_gt = (se.sem(n) for n in ("s_one", "s_oh", "s_oh0", "s_m", "s_acc", "s_gt"))
                    with nc.Block() as block:
                        @block.sync
                        def _(sp):
                            sp.wait_ge(s_z, 1)
                            for j in range(4):
                                sp.dma_start(w1p[j * NBAS:(j + 1) * NBAS, j, :], a["L0_gnn_W_mlp1"]).then_inc(s_w, 16)
                            for q, c in enumerate((0, 2, 3, 1)):
                                sp.dma_start(w2s[:, q * MUL:(q + 1) * MUL], a["L0_gnn_W_mlp2"][:, c * MUL:(c + 1) * MUL]).then_inc(s_w, 16)

                        @block.gpsimd
                        def _(pool):
                            gather_rows(pool, U, G, ib, gate, table[0], s_ib, s_g, s_gt)

                        @block.scalar
                        def _(act):
                            act.wait_ge(s_z, 4)

                            def features(k, q, h):
                                freed(act, s_at, q - 1)
                                nc.scalar.activation(a10[h][:, 0:4 * NBAS].rearrange("p (k c) -> p k c", k=4),
                                                     a10S[:, :, ds(k, 4)].rearrange("p c k -> p k c"), ACT.Copy).then_inc(s_a, 1)

                            def turned(q, h):
                                act.wait_ge(s_at, q + 1)
                                freed(act, s_h, 4 * q - 4)
                                nc.scalar.activation(a10T[h][:, :], pA[0:4 * NBAS, :], ACT.Copy).then_inc(s_ac, 1)

                            def next_quad(k, j):
                                if j % 4 in (0, 3):
                                    q = (k - j) // 4 + j // 4 + 1
                                    if j % 4 == 0:
                                        features(k + 4, q, 1 - j // 4)
                                    else:
                                        turned(q, 1 - j // 4)

                            def silu(k, j):
                                act.wait_ge(s_h, k + 1)
                                freed(act, s_e, k - 1)
                                nc.scalar.activation(hid[j % 2][:, :], pH[j % 2][:, :], ACT.Silu,
                                                     scale=1 / math.sqrt(NBAS)).then_inc(s_hs, 1)

                            def vectors(k, j):
                                act.wait_ge(s_one, k + 1)
                                freed(act, s_m, k - 3)
                                for m in range(1, 4):
                                    ins = nc.scalar.activation(oh[j % 4][:, m, :], one[j % 2][:, :], ACT.Copy,
                                                               scale=a4S[:, m, ds(k, 1)])
                                ins.then_inc(s_oh, 1)
                            features(0, 0, 0)
                            turned(0, 0)
                            steps(act, U, (0, gather_indices(act, U, 0, ib, s_ib, s_cons, s_gt)), (0, silu), (0, vectors), (0, next_quad))

                        @block.vector
                        def _(dve):
                            nc.vector.memset(w1p[:, :, :], 0.0).then_inc(s_z, 1)
                            for h in range(2):
                                nc.vector.memset(a10[h][:, :], 0.0).then_inc(s_z, 1)
                            nc.vector.memset(acc[:, :, :], 0.0).then_inc(s_z, 1)
                            dve.wait_ge(s_w, 16 * 8)
                            dve.wait_ge(s_z, 4)
                            link = chain(dve, s_c)
                            link(nc.vector.tensor_scalar(w2s[:, 0:3 * MUL], w2s[:, 0:3 * MUL], 1 / math.sqrt(NHID), None, ALU.mult))
                            link(nc.vector.tensor_scalar(w2s[:, 3 * MUL:D], w2s[:, 3 * MUL:D], 1 / math.sqrt(3 * NHID), None, ALU.mult))
                            load, node = step_nodes(dve, U)

                            def mark(k, j):
                                freed(dve, s_oh, k - 1)
                                nc.vector.tensor_scalar(one[j % 2][:, :], iota[:, :], relS[:, ds(k, 1)], None, ALU.is_equal).then_inc(s_one, 1)
                                freed(dve, s_m, k - 3)
                                nc.vector.tensor_scalar(oh[j % 4][:, 0, :], iota[:, :], relS[:, ds(k, 1)], a4S[:, 0, ds(k, 1)],
                                                        ALU.is_equal, ALU.mult).then_inc(s_oh0, 1)

                            def products(k, j):
                                dve.wait_ge(s_e, k + 1)
                                gathered(dve, U, s_g, k, j)
                                freed(dve, s_m, k - 1)
                                w = pE[j % 2][:, :].rearrange("p (b c) -> p b c", c=MUL)
                                g = G[j][:, :].rearrange("p (b c) -> p b c", c=MUL)
                                nc.vector.tensor_tensor(prod[j % 2][:, 0:8:7, :], w[:, 0:2, :], g[:, 0:1, :].broadcast_to([P, 2, MUL]), ALU.mult)
                                nc.vector.tensor_tensor(prod[j % 2][:, 1:7, :].rearrange("p (q m) c -> p q m c", q=2),
                                                        w[:, 2:4, :].unsqueeze(2).broadcast_to([P, 2, 3, MUL]),
                                                        g[:, 1:4, :].unsqueeze(1).broadcast_to([P, 2, 3, MUL]), ALU.mult).then_inc(s_cons, 1)
                            flat = [t.rearrange("p b c -> p (b c)") for t in pM]
                            steps(dve, U, (AHEAD, load), (0, mark), (1, products), (LAG, adder(dve, acc, flat, 2, s_m, s_acc, node)))

                        @block.tensor
                        def _(pe):
                            pe.wait_ge(s_w, 16 * 8)
                            pe.wait_ge(s_c, 2)

                            def turn(q, h):
                                pe.wait_ge(s_a, q + 1)
                                freed(pe, s_ac, q)
                                nc.tensor.transpose(pA[:, :], a10[h][:, :], ident[:, :]).then_inc(s_at, 1)

                            def next_quad(k, j):
                                if j % 4 == 2:
                                    turn((k - j) // 4 + j // 4 + 1, 1 - j // 4)

                            def hidden(k, j):
                                if j % 4 == 0:
                                    pe.wait_ge(s_ac, (k - j) // 4 + j // 4 + 1)
                                freed(pe, s_hs, k - 1)
                                nc.tensor.matmul(pH[j % 2][:, :], w1p[:, j % 4, :], a10T[j // 4][:, :], start=True, stop=True).then_inc(s_h, 1)

                            def edge_weights(k, j):
                                pe.wait_ge(s_hs, k + 1)
                                freed(pe, s_cons, k - 1)
                                nc.tensor.matmul(pE[j % 2][:, :], hid[j % 2][:, :], w2s[:, :], start=True, stop=True).then_inc(s_e, 1)

                            def scatter(k, j):
                                pe.wait_ge(s_oh, k + 1)
                                pe.wait_ge(s_oh0, k + 1)
                                pe.wait_ge(s_cons, k + 1)
                                freed(pe, s_acc, k - 1)
                                o, p, m = oh[j % 4], prod[j % 2], pM[j % 2]
                                nc.tensor.matmul(m[:, 0:4, :], o[:, 0, :], p[:, 0:4, :], start=True, stop=False)
                                nc.tensor.matmul(m[:, 4:6, :], o[:, 1, :], p[:, 4:8:3, :], start=False, stop=False)
                                for q in range(2):
                                    nc.tensor.matmul(m[:, 4, :], o[:, 2 + q, :], p[:, 5 + q, :], start=False, stop=False)
                                    ins = nc.tensor.matmul(m[:, 6 + q, :], o[:, 2 + q, :], p[:, 7, :], start=False, stop=(q == 1))
                                ins.then_inc(s_m, 1)
                            turn(0, 0)
                            steps(pe, U, (0, hidden), (1, edge_weights), (2, scatter), (0, next_quad))

                with Stage() as se:
                    wo = se.sb("wo", [P, 2, MUL])
                    ms = [se.sb(f"ms{j}", [P, 8, MUL]) for j in range(2)]
                    mT = [se.sb(f"mT{j}", [P, 2 * D]) for j in range(2)]
                    bs = [se.sb(f"bs{j}", [P, D]) for j in range(2)]
                    xo = [se.sb(f"xo{j}", [P, D]) for j in range(2)]
                    pT = [se.ps(f"pT{j}", [P, 2 * D]) for j in range(2)]
                    pO = [se.ps(f"pO{j}", [P, D]) for j in range(2)]
                    s_w, s_ms, s_t, s_mt, s_o, s_x = (se.sem(n) for n in ("s_w", "s_ms", "s_t", "s_mt", "s_o", "s_x"))
                    s_b = [se.sem(f"s_b{j}") for j in range(2)]
                    s_st = [se.sem(f"s_st{j}") for j in range(2)]

                    with nc.Block() as block:
                        @block.sync
                        def _(sp):
                            sp.dma_start(wo[:, 0, :], a["L0_gnn_W_lo0"]).then_inc(s_w, 16)
                            sp.dma_start(wo[0:MUL, 1, :], a["L0_gnn_W_lo1"][MUL:2 * MUL, :]).then_inc(s_w, 16)
                            sp.dma_start(wo[MUL:P, 1, :], a["L0_gnn_W_lo1"][0:MUL, :]).then_inc(s_w, 16)

                            def base_rows(n, j):
                                freed(sp, s_x, n - 1)
                                sp.dma_start(bs[j][:, :], base0[ds(n * P, P), :]).then_inc(s_b[j], 16)
                            tiles(sp, (0, base_rows))

                        @block.scalar
                        def _(act):
                            def scaled(n, j):
                                freed(act, s_t, n - 1)
                                nc.scalar.activation(ms[j][:, :, :].rearrange("p (c h) k -> p h c k", h=2),
                                                     tile(acc, n).rearrange("p (h c k) -> p h c k", h=2, k=MUL), ACT.Copy,
                                                     scale=sc_o[:, ds(n, 1)]).then_inc(s_ms, 1)

                            def out_rows(n, j):
                                act.wait_ge(s_x, n + 1)
                                act.dma_start(x1[ds(n * P, P), :], xo[j][:, :]).then_inc(s_st[j], 16)
                            tiles(act, (0, scaled), (3, out_rows))
                            for j in range(2):
                                act.wait_ge(s_st[j], 16 * (NT // 2))

                        @block.vector
                        def _(dve):
                            def turned(n, j):
                                dve.wait_ge(s_t, n + 1)
                                freed(dve, s_o, n - 1)
                                nc.vector.tensor_copy(mT[j][:, :], pT[j][:, :]).then_inc(s_mt, 1)

                            def added(n, j):
                                dve.wait_ge(s_o, n + 1)
                                dve.wait_ge(s_b[j], 8 * (n - j) + 16)
                                freed(dve, s_st[j], 8 * (n - j))
                                nc.vector.tensor_tensor(xo[j][:, 0:MUL], pO[j][:, 0:MUL], bs[j][:, 0:MUL], ALU.add)
                                nc.vector.tensor_tensor(xo[j][:, MUL:D].rearrange("p (k m) -> p m k", m=3),
                                                        pO[j][:, MUL:D].rearrange("p (m k) -> p m k", m=3),
                                                        bs[j][:, MUL:D].rearrange("p (k m) -> p m k", m=3), ALU.add).then_inc(s_x, 1)
                            tiles(dve, (0, turned), (2, added))

                        @block.tensor
                        def _(pe):
                            pe.wait_ge(s_w, 48)

                            def turn(n, j):
                                pe.wait_ge(s_ms, n + 1)
                                freed(pe, s_mt, n - 1)
                                for c in range(4):
                                    ins = nc.tensor.transpose(pT[j][:, c * P:(c + 1) * P],
                                                              ms[j][:, 2 * c:2 * c + 2, :].rearrange("p b k -> p (b k)"), ident[:, :])
                                ins.then_inc(s_t, 1)

                            def multiply(n, j):
                                pe.wait_ge(s_mt, n + 1)
                                freed(pe, s_x, n - 1)
                                for c in range(4):
                                    ins = nc.tensor.matmul(pO[j][:, c * MUL:(c + 1) * MUL], mT[j][:, c * P:(c + 1) * P],
                                                           wo[:, min(c, 1), :], start=True, stop=True)
                                ins.then_inc(s_o, 1)
                            tiles(pe, (0, turn), (1, multiply))

        x_sb = top.sb("x_sb", [P, NT, D])
        rstd, shift = top.sb("rstd", [P, NT]), top.sb("shift", [P, NT])
        load_nodes(x_sb, x1, N)
        layernorm_stats(x_sb, rstd, shift)
        with Stage() as st1:
            F1 = D // H1
            gS, dS = st1.sb("gS", [P, KP, H1]), st1.sb("dS", [P, KP, H1])
            score = st1.sb("score", [P, NT, 2 * H1])
            with Stage() as st:
                wz = st.sb("wz", [P, 2, D])
                wa = st.sb("wa", [P, 2, 2 * H1])
                att = st.sb("att", [P, H1, 2 * F1])
                wp = st.sb("wp", [P, 2, D])
                s_w, s_c = st.sem("s_w"), st.sem("s_c")
                with nc.Block() as block:
                    @block.sync
                    def _(sp):
                        for h in range(H1):
                            sp.dma_start(wz[:, :, h * F1:(h + 1) * F1], a["L1_gnn_W"][h].rearrange("(c p) f -> p c f", p=P)).then_inc(s_w, 16)
                        sp.dma_start(att[:, :, :].rearrange("p h f -> p (h f)"),
                                     a["L1_gnn_att"].rearrange("(a h) f -> a (h f)", a=1).broadcast_to([P, H1 * 2 * F1])).then_inc(s_w, 16)

                    @block.vector
                    def _(dve):
                        dve.wait_ge(s_w, 16 * (H1 + 1))
                        link = chain(dve, s_c)
                        for half in range(2):
                            for c in range(2):
                                link(nc.vector.tensor_tensor(wp[:, c, :].rearrange("p (h f) -> p h f", h=H1),
                                                             wz[:, c, :].rearrange("p (h f) -> p h f", h=H1),
                                                             att[:, :, half * F1:(half + 1) * F1], ALU.mult))
                                link(nc.vector.tensor_reduce(wa[:, c, half * H1:(half + 1) * H1],
                                                             wp[:, c, :].rearrange("p (h f) -> p h f", h=H1), AX.X, ALU.add))

                def act_end(act, n, j, pO, row, aux):
                    return nc.scalar.activation(row[:, :], pO[0][:, :], ACT.Copy)

                def dve_end(dve, n, j, pO, row, aux, s_ae):
                    return nc.vector.tensor_copy(tile(score, n), pO[1][:, :])

                node_stage(1, x_sb, rstd, shift, [D, 2 * H1], lambda w, b: [], [False, False], act_end, dve_end,
                           [(lambda n: table[1][ds(n * P, P), :], lambda row, aux: row[:, :])], ready={0: wz, 1: wa})
            with Stage() as st:
                sc_d = st.sb("sc_d", [P, NT, H1])
                s_s, s_c = st.sem("s_s"), st.sem("s_c")
                with nc.Block() as block:
                    @block.sync
                    def _(sp):
                        sp.dma_start(small1.rearrange("(t p) h -> p t h", p=P), score[:, :, 0:H1]).then_inc(s_s, 16)
                        sp.wait_ge(s_s, 16)

                    @block.vector
                    def _(dve):
                        nc.vector.tensor_copy(sc_d[:, :, :], score[:, :, H1:2 * H1]).then_inc(s_c, 1)
                edge_scores(small1, sc_d, H1, gS, dS)
            edge_softmax(H1, gS, dS, 0.01, -1000.0, False)
            with Stage() as st:
                acc = st.sb("acc1", [P, NT, D + H1])
                den = st.sb("den", [P, NT, H1])
                s_z, s_c = st.sem("s_z"), st.sem("s_c")
                with nc.Block() as block:
                    @block.vector
                    def _(dve):
                        nc.vector.memset(acc[:, :, :], 0.0).then_inc(s_z, 1)
                edge_sum(U2, table[1], acc, D + H1, H1, gS, None)
                with nc.Block() as block:
                    @block.vector
                    def _(dve):
                        link = chain(dve, s_c)
                        link(nc.vector.tensor_scalar(den[:, :, :], acc[:, :, D:D + H1], 1e-30, None, ALU.max))
                        link(nc.vector.reciprocal(den[:, :, :], den[:, :, :]))
                        heads = acc[:, :, 0:D].rearrange("p t (h f) -> p t h f", h=H1)
                        link(nc.vector.tensor_tensor(heads, heads, den[:, :, :].unsqueeze(3).broadcast_to([P, NT, H1, F1]), ALU.mult))
                        link(nc.vector.tensor_tensor(x_sb[:, :, :], x_sb[:, :, :], acc[:, :, 0:D], ALU.add))

        layernorm_stats(x_sb, rstd, shift)

        def act_end(act, n, j, pO, row, aux):
            return nc.scalar.activation(row[:, :], pO[0][:, :], ACT.Copy)

        def dve_end(dve, n, j, pO, row, aux, s_ae):
            return nc.vector.tensor_tensor(tile(x_sb, n), tile(x_sb, n), pO[1][:, :], ALU.add)

        node_stage(2, x_sb, rstd, shift, [D, D],
                   lambda w, b: [(w[0][:, :, :], a["L2_gnn_w_nbr"].rearrange("(c p) n -> p c n", p=P)),
                                 (w[1][:, :, :], a["L2_gnn_w_own"].rearrange("(c p) n -> p c n", p=P)),
                                 (b[1][0:1, :], a["L2_gnn_bias"].rearrange("(a n) -> a n", a=1))],
                   [False, True], act_end, dve_end, [(lambda n: table[2][ds(n * P, P), :], lambda row, aux: row[:, :])])
        edge_sum(U2, table[2], x_sb, D, 0, None, None)

        layernorm_stats(x_sb, rstd, shift)
        with Stage() as st3:
            F3 = D // H3
            gS, dS = st3.sb("gS", [P, KP, H3]), st3.sb("dS", [P, KP, H3])
            with Stage() as st:
                score = st.sb("score", [P, NT, H3])
                s_l = st.sem("s_l")

                def act_end(act, n, j, pO, row, aux):
                    nc.scalar.activation(aux[:, :], pO[0][:, 0:D], ACT.Copy)
                    return nc.scalar.activation(row[:, :], pO[1][:, :], ACT.Copy)

                def dve_end(dve, n, j, pO, row, aux, s_ae):
                    dve.wait_ge(s_ae, n + 1)
                    nc.vector.tensor_tensor(aux[:, :], aux[:, :], pO[0][:, D:2 * D], ALU.mult).then_inc(s_l, 1)
                    dve.wait_ge(s_l, n + 1)
                    return nc.vector.tensor_reduce(tile(score, n), aux[:, :].rearrange("p (h c) -> p h c", h=H3), AX.X, ALU.add)

                def qkv(w, b):
                    for q, (name, o) in enumerate((("q", 0), ("k", D), ("v", 0))):
                        yield w[q // 2][:, :, o:o + D], a[f"L3_gnn_W{name}"].rearrange("(c p) n -> p c n", p=P)
                        yield b[q // 2][0:1, o:o + D], a[f"L3_gnn_b{name}"].rearrange("(a n) -> a n", a=1)

                node_stage(3, x_sb, rstd, shift, [2 * D, D], qkv, [True, True], act_end, dve_end,
                           [(lambda n: table[3][ds(n * P, P), :], lambda row, aux: row[:, :])])
                with Stage() as se:
                    s_c, s_s = se.sem("s_c"), se.sem("s_s")
                    with nc.Block() as block:
                        @block.vector
                        def _(dve):
                            nc.vector.tensor_scalar(score[:, :, :], score[:, :, :], 1 / math.sqrt(F3), None, ALU.mult).then_inc(s_c, 1)

                        @block.sync
                        def _(sp):
                            sp.wait_ge(s_c, 1)
                            sp.dma_start(small3.rearrange("(t p) h -> p t h", p=P), score[:, :, :]).then_inc(s_s, 16)
                            sp.wait_ge(s_s, 16)
                edge_scores(small3, score, H3, gS, dS)
            edge_softmax(H3, gS, dS, 0.2, None, True)
            acc = st3.sb("acc3", [P, NT, D + 2 * H3])
            with Stage() as st:
                s_z = st.sem("s_z")
                with nc.Block() as block:
                    @block.vector
                    def _(dve):
                        nc.vector.memset(acc[:, :, :], 0.0).then_inc(s_z, 1)
            edge_sum(U, table[3], acc, D + 2 * H3, H3, gS, dS)

            with Stage() as st:
                own, den = st.sb("own", [P, NT, H3]), st.sb("den", [P, NT, H3])
                alone = st.sb("alone", [P, NT])
                wo = st.sb("wo", [P, 2, D])
                bo = st.sb("bo", [1, D])
                v = [st.sb(f"v{j}", [P, D]) for j in range(4)]
                y = [st.sb(f"y{j}", [P, D]) for j in range(4)]
                vT = [st.sb(f"vT{j}", [P, D]) for j in range(2)]
                pT = [st.ps(f"pT{j}", [P, D]) for j in range(2)]
                pO = [st.ps(f"pO{j}", [P, D]) for j in range(2)]
                s_w, s_c, s_at, s_t, s_tc, s_o, s_r, s_y, s_l = (st.sem(n) for n in ("s_w", "s_c", "s_at", "s_t", "s_tc", "s_o", "s_r", "s_y", "s_l"))
                s_v = [st.sem(f"s_v{j}") for j in range(4)]
                with nc.Block() as block:
                    @block.sync
                    def _(sp):
                        sp.dma_start(wo[:, :, :], a["L3_gnn_Wo"].rearrange("(c p) n -> p c n", p=P)).then_inc(s_w, 16)
                        sp.dma_start(bo[0:1, :], a["L3_gnn_bo"].rearrange("(a n) -> a n", a=1)).then_inc(s_w, 16)

                        def own_rows(n, j):
                            freed(sp, s_t, n - 3)
                            sp.dma_start(v[j][:, :], table[3][ds(n * P, P), :]).then_inc(s_v[j], 16)
                        tiles4(sp, (0, own_rows))

                    @block.vector
                    def _(dve):
                        link = chain(dve, s_c)
                        link(nc.vector.tensor_scalar(alone[:, :], cnt[:, :], 0.0, None, ALU.is_equal))
                        link(nc.vector.tensor_tensor(own[:, :, :], acc[:, :, D + H3:D + 2 * H3],
                                                     alone[:, :].unsqueeze(2).broadcast_to([P, NT, H3]), ALU.add))
                        link(nc.vector.tensor_tensor(den[:, :, :], own[:, :, :], acc[:, :, D:D + H3], ALU.add))
                        link(nc.vector.reciprocal(den[:, :, :], den[:, :, :]))
                        heads = lambda t: t.rearrange("p (h c) -> p h c", h=H3)
                        wide = lambda t, n: t[:, ds(n, 1), :].rearrange("p a h -> p h a").broadcast_to([P, H3, F3])

                        def weighted(n, j):
                            dve.wait_ge(s_v[j], (n - j) * 4 + 16)
                            at = tile(acc[:, :, 0:D], n)
                            nc.vector.tensor_tensor(heads(v[j][:, :]), heads(v[j][:, :]), wide(own, n), ALU.mult).then_inc(s_l, 1)
                            dve.wait_ge(s_l, 2 * n + 1)
                            nc.vector.tensor_tensor(v[j][:, :], v[j][:, :], at, ALU.add).then_inc(s_l, 1)
                            dve.wait_ge(s_l, 2 * n + 2)
                            nc.vector.tensor_tensor(heads(v[j][:, :]), heads(v[j][:, :]), wide(den, n), ALU.mult).then_inc(s_at, 1)

                        def added(n, j):
                            dve.wait_ge(s_o, n + 1)
                            dve.wait_ge(s_y, n + 1)
                            nc.vector.tensor_tensor(tile(acc[:, :, 0:D], n), pO[j % 2][:, :], y[j][:, :], ALU.add).then_inc(s_r, 1)
                        tiles4(dve, (0, weighted), (2, added))

                    @block.scalar
                    def _(act):
                        def norm(n, j):
                            freed(act, s_r, n - 3)
                            nc.scalar.activation(y[j][:, :], tile(x_sb, n), ACT.Relu, bias=shift[:, ds(n, 1)],
                                                 scale=rstd[:, ds(n, 1)]).then_inc(s_y, 1)

                        def turned(n, j):
                            act.wait_ge(s_t, n + 1)
                            freed(act, s_o, n - 1)
                            nc.scalar.activation(vT[j % 2][:, :], pT[j % 2][:, :], ACT.Copy).then_inc(s_tc, 1)
                        tiles4(act, (0, norm), (0, turned))

                    @block.tensor
                    def _(pe):
                        pe.wait_ge(s_w, 32)

                        def turn(n, j):
                            pe.wait_ge(s_at, n + 1)
                            freed(pe, s_tc, n - 1)
                            for c in range(2):
                                ins = nc.tensor.transpose(pT[j % 2][:, c * P:(c + 1) * P], v[j][:, c * P:(c + 1) * P], ident[:, :])
                            ins.then_inc(s_t, 1)

                        def multiply(n, j):
                            pe.wait_ge(s_tc, n + 1)
                            freed(pe, s_r, n - 1)
                            nc.tensor.matmul(pO[j % 2][:, :], ones[0:1, :], bo[0:1, :], start=True, stop=False)
                            for c in range(2):
                                ins = nc.tensor.matmul(pO[j % 2][:, :], vT[j % 2][:, c * P:(c + 1) * P], wo[:, c, :], start=False, stop=(c == 1))
                            ins.then_inc(s_o, 1)
                        tiles4(pe, (0, turn), (1, multiply))

            rsg, brow = st3.sb("rsg", [P, D]), st3.sb("brow", [P, D])
            batch_norm(acc, a["L3_gnn_bn1_g"], a["L3_gnn_bn1_b"], rsg, brow)

            with Stage() as st:
                FB = 2 * D // P
                w1 = st.sb("w1", [P, 2, 2 * D])
                w2 = st.sb("w2", [P, FB, D])
                b1 = st.sb("b1", [P, FB])
                b2 = st.sb("b2", [1, D])
                h1 = [st.sb(f"h1_{j}", [P, D]) for j in range(4)]
                hT = [st.sb(f"hT{j}", [P, D]) for j in range(2)]
                fT = [st.sb(f"fT{j}", [P, FB, P]) for j in range(2)]
                pT = [st.ps(f"pT{j}", [P, D]) for j in range(2)]
                pF = [st.ps(f"pF{j}", [P, FB, P]) for j in range(2)]
                pO = [st.ps(f"pO{j}", [P, D]) for j in range(2)]
                s_w, s_l, s_h, s_t, s_tc, s_f, s_fc, s_o, s_r = (st.sem(n) for n in ("s_w", "s_l", "s_h", "s_t", "s_tc", "s_f", "s_fc", "s_o", "s_r"))
                with nc.Block() as block:
                    @block.sync
                    def _(sp):
                        sp.dma_start(w1[:, :, :], a["L3_gnn_W1"].rearrange("(c p) n -> p c n", p=P)).then_inc(s_w, 16)
                        sp.dma_start(w2[:, :, :], a["L3_gnn_W2"].rearrange("(c p) n -> p c n", p=P)).then_inc(s_w, 16)
                        with nc.allow_non_contiguous_dma(reason="512 biases, feature on partition"):
                            sp.dma_start(b1[:, :], a["L3_gnn_b1"].rearrange("(c p) -> p c", p=P)).then_inc(s_w, 16)
                        sp.dma_start(b2[0:1, :], a["L3_gnn_b2"].rearrange("(a n) -> a n", a=1)).then_inc(s_w, 16)

                    @block.vector
                    def _(dve):
                        def normed(n, j):
                            freed(dve, s_r, n - 3)
                            nc.vector.tensor_tensor(h1[j][:, :], tile(acc[:, :, 0:D], n), rsg[:, :], ALU.mult).then_inc(s_l, 1)
                            dve.wait_ge(s_l, n + 1)
                            nc.vector.tensor_tensor(h1[j][:, :], h1[j][:, :], brow[:, :], ALU.add).then_inc(s_h, 1)

                        def added(n, j):
                            dve.wait_ge(s_o, n + 1)
                            nc.vector.tensor_tensor(tile(acc[:, :, 0:D], n), pO[j % 2][:, :], h1[j][:, :], ALU.add).then_inc(s_r, 1)
                        tiles4(dve, (0, normed), (3, added))

                    @block.scalar
                    def _(act):
                        act.wait_ge(s_w, 64)

                        def turned(n, j):
                            act.wait_ge(s_t, n + 1)
                            freed(act, s_f, n - 1)
                            nc.scalar.activation(hT[j % 2][:, :], pT[j % 2][:, :], ACT.Copy).then_inc(s_tc, 1)

                        def hidden(n, j):
                            act.wait_ge(s_f, n + 1)
                            freed(act, s_o, n - 1)
                            for q in range(FB):
                                ins = nc.scalar.activation(fT[j % 2][:, q, :], pF[j % 2][:, q, :], ACT.Relu, bias=b1[:, q:q + 1])
                            ins.then_inc(s_fc, 1)
                        tiles4(act, (0, turned), (1, hidden))

                    @block.tensor
                    def _(pe):
                        pe.wait_ge(s_w, 64)

                        def turn(n, j):
                            pe.wait_ge(s_h, n + 1)
                            freed(pe, s_tc, n - 1)
                            for c in range(2):
                                ins = nc.tensor.transpose(pT[j % 2][:, c * P:(c + 1) * P], h1[j][:, c * P:(c + 1) * P], ident[:, :])
                            ins.then_inc(s_t, 1)

                        def widen(n, j):
                            pe.wait_ge(s_tc, n + 1)
                            freed(pe, s_fc, n - 1)
                            for q in range(FB):
                                for c in range(2):
                                    ins = nc.tensor.matmul(pF[j % 2][:, q, :], w1[:, c, q * P:(q + 1) * P], hT[j % 2][:, c * P:(c + 1) * P],
                                                           start=(c == 0), stop=(c == 1))
                            ins.then_inc(s_f, 1)

                        def narrow(n, j):
                            pe.wait_ge(s_fc, n + 1)
                            freed(pe, s_r, n - 1)
                            nc.tensor.matmul(pO[j % 2][:, :], ones[0:1, :], b2[0:1, :], start=True, stop=False)
                            for q in range(FB):
                                ins = nc.tensor.matmul(pO[j % 2][:, :], fT[j % 2][:, q, :], w2[:, q, :], start=False, stop=(q == FB - 1))
                            ins.then_inc(s_o, 1)
                        tiles4(pe, (0, turn), (1, widen), (2, narrow))

            batch_norm(acc, a["L3_gnn_bn2_g"], a["L3_gnn_bn2_b"], rsg, brow)

            with Stage() as st:
                CH = NT // 5
                s_c, s_out = st.sem("s_c"), st.sem("s_out")
                with nc.Block() as block:
                    @block.vector
                    def _(dve):
                        for q in range(5):
                            link = chain(dve, s_c, 3 * q)
                            at = acc[:, q * CH:(q + 1) * CH, 0:D]
                            xt = x_sb[:, q * CH:(q + 1) * CH, :]
                            link(nc.vector.tensor_tensor(at, at, rsg[:, :].unsqueeze(1).broadcast_to([P, CH, D]), ALU.mult))
                            link(nc.vector.tensor_tensor(xt, xt, brow[:, :].unsqueeze(1).broadcast_to([P, CH, D]), ALU.add))
                            link(nc.vector.tensor_tensor(xt, xt, at, ALU.add))

                    @block.sync
                    def _(sp):
                        for q in range(5):
                            sp.wait_ge(s_c, 3 * q + 3)
                            last = min(FULL, (q + 1) * CH)
                            sp.dma_start(out[q * CH * P:last * P, :].rearrange("(t p) c -> p t c", p=P), x_sb[:, q * CH:last, :]).then_inc(s_out, 16)
                        sp.dma_start(out[FULL * P:N, :], x_sb[0:REST, FULL, :]).then_inc(s_out, 16)
                        sp.wait_ge(s_out, 96)

def kernel(**inputs):
    import concourse.bacc as _bacc
    from concourse import mybir as _mybir
    from concourse.bass_utils import run_bass_kernel_spmd as _run

    nc = _bacc.Bacc("TRN2", target_bir_lowering=False, num_devices=1)
    arrays, args = {}, {}
    for name, value in inputs.items():
        value = np.ascontiguousarray(value)
        arrays[f"in_{name}"] = value
        args[name] = nc.dram_tensor(f"in_{name}", value.shape, _mybir.dt.from_np(value.dtype), kind="ExternalInput").ap()
    out = nc.dram_tensor("out_x", (N, D), _mybir.dt.from_np(np.dtype("float32")), kind="ExternalOutput").ap()
    build(nc, args, out)
    r = _run(nc, [arrays], core_ids=[0])
    return r.results[0]["out_x"]
```
